# Optimizing a Trainium2 kernel written in Bass

```python
import numpy as np
import jax
import jax.numpy as jnp

def _softmax(x, axis=-1):
    return jax.nn.softmax(x, axis=axis)

def _gelu(x):
    return jax.nn.gelu(x, approximate=True)

def _silu(x):
    return jax.nn.silu(x)

def _sigmoid(x):
    return jax.nn.sigmoid(x)

def _layernorm(x, axis=-1, eps=1e-05):
    m = jnp.mean(x, axis=axis, keepdims=True)
    v = jnp.var(x, axis=axis, keepdims=True)
    return (x - m) / jnp.sqrt(v + eps)

def _scatter_add(tgt, idx, src, axis=0):
    return tgt.at[idx].add(src)

def _segment_sum(src, seg, n):
    return jax.ops.segment_sum(src, seg, n)
kernel_name = 'mk_gps_d1_gnn_r8_096f5d'

def setup_inputs(seed: int=0):
    np.random.seed(seed)
    _w = jnp.asarray

    def _rec_inputs():
        import jax
        import jax.numpy as jnp
        _gk = jax.random.key(seed)
        x = -0.0003929 + 0.9999 * jax.random.normal(jax.random.fold_in(_gk, 1), (1250, 512), jnp.float32)
        src = jax.random.randint(jax.random.fold_in(_gk, 2), (40000,), 0, 1250, jnp.int32)
        dst = jnp.minimum((1250 * jax.random.uniform(jax.random.fold_in(_gk, 3), (40000,)) ** 2.0).astype(jnp.int32), 9999)
        _o = jnp.argsort(dst, stable=True)
        src = src[_o]
        dst = dst[_o]
        return (x, src, dst)
    x, src, dst = _rec_inputs()

    def _L0_gnn_setup():
        import jax, jax.numpy as jnp
        import numpy as np
        N_NODES = 4096
        N_EDGES = 32768
        D = 512
        NUM_EXPERTS = 4
        TOP_K = 2
        LAYERS = 2
        key = jax.random.key(seed)
        ks = jax.random.split(key, 8)
        x = jax.random.normal(ks[0], (N_NODES, D), dtype=jnp.float32)
        edge_index = jax.random.randint(ks[1], (2, N_EDGES), 0, N_NODES, dtype=jnp.int64)
        s = 1.0 / np.sqrt(D)
        gate_W = jax.random.uniform(ks[2], (D, NUM_EXPERTS), jnp.float32, -s, s)
        gate_b = jax.random.uniform(ks[3], (NUM_EXPERTS,), jnp.float32, -s, s)
        Wl = jax.random.uniform(ks[4], (NUM_EXPERTS, LAYERS, D, D), jnp.float32, -s, s)
        bl = jax.random.uniform(ks[5], (NUM_EXPERTS, LAYERS, D), jnp.float32, -s, s)
        Wr = jax.random.uniform(ks[6], (NUM_EXPERTS, LAYERS, D, D), jnp.float32, -s, s)
        return {'x': x, 'gate_W': gate_W, 'gate_b': gate_b, 'Wl': Wl, 'bl': bl, 'Wr': Wr, 'edge_index': edge_index}
    _L0_gnn_all = _L0_gnn_setup()
    _L0_gnn_in = {k: v for k, v in _L0_gnn_all.items() if k in ('gate_W', 'gate_b', 'Wl', 'bl', 'Wr')}
    del _L0_gnn_all

    def _L0_mix_setup():
        import jax, jax.numpy as jnp
        import numpy as np
        DEPTH, DIM, HEADS, DIM_HEAD, NBF, MULT = (2, 512, 8, 64, 256, 4)
        INNER = HEADS * DIM_HEAD

        def layernorm(x, g, b, eps=1e-05):
            mu = jnp.mean(x, axis=-1, keepdims=True)
            var = jnp.mean((x - mu) ** 2, axis=-1, keepdims=True)
            return (x - mu) * jax.lax.rsqrt(var + eps) * g + b

        def softmax_kernel(data, proj, is_query, eps=0.0001):
            d = data.shape[-1]
            normalizer = d ** (-0.25)
            ratio = proj.shape[0] ** (-0.5)
            data_dash = jnp.einsum('bhnd,md->bhnm', data * normalizer, proj)
            diag = jnp.sum(data ** 2, axis=-1, keepdims=True) * 0.5 * normalizer ** 2
            if is_query:
                m = jnp.max(data_dash, axis=-1, keepdims=True)
            else:
                m = jnp.max(data_dash, axis=(-2, -1), keepdims=True)
            m = jax.lax.stop_gradient(m)
            return ratio * (jnp.exp(data_dash - diag - m) + eps)
        key = jax.random.key(seed)
        ks = jax.random.split(key, 16)
        s = 0.02
        B, N = (4, 1024)
        inp = {'x': jax.random.normal(ks[0], (B, N, DIM), jnp.float32), 'ln1_g': jnp.ones((DEPTH, DIM), jnp.float32), 'ln1_b': jnp.zeros((DEPTH, DIM), jnp.float32), 'ln2_g': jnp.ones((DEPTH, DIM), jnp.float32), 'ln2_b': jnp.zeros((DEPTH, DIM), jnp.float32), 'Wq': jax.random.normal(ks[1], (DEPTH, DIM, INNER), jnp.float32) * s, 'bq': jnp.zeros((DEPTH, INNER), jnp.float32), 'Wk': jax.random.normal(ks[2], (DEPTH, DIM, INNER), jnp.float32) * s, 'bk': jnp.zeros((DEPTH, INNER), jnp.float32), 'Wv': jax.random.normal(ks[3], (DEPTH, DIM, INNER), jnp.float32) * s, 'bv': jnp.zeros((DEPTH, INNER), jnp.float32), 'Wo': jax.random.normal(ks[4], (DEPTH, INNER, DIM), jnp.float32) * s, 'bo': jnp.zeros((DEPTH, DIM), jnp.float32), 'proj': jax.random.normal(ks[5], (DEPTH, NBF, DIM_HEAD), jnp.float32), 'W1': jax.random.normal(ks[6], (DEPTH, DIM, DIM * MULT), jnp.float32) * s, 'b1': jnp.zeros((DEPTH, DIM * MULT), jnp.float32), 'W2': jax.random.normal(ks[7], (DEPTH, DIM * MULT, DIM), jnp.float32) * s, 'b2': jnp.zeros((DEPTH, DIM), jnp.float32)}
        return inp
    _L0_mix_all = _L0_mix_setup()
    _L0_mix_in = {k: v for k, v in _L0_mix_all.items() if k in ('ln1_g', 'ln1_b', 'ln2_g', 'ln2_b', 'Wq', 'bq', 'Wk', 'bk', 'Wv', 'bv', 'Wo', 'bo', 'proj', 'W1', 'b1', 'W2', 'b2')}
    del _L0_mix_all

    def _L0_ffn_setup():
        import jax, jax.numpy as jnp
        import numpy as np
        MARK_AX = 0
        OPCODE_BASE = 16
        OP_SHL = OPCODE_BASE + 23
        OP_SHR = OPCODE_BASE + 24
        ALU_LO = 64
        ALU_HI = 80
        AX_CARRY_LO = 96
        OUTPUT_LO = 128
        OUTPUT_HI = 144
        B, SEQ, D = (8, 4096, 512)
        key = jax.random.key(seed)
        ks = jax.random.split(key, 6)
        x = jax.random.uniform(ks[0], (B, SEQ, D), dtype=jnp.float32) * 0.4
        mark = (jax.random.uniform(ks[1], (B, SEQ)) < 0.75).astype(jnp.float32)
        op_sel = jax.random.randint(ks[2], (B, SEQ), 0, 3)
        lo = jax.random.randint(ks[3], (B, SEQ), 0, 16)
        hi = jax.random.randint(ks[4], (B, SEQ), 0, 16)
        sa = jax.random.randint(ks[5], (B, SEQ), 0, 16)
        oh = lambda idx: jax.nn.one_hot(idx, 16, dtype=jnp.float32)
        x = x.at[..., MARK_AX].set(mark)
        x = x.at[..., OP_SHL].set((op_sel == 1).astype(jnp.float32))
        x = x.at[..., OP_SHR].set((op_sel == 2).astype(jnp.float32))
        x = x.at[..., ALU_LO:ALU_LO + 16].set(oh(lo))
        x = x.at[..., ALU_HI:ALU_HI + 16].set(oh(hi))
        x = x.at[..., AX_CARRY_LO:AX_CARRY_LO + 16].set(oh(sa))
        return {'x_bd': x}
    _L0_ffn_all = _L0_ffn_setup()
    _L0_ffn_in = {k: v for k, v in _L0_ffn_all.items() if k in ()}
    del _L0_ffn_all
    return {'x': x, 'src': src, 'dst': dst, 'L0_gnn_gate_W': _L0_gnn_in['gate_W'], 'L0_gnn_gate_b': _L0_gnn_in['gate_b'], 'L0_gnn_Wl': _L0_gnn_in['Wl'], 'L0_gnn_bl': _L0_gnn_in['bl'], 'L0_gnn_Wr': _L0_gnn_in['Wr'], 'L0_mix_ln1_g': _L0_mix_in['ln1_g'], 'L0_mix_ln1_b': _L0_mix_in['ln1_b'], 'L0_mix_ln2_g': _L0_mix_in['ln2_g'], 'L0_mix_ln2_b': _L0_mix_in['ln2_b'], 'L0_mix_Wq': _L0_mix_in['Wq'], 'L0_mix_bq': _L0_mix_in['bq'], 'L0_mix_Wk': _L0_mix_in['Wk'], 'L0_mix_bk': _L0_mix_in['bk'], 'L0_mix_Wv': _L0_mix_in['Wv'], 'L0_mix_bv': _L0_mix_in['bv'], 'L0_mix_Wo': _L0_mix_in['Wo'], 'L0_mix_bo': _L0_mix_in['bo'], 'L0_mix_proj': _L0_mix_in['proj'], 'L0_mix_W1': _L0_mix_in['W1'], 'L0_mix_b1': _L0_mix_in['b1'], 'L0_mix_W2': _L0_mix_in['W2'], 'L0_mix_b2': _L0_mix_in['b2']}

def reference(x, src, dst, L0_gnn_gate_W, L0_gnn_gate_b, L0_gnn_Wl, L0_gnn_bl, L0_gnn_Wr, L0_mix_ln1_g, L0_mix_ln1_b, L0_mix_ln2_g, L0_mix_ln2_b, L0_mix_Wq, L0_mix_bq, L0_mix_Wk, L0_mix_bk, L0_mix_Wv, L0_mix_bv, L0_mix_Wo, L0_mix_bo, L0_mix_proj, L0_mix_W1, L0_mix_b1, L0_mix_W2, L0_mix_b2):
    import jax
    import jax.numpy as jnp

    def _L0_gnn_ref(x, gate_W, gate_b, Wl, bl, Wr, edge_index):
        import jax, jax.numpy as jnp
        import numpy as np
        N_NODES = 4096
        N_EDGES = 32768
        D = 512
        NUM_EXPERTS = 4
        TOP_K = 2
        LAYERS = 2
        n = x.shape[0]
        src, dst = (edge_index[0], edge_index[1])
        gates = jax.nn.softmax(x @ gate_W + gate_b, axis=-1)
        top_v, top_i = jax.lax.top_k(gates, TOP_K)
        deg = jax.ops.segment_sum(jnp.ones((src.shape[0],), x.dtype), dst, num_segments=n)
        inv_deg = jnp.where(deg > 0, 1.0 / jnp.maximum(deg, 1.0), 0.0)[:, None]

        def sage_conv(h, W_l, b_l, W_r):
            aggr = jax.ops.segment_sum(h[src], dst, num_segments=n) * inv_deg
            return aggr @ W_l + b_l + h @ W_r
        expert_outs = []
        for e in range(NUM_EXPERTS):
            h = x
            for l in range(LAYERS):
                h = sage_conv(h, Wl[e, l], bl[e, l], Wr[e, l])
                h = jax.nn.relu(h)
            expert_outs.append(h)
        expert_outputs = jnp.stack(expert_outs, axis=1)
        sel = jnp.take_along_axis(expert_outputs, top_i[:, :, None], axis=1)
        out = jnp.sum(sel * top_v[:, :, None], axis=1)
        return out

    def _L0_mix_ref(x, ln1_g, ln1_b, ln2_g, ln2_b, Wq, bq, Wk, bk, Wv, bv, Wo, bo, proj, W1, b1, W2, b2):
        import jax, jax.numpy as jnp
        import numpy as np
        DEPTH, DIM, HEADS, DIM_HEAD, NBF, MULT = (2, 512, 8, 64, 256, 4)
        INNER = HEADS * DIM_HEAD

        def layernorm(x, g, b, eps=1e-05):
            mu = jnp.mean(x, axis=-1, keepdims=True)
            var = jnp.mean((x - mu) ** 2, axis=-1, keepdims=True)
            return (x - mu) * jax.lax.rsqrt(var + eps) * g + b

        def softmax_kernel(data, proj, is_query, eps=0.0001):
            d = data.shape[-1]
            normalizer = d ** (-0.25)
            ratio = proj.shape[0] ** (-0.5)
            data_dash = jnp.einsum('bhnd,md->bhnm', data * normalizer, proj)
            diag = jnp.sum(data ** 2, axis=-1, keepdims=True) * 0.5 * normalizer ** 2
            if is_query:
                m = jnp.max(data_dash, axis=-1, keepdims=True)
            else:
                m = jnp.max(data_dash, axis=(-2, -1), keepdims=True)
            m = jax.lax.stop_gradient(m)
            return ratio * (jnp.exp(data_dash - diag - m) + eps)
        B, N, D = x.shape
        for i in range(DEPTH):
            y = layernorm(x, ln1_g[i], ln1_b[i])
            q = (y @ Wq[i] + bq[i]).reshape(B, N, HEADS, DIM_HEAD).transpose(0, 2, 1, 3)
            k = (y @ Wk[i] + bk[i]).reshape(B, N, HEADS, DIM_HEAD).transpose(0, 2, 1, 3)
            v = (y @ Wv[i] + bv[i]).reshape(B, N, HEADS, DIM_HEAD).transpose(0, 2, 1, 3)
            qp = softmax_kernel(q, proj[i], True)
            kp = softmax_kernel(k, proj[i], False)
            k_sum = kp.sum(axis=2)
            d_inv = 1.0 / jnp.einsum('bhnm,bhm->bhn', qp, k_sum)
            ctx = jnp.einsum('bhnm,bhnd->bhmd', kp, v)
            o = jnp.einsum('bhmd,bhnm,bhn->bhnd', ctx, qp, d_inv)
            o = o.transpose(0, 2, 1, 3).reshape(B, N, INNER)
            x = x + o @ Wo[i] + bo[i]
            y = layernorm(x, ln2_g[i], ln2_b[i])
            h = jax.nn.gelu(y @ W1[i] + b1[i], approximate=False)
            x = x + h @ W2[i] + b2[i]
        return x

    def _L0_ffn_ref(x_bd):
        import jax, jax.numpy as jnp
        import numpy as np
        MARK_AX = 0
        OPCODE_BASE = 16
        OP_SHL = OPCODE_BASE + 23
        OP_SHR = OPCODE_BASE + 24
        ALU_LO = 64
        ALU_HI = 80
        AX_CARRY_LO = 96
        OUTPUT_LO = 128
        OUTPUT_HI = 144
        B, SEQ, D = (8, 4096, 512)
        hot = x_bd > 0.5
        first16 = lambda off: jnp.argmax(hot[..., off:off + 16], axis=-1).astype(jnp.int32)
        lo = first16(ALU_LO)
        hi = first16(ALU_HI)
        sa = first16(AX_CARRY_LO)
        val = lo + 16 * hi
        shl = jnp.left_shift(val, sa) & 255
        shr = jnp.right_shift(val, sa)
        mark = hot[..., MARK_AX]
        is_shl = hot[..., OP_SHL]
        is_shr = jnp.logical_and(hot[..., OP_SHR], jnp.logical_not(is_shl))
        act_shl = jnp.logical_and(mark, is_shl)
        act_shr = jnp.logical_and(mark, is_shr)
        active = jnp.logical_or(act_shl, act_shr)
        res = jnp.where(act_shl, shl, jnp.where(act_shr, shr, 0))
        res = jnp.clip(res, 0, 255)
        rlo = res & 15
        rhi = res >> 4
        amp = 2.0 * active.astype(x_bd.dtype)
        add_lo = amp[..., None] * jax.nn.one_hot(rlo, 16, dtype=x_bd.dtype)
        add_hi = amp[..., None] * jax.nn.one_hot(rhi, 16, dtype=x_bd.dtype)
        out = x_bd.at[..., OUTPUT_LO:OUTPUT_LO + 16].add(add_lo)
        out = out.at[..., OUTPUT_HI:OUTPUT_HI + 16].add(add_hi)
        return out
    edge_index = jnp.stack([src, dst])
    xn = _layernorm(x, axis=-1)
    x = x + _L0_gnn_ref(xn, L0_gnn_gate_W, L0_gnn_gate_b, L0_gnn_Wl, L0_gnn_bl, L0_gnn_Wr, edge_index) + _L0_mix_ref(xn[None], L0_mix_ln1_g, L0_mix_ln1_b, L0_mix_ln2_g, L0_mix_ln2_b, L0_mix_Wq, L0_mix_bq, L0_mix_Wk, L0_mix_bk, L0_mix_Wv, L0_mix_bv, L0_mix_Wo, L0_mix_bo, L0_mix_proj, L0_mix_W1, L0_mix_b1, L0_mix_W2, L0_mix_b2)[0]
    x = x + _L0_ffn_ref(_layernorm(x, axis=-1)[None])[0]
    return x

_drawn_inputs = setup_inputs


def setup_inputs(seed=0):
    import zlib

    import numpy as np

    out = dict(_drawn_inputs(seed))
    spreads = {'L0_mix_ln1_g': (1.0, 0.6),
     'L0_mix_ln1_b': (0.0, 0.55),
     'L0_mix_ln2_g': (1.0, 0.2),
     'L0_mix_ln2_b': (0.0, 0.464),
     'L0_mix_bq': (0.0, 0.8),
     'L0_mix_bk': (0.0, 0.8),
     'L0_mix_bv': (0.0, 0.1),
     'L0_mix_bo': (0.0, 0.1),
     'L0_mix_b1': (0.0, 0.1),
     'L0_mix_b2': (0.0, 0.1)}
    factors = {'L0_gnn_gate_b': 8.0,
     'L0_gnn_bl': 8.0,
     'L0_mix_Wq': 8.0,
     'L0_mix_Wk': 8.0,
     'L0_mix_proj': 8.0}
    for name, (base, spread) in spreads.items():
        noise = np.random.default_rng([zlib.crc32(name.encode()), seed]).standard_normal(out[name].shape)
        drawn = base * np.exp(spread * noise) if base else spread * noise
        out[name] = jnp.asarray(drawn.astype(out[name].dtype))
    for name, factor in factors.items():
        out[name] = (out[name] * factor).astype(out[name].dtype)
    return out
```

```python
from contextlib import ExitStack

import numpy as np

import concourse.bass as bass
from concourse import mybir

F32 = mybir.dt.float32
F16 = mybir.dt.float16
BF16 = mybir.dt.bfloat16
I32 = mybir.dt.int32
ACT = mybir.ActivationFunctionType
ALU = mybir.AluOpType
X = mybir.AxisListType.X
MAX_REDUCE = bass.bass_isa.ReduceOp.max

N, D, E = 1250, 512, 40000
T = 10
P = N // T
K = D // 128
CHUNKS = ((0, 500), (500, 500), (1000, 250))
GROUPS3 = ((0, 4), (4, 8), (8, 10))

CE = 125
NC = E // CE
CQ, CR = 4, NC // 4
B = 5
NB = NC // B
DG = 32
NG = -(-N // DG)
GW = DG * T
NPAD = NG * DG
SLOTS = 4

EXPERTS = 4
DEPTH, HEADS, DH, M = 2, 8, 64, 256
PAIRS = HEADS // 2
FF = 2048
FT = FF // 128
NORM = float(DH) ** -0.25
FEATURE_EPS = 1e-4
LN_EPS = 1e-5
FC, FCN = 5, 250
FCT = FCN // P


class OnChip:
    pass


def tile(t):
    return slice(t * P, (t + 1) * P)


def emit_norm_stats(nc, vec, act_done, std_ready, seen, src, st, mv, rstd, std):
    for t in range(T):
        last = nc.vector.bn_stats(st[:, t, :], src[:, t, :])
    vec.drain()
    for t in range(T):
        last = nc.vector.bn_aggr(mv[:, t, :], st[:, t, :])
    last.then_inc(std_ready, 1)
    vec.wait_ge(act_done, seen)
    nc.vector.reciprocal(rstd[:], std[:])
    vec.drain()


def stage_normalise_and_index(nc, m, x, src, dst, xn_dram):
    with ExitStack() as ctx:
        def sb(name, shape, dt=F32):
            return ctx.enter_context(nc.sbuf_tensor(name, shape, dt))

        def sem(name):
            return ctx.enter_context(nc.semaphore(name))

        x_in = sb("x_in", [P, T, D])
        st = sb("st0", [P, T, 6])
        mv = sb("mv0", [P, T, 2])
        std = sb("std0", [P, T])
        rstd = sb("rstd0", [P, T])
        edge_i = sb("edge_i", [CR, 2, CQ, CE], I32)
        edge_f = sb("edge_f", [CR, 2, CQ, CE])
        src_tile = sb("src_tile", [CR, CQ, CE])
        src_row = sb("src_row", [CR, CQ, CE])
        key = sb("key", [CR, CQ, CE])
        chunk_min = sb("chunk_min", [CR, CQ])
        chunk_max = sb("chunk_max", [CR, CQ])
        step_i = sb("step_i", [CR, CQ, CR // B], I32)
        step_f = sb("step_f", [CR, CQ, CR // B])
        step_of = sb("step_of", [CR, CQ])
        step_up = sb("step_up", [CR, CQ])
        step_down = sb("step_down", [CR, CQ])
        group_i = sb("group_i", [CR, NG], I32)
        group_lo = sb("group_lo", [CR, NG])
        group_hi = sb("group_hi", [CR, NG])
        cand = sb("cand", [CR, 2, CQ, NG])
        ends = sb("ends", [CR, 2, NG])
        ends_all = sb("ends_all", [CR, 2, NG])
        rng = sb("rng", [1, 6, NG])
        shift_i = sb("shift_i", [P, NG], I32)
        hot_i = sb("hot_i", [P, GW], I32)

        x_loaded = [sem("x_loaded0"), sem("x_loaded1")]
        edges_loaded = sem("edges_loaded")
        consts_made = sem("consts_made")
        ident_cleared = sem("ident_cleared")
        var_ready = sem("var_ready")
        std_made = sem("std_made")
        xn_ready = sem("xn_ready")
        xn_turned = sem("xn_turned")
        xnT_copied = sem("xnT_copied")
        keys_ready = sem("keys_ready")
        keys_turned = sem("keys_turned")
        ends_local = sem("ends_local")
        ends_global = sem("ends_global")
        xn_stored = sem("xn_stored")

        xv = x.rearrange("(t p) d -> p t d", p=P)
        H = T // 2
        with nc.Block() as block:
            @block.sync
            def _(sp):
                for h in range(2):
                    sp.dma_start(x_in[:, h * H:(h + 1) * H, :], xv[:, h * H:(h + 1) * H, :]).then_inc(x_loaded[h], 16)
                for n, a in enumerate((src, dst)):
                    sp.dma_start(edge_i[:, n], a.rearrange("(q r e) -> r q e", q=CQ, e=CE)).then_inc(edges_loaded, 16)
                sp.wait_ge(xn_ready, T)
                sp.dma_start(xn_dram.rearrange("(t p) d -> p t d", p=P), m.xn[:]).then_inc(xn_stored, 16)
                sp.wait_ge(xn_stored, 16)

            @block.gpsimd
            def _(pool):
                pool.memset(m.ident[:], 0.0).then_inc(ident_cleared, 1)
                pool.wait_ge(ident_cleared, 1)
                pool.affine_select(out=m.ident[:], in_=m.ident[:], compare_op=ALU.not_equal, fill=1.0,
                                   base=0, pattern=[[-1, 128]], channel_multiplier=1).then_inc(consts_made, 1)
                pool.memset(m.ones[:], 1.0).then_inc(consts_made, 1)
                pool.memset(m.eps_col[:], LN_EPS).then_inc(consts_made, 1)
                pool.iota(step_i[:], pattern=[[0, CQ], [-B, CR // B]], base=-B, channel_multiplier=1).then_inc(consts_made, 1)
                pool.iota(group_i[:], pattern=[[DG, NG]], base=0, channel_multiplier=0).then_inc(consts_made, 1)
                pool.iota(shift_i[:], pattern=[[-GW, NG]], base=0, channel_multiplier=0).then_inc(consts_made, 1)
                pool.iota(hot_i[:], pattern=[[1, GW]], base=0, channel_multiplier=0).then_inc(consts_made, 1)
                pool.wait_ge(ends_local, 1)
                pool.partition_all_reduce(ends_all[:], ends[:], CR, MAX_REDUCE).then_inc(ends_global, 1)

            @block.scalar
            def _(act):
                act.wait_ge(consts_made, 7)
                act.wait_ge(var_ready, 1)
                nc.scalar.activation(std[:], mv[:, :, 1], ACT.Sqrt, bias=m.eps_col[0:P, :]).then_inc(std_made, 1)
                for t in range(T):
                    act.wait_ge(xn_turned, t + 1)
                    nc.scalar.activation(m.xnT[:, :, tile(t)],
                                         m.ps[:, t % 4, 0:D // 128 * P].rearrange("p (k n) -> p k n", k=K),
                                         ACT.Copy).then_inc(xnT_copied, 1)

            @block.vector
            def _(vec):
                vec.wait_ge(consts_made, 7)
                for h in range(2):
                    vec.wait_ge(x_loaded[h], 16)
                emit_norm_stats(nc, vec, std_made, var_ready, 1, x_in, st, mv, rstd, std)
                for t in range(T):
                    nc.vector.tensor_scalar(m.xn[:, t, :], x_in[:, t, :], mv[:, t, 0:1], rstd[:, t:t + 1],
                                            ALU.subtract, ALU.mult).then_inc(xn_ready, 1)

                vec.wait_ge(edges_loaded, 32)
                nc.vector.tensor_copy(edge_f[:], edge_i[:])
                vec.drain()
                nc.vector.tensor_scalar(src_tile[:], edge_f[:, 0], float(P), None, ALU.is_ge)
                for k in range(2, T):
                    vec.drain()
                    nc.vector.scalar_tensor_tensor(src_tile[:], edge_f[:, 0], float(k * P), src_tile[:], ALU.is_ge, ALU.add)
                vec.drain()
                nc.vector.scalar_tensor_tensor(src_row[:], src_tile[:], -float(P), edge_f[:, 0], ALU.mult, ALU.add)
                nc.vector.scalar_tensor_tensor(key[:], edge_f[:, 1], float(T), src_tile[:], ALU.mult, ALU.add)\
                    .then_inc(keys_ready, 1)

                nc.vector.tensor_reduce(chunk_min[:], edge_f[:, 1], X, ALU.min)
                nc.vector.tensor_reduce(chunk_max[:], edge_f[:, 1], X, ALU.max)
                nc.vector.tensor_copy(step_f[:], step_i[:])
                nc.vector.tensor_copy(group_lo[:], group_i[:])
                vec.drain()
                nc.vector.tensor_scalar(step_f[:], step_f[:], 0.0, None, ALU.is_ge)
                nc.vector.tensor_scalar(group_hi[:], group_lo[:], float(DG), None, ALU.add)
                vec.drain()
                nc.vector.tensor_reduce(step_of[:], step_f[:], X, ALU.add)
                vec.drain()
                for q in range(CQ):
                    nc.vector.tensor_scalar(step_up[:, q:q + 1], step_of[:, q:q + 1], float(q * CR // B + 1), None, ALU.add)
                vec.drain()
                nc.vector.tensor_scalar(step_down[:], step_up[:], -1.0, float(NB + 1), ALU.mult, ALU.add)
                vec.drain()
                for q in range(CQ):
                    nc.vector.tensor_scalar(cand[:, 0, q, :], group_lo[:], chunk_max[:, q:q + 1], step_down[:, q:q + 1],
                                            ALU.is_le, ALU.mult)
                    nc.vector.tensor_scalar(cand[:, 1, q, :], group_hi[:], chunk_min[:, q:q + 1], step_up[:, q:q + 1],
                                            ALU.is_gt, ALU.mult)
                vec.drain()
                for n in range(2):
                    nc.vector.tensor_reduce(ends[:, n, :], cand[:, n].rearrange("p q g -> p g q"), X, ALU.max)\
                        .then_inc(ends_local, 1) if n else \
                        nc.vector.tensor_reduce(ends[:, n, :], cand[:, n].rearrange("p q g -> p g q"), X, ALU.max)
                nc.vector.tensor_copy(m.shift[:], shift_i[:])
                nc.vector.tensor_copy(m.hot[:], hot_i[:])
                vec.wait_ge(ends_global, 1)
                nc.vector.tensor_scalar(rng[:, 0], ends_all[0:1, 0], -1.0, float(NB), ALU.mult, ALU.add)
                vec.drain()
                nc.vector.tensor_scalar(rng[:, 0], rng[:, 0], float(NB - 1), None, ALU.min)
                vec.drain()
                nc.vector.tensor_tensor(rng[:, 1], ends_all[0:1, 1], rng[:, 0], ALU.subtract)
                vec.drain()
                nc.vector.tensor_scalar(rng[:, 1], rng[:, 1], 1.0, None, ALU.max)
                vec.drain()
                at, width = 1, 1
                while width < NG:
                    to = 2 if at != 2 else 3
                    nc.vector.tensor_copy(rng[:, to, 0:width], rng[:, at, 0:width])
                    nc.vector.tensor_tensor(rng[:, to, width:NG], rng[:, at, width:NG], rng[:, at, 0:NG - width], ALU.add)
                    vec.drain()
                    at, width = to, 2 * width
                nc.vector.tensor_tensor(rng[:, 4], rng[:, at], rng[:, 1], ALU.subtract)
                vec.drain()
                nc.vector.tensor_copy(m.ranges[:, 0], rng[:, 0])
                nc.vector.tensor_copy(m.ranges[:, 1], rng[:, 1])
                nc.vector.tensor_copy(m.ranges[:, 2], rng[:, 4])
                vec.wait_ge(keys_turned, 1)
                nc.vector.tensor_copy(m.src_rowT[:], m.ps[0:CE, 4, 0:NC])
                nc.vector.tensor_copy(m.keyT[:], m.ps[0:CE, 5, 0:NC])

            @block.tensor
            def _(pe):
                pe.wait_ge(consts_made, 7)
                for t in range(T):
                    pe.wait_ge(xn_ready, t + 1)
                    if t >= 4:
                        pe.wait_ge(xnT_copied, t - 3)
                    for k in range(K):
                        last = nc.tensor.transpose(m.ps[:, t % 4, k * P:(k + 1) * P], m.xn[:, t, k * 128:(k + 1) * 128],
                                                   m.ident[0:P, 0:P])
                    last.then_inc(xn_turned, 1)
                pe.wait_ge(keys_ready, 1)
                for n, a in enumerate((src_row, key)):
                    for q in range(CQ):
                        last = nc.tensor.transpose(m.ps[0:CE, 4 + n, q * CR:(q + 1) * CR], a[:, q, :], m.ident[0:CR, 0:CR])
                last.then_inc(keys_turned, 1)


def stage_count_edges(nc, m):
    with ExitStack() as ctx:
        def sem(name):
            return ctx.enter_context(nc.semaphore(name))

        row_hot = ctx.enter_context(nc.sbuf_tensor("row_hot", [CE, SLOTS, B, P], BF16))
        key_hot = ctx.enter_context(nc.sbuf_tensor("key_hot", [CE, SLOTS, B, GW], BF16))
        zeros = ctx.enter_context(nc.sbuf_tensor("zeros", [CE, GW], BF16))
        hots_ready = sem("hots_ready")
        slots_free = sem("slots_free")
        group_counted = sem("group_counted")
        banks_free = sem("banks_free")
        zeroed = sem("zeroed")

        with nc.Block() as block:
            @block.vector
            def _(vec):
                nc.vector.memset(zeros[:], 0.0).then_inc(zeroed, 1)
                with vec.Fori(0, NG) as g:
                    lo = vec.value_load(m.ranges[0:1, 0, bass.ds(g, 1)], min_val=0, max_val=NB - 1)
                    steps = vec.value_load(m.ranges[0:1, 1, bass.ds(g, 1)], min_val=1, max_val=NB)
                    before = vec.value_load(m.ranges[0:1, 2, bass.ds(g, 1)], min_val=0, max_val=NB * NG)
                    with vec.Fori(0, steps) as j:
                        vec.wait_ge(slots_free, before + j + 1)
                        slot = (before + j) & (SLOTS - 1)
                        step = nc.s_assert_within(lo + j, 0, NB - 1, skip_runtime_bounds_check_because="lo + steps <= NB")
                        for b in range(B):
                            c = step * B + b
                            nc.vector.tensor_scalar(row_hot[:, bass.ds(slot, 1), b, :], m.hot[0:CE, 0:P],
                                                    m.src_rowT[:, bass.ds(c, 1)], None, ALU.is_equal)
                            last = nc.vector.tensor_scalar(key_hot[:, bass.ds(slot, 1), b, :], m.hot[0:CE, :],
                                                           m.keyT[:, bass.ds(c, 1)], m.shift[0:CE, bass.ds(g, 1)],
                                                           ALU.subtract, ALU.is_equal)
                        last.then_inc(hots_ready, 1)

            @block.tensor
            def _(pe):
                pe.sem_inc(slots_free, SLOTS)
                pe.wait_ge(zeroed, 1)
                with pe.Fori(0, NG // 2) as pair:
                    for half in range(2):
                        g = pair * 2 + half
                        acc = m.ps[0:P, half, 0:GW]
                        lo = pe.value_load(m.ranges[0:1, 1, bass.ds(g, 1)], min_val=1, max_val=NB)
                        before = pe.value_load(m.ranges[0:1, 2, bass.ds(g, 1)], min_val=0, max_val=NB * NG)
                        pe.wait_ge(banks_free, g + 1)
                        nc.tensor.matmul(acc, zeros[:, 0:P], zeros[:], start=True, stop=False)
                        with pe.Fori(0, lo) as j:
                            pe.wait_ge(hots_ready, before + j + 1)
                            slot = (before + j) & (SLOTS - 1)
                            for b in range(B):
                                last = nc.tensor.matmul(acc, row_hot[:, bass.ds(slot, 1), b, :].rearrange("p o n -> p (o n)"),
                                                        key_hot[:, bass.ds(slot, 1), b, :].rearrange("p o n -> p (o n)"),
                                                        start=False, stop=False)
                            last.then_inc(slots_free, 1)
                        nc.tensor.matmul(acc, zeros[:, 0:P], zeros[:], start=False, stop=True).then_inc(group_counted, 1)

            @block.scalar
            def _(act):
                act.sem_inc(banks_free, 2)
                with act.Fori(0, NG // 2) as pair:
                    for half in range(2):
                        g = pair * 2 + half
                        act.wait_ge(group_counted, g + 1)
                        act.wait_ge(group_counted, 1)
                        nc.scalar.activation(m.adjT[:, :, bass.ds(g * DG, DG)],
                                             m.ps[0:P, half, 0:GW].rearrange("p (d s) -> p s d", s=T),
                                             ACT.Copy).then_inc(banks_free, 1)


def stage_gates_and_first_sum(nc, m, gate_W, gate_b):
    with ExitStack() as ctx:
        def sb(name, shape, dt=F32):
            return ctx.enter_context(nc.sbuf_tensor(name, shape, dt))

        def sem(name):
            return ctx.enter_context(nc.semaphore(name))

        gw = sb("gw", [128, K, EXPERTS])
        gb = sb("gb", [P, EXPERTS])
        lg = sb("lg", [P, T, EXPERTS])
        top = sb("top", [P, T])
        total = sb("total", [P, T])
        gates = sb("gates", [P, EXPERTS, T])
        rank = sb("rank", [P, EXPERTS, T])
        beats = sb("beats", [P, EXPERTS, T])
        deg_part = sb("deg_part", [P, N])
        inv_row = sb("inv_row", [128, N])
        inv_tmp = sb("inv_tmp", [128, N])
        inv_ctmp = sb("inv_ctmp", [P, T])

        gate_loaded = sem("gate_loaded")
        gate_summed = sem("gate_summed")
        gate_shifted = sem("gate_shifted")
        gate_exp = sem("gate_exp")
        deg_part_ready = sem("deg_part_ready")
        deg_summed = sem("deg_summed")
        sums_ready = sem("sums_ready")
        sums_copied = sem("sums_copied")

        RING = 3
        with nc.Block() as block:
            @block.sync
            def _(sp):
                sp.dma_start(gw[:], gate_W.rearrange("(k p) e -> p k e", p=128)).then_inc(gate_loaded, 16)
                sp.dma_start(gb[:], gate_b.partition_broadcast(P)).then_inc(gate_loaded, 16)

            @block.tensor
            def _(pe):
                pe.wait_ge(gate_loaded, 32)
                for t in range(T):
                    for k in range(K):
                        last = nc.tensor.matmul(m.ps[0:P, 7, t * EXPERTS:(t + 1) * EXPERTS], m.xnT[:, k, tile(t)], gw[:, k, :],
                                                start=(k == 0), stop=(k == K - 1))
                last.then_inc(gate_summed, 1)
                n = 0
                for f in range(K):
                    for c0, cn in CHUNKS:
                        if n == 3:
                            pe.wait_ge(deg_part_ready, 1)
                            for i, (d0, dn) in enumerate(CHUNKS):
                                nc.tensor.matmul(m.ps[:, i, 0:dn], m.ones[0:P, :], deg_part[:, d0:d0 + dn], start=True, stop=True)
                            for t in range(T):
                                last = nc.tensor.matmul(m.ps[0:P, 3, t:t + 1], deg_part[:, tile(t)], m.ones[0:P, 0:1],
                                                        start=True, stop=True)
                            last.then_inc(deg_summed, 1)
                        if n >= RING:
                            pe.wait_ge(sums_copied, n - RING + 1)
                        for s in range(T):
                            last = nc.tensor.matmul(m.ps[:, 4 + n % RING, 0:cn], m.xn[:, s, f * 128:(f + 1) * 128],
                                                    m.adjT[:, s, c0:c0 + cn], start=(s == 0), stop=(s == T - 1))
                        last.then_inc(sums_ready, 1)
                        n += 1

            @block.scalar
            def _(act):
                act.wait_ge(gate_shifted, 1)
                nc.scalar.activation(lg[:], lg[:], ACT.Exp).then_inc(gate_exp, 1)

            @block.vector
            def _(vec):
                nc.vector.tensor_reduce(deg_part[:], m.adjT[:, :, 0:N].rearrange("p s d -> p d s"), X, ALU.add)\
                    .then_inc(deg_part_ready, 1)
                vec.wait_ge(gate_loaded, 32)
                vec.wait_ge(gate_summed, 1)
                nc.vector.tensor_tensor(lg[:], m.ps[0:P, 7, 0:T * EXPERTS].rearrange("p (t e) -> p t e", e=EXPERTS),
                                        gb[:].unsqueeze(1).to_broadcast([P, T, EXPERTS]), ALU.add)
                vec.drain()
                nc.vector.tensor_reduce(top[:], lg[:], X, ALU.max)
                vec.drain()
                nc.vector.tensor_tensor(lg[:], lg[:], top[:].unsqueeze(2).to_broadcast([P, T, EXPERTS]), ALU.subtract)\
                    .then_inc(gate_shifted, 1)
                vec.wait_ge(deg_summed, 1)
                for i, (d0, dn) in enumerate(CHUNKS):
                    nc.vector.tensor_scalar(inv_tmp[:, d0:d0 + dn], m.ps[:, i, 0:dn], 1.0, None, ALU.max)
                nc.vector.tensor_scalar(inv_ctmp[:], m.ps[0:P, 3, 0:T], 1.0, None, ALU.max)
                vec.drain()
                nc.vector.reciprocal(inv_tmp[:], inv_tmp[:])
                nc.vector.reciprocal(inv_ctmp[:], inv_ctmp[:])
                vec.drain()
                for i, (d0, dn) in enumerate(CHUNKS):
                    nc.vector.scalar_tensor_tensor(inv_row[:, d0:d0 + dn], m.ps[:, i, 0:dn], 0.0, inv_tmp[:, d0:d0 + dn],
                                                   ALU.is_gt, ALU.mult)
                nc.vector.scalar_tensor_tensor(m.inv_col[:], m.ps[0:P, 3, 0:T], 0.0, inv_ctmp[:], ALU.is_gt, ALU.mult)
                vec.drain()
                n = 0
                for f in range(K):
                    for c0, cn in CHUNKS:
                        vec.wait_ge(sums_ready, n + 1)
                        nc.vector.tensor_tensor(m.meanT[:, f, c0:c0 + cn], m.ps[:, 4 + n % RING, 0:cn], inv_row[:, c0:c0 + cn],
                                                ALU.mult).then_inc(sums_copied, 1)
                        n += 1
                vec.wait_ge(gate_exp, 1)
                nc.vector.tensor_reduce(total[:], lg[:], X, ALU.add)
                vec.drain()
                nc.vector.reciprocal(total[:], total[:])
                vec.drain()
                for e in range(EXPERTS):
                    nc.vector.tensor_tensor(gates[:, e, :], lg[:, :, e], total[:], ALU.mult)
                vec.drain()
                for e in range(EXPERTS):
                    rest = [f for f in range(EXPERTS) if f != e]
                    for f in rest:
                        nc.vector.tensor_tensor(beats[:, f, :], gates[:, f, :], gates[:, e, :], ALU.is_ge if f < e else ALU.is_gt)
                    vec.drain()
                    nc.vector.tensor_tensor(rank[:, e, :], beats[:, rest[0], :], beats[:, rest[1], :], ALU.add)
                    vec.drain()
                    nc.vector.tensor_tensor(rank[:, e, :], rank[:, e, :], beats[:, rest[2], :], ALU.add)
                    vec.drain()
                    nc.vector.scalar_tensor_tensor(m.gate[:, e, :], rank[:, e, :], 1.5, gates[:, e, :], ALU.is_lt, ALU.mult)


def stage_experts(nc, m, Wl, bl, Wr, gnn_dram):
    with ExitStack() as ctx:
        def sb(name, shape, dt=F32):
            return ctx.enter_context(nc.sbuf_tensor(name, shape, dt))

        def sem(name):
            return ctx.enter_context(nc.semaphore(name))

        wl1 = sb("wl1", [128, K, D])
        wr1 = sb("wr1", [128, K, D])
        wl2 = sb("wl2", [128, K, D])
        wr2 = sb("wr2", [128, K, D])
        bl1 = sb("bl1", [128, K])
        bl2 = sb("bl2", [P, D])
        hT = sb("hT", [128, K, N])
        g = sb("g", [P, T, D])
        acc = sb("acc", [P, T, D])
        o = sb("o", [P, 2, D])

        first_loaded = sem("first_loaded")
        second_loaded = sem("second_loaded")
        h_summed = sem("h_summed")
        h_free = sem("h_free")
        g_summed = sem("g_summed")
        g_free = sem("g_free")
        out_summed = sem("out_summed")
        out_free = sem("out_free")
        out_gated = sem("out_gated")
        out_added = sem("out_added")
        acc_cleared = sem("acc_cleared")
        gnn_stored = sem("gnn_stored")
        NH = K * len(CHUNKS)

        with nc.Block() as block:
            @block.sync
            def _(sp):
                for e in range(EXPERTS):
                    def matrix(W, layer):
                        return W[e, layer].rearrange("(k p) n -> p k n", p=128)

                    if e:
                        sp.wait_ge(h_summed, e * NH)
                        sp.wait_ge(h_free, e * NH + 4)
                    sp.dma_start(wl1[:], matrix(Wl, 0)).then_inc(first_loaded, 16)
                    sp.dma_start(wr1[:], matrix(Wr, 0)).then_inc(first_loaded, 16)
                    sp.dma_start(bl1[:], bl[e, 0].rearrange("(k p) -> p k", p=128)).then_inc(first_loaded, 16)
                    if e:
                        sp.wait_ge(out_summed, e * T)
                        sp.wait_ge(out_added, e * T)
                    sp.dma_start(wl2[:], matrix(Wl, 1)).then_inc(second_loaded, 16)
                    sp.dma_start(wr2[:], matrix(Wr, 1)).then_inc(second_loaded, 16)
                    sp.dma_start(bl2[:], bl[e, 1].partition_broadcast(P)).then_inc(second_loaded, 16)
                sp.wait_ge(out_added, EXPERTS * T)
                sp.dma_start(gnn_dram.rearrange("(t p) d -> p t d", p=P), acc[:]).then_inc(gnn_stored, 16)
                sp.wait_ge(gnn_stored, 16)

            @block.tensor
            def _(pe):
                with pe.Fori(0, EXPERTS) as e:
                    pe.wait_ge(first_loaded, e * 48 + 48)
                    pe.wait_ge(out_free, e * T + 2)
                    n = 0
                    for f in range(K):
                        for c0, cn in CHUNKS:
                            pe.wait_ge(h_free, e * NH + (n + 1))
                            for k in range(K):
                                nc.tensor.matmul(m.ps[:, n % 4, 0:cn], wl1[:, k, f * 128:(f + 1) * 128], m.meanT[:, k, c0:c0 + cn],
                                                 start=(k == 0), stop=False)
                            for k in range(K):
                                last = nc.tensor.matmul(m.ps[:, n % 4, 0:cn], wr1[:, k, f * 128:(f + 1) * 128],
                                                        m.xnT[:, k, c0:c0 + cn], start=False, stop=(k == K - 1))
                            last.then_inc(h_summed, 1)
                            n += 1
                    pe.wait_ge(second_loaded, e * 48 + 48)
                    pe.wait_ge(h_free, e * NH + (NH + 4))
                    for t in range(T):
                        pe.wait_ge(g_free, e * T + (t + 1))
                        for k in range(K):
                            last = nc.tensor.matmul(m.ps[0:P, 4 + t % 2, :], hT[:, k, tile(t)], wl2[:, k, :],
                                                    start=(k == 0), stop=(k == K - 1))
                        last.then_inc(g_summed, 1)
                    for t in range(T):
                        pe.wait_ge(out_free, e * T + (t + 1))
                        for k in range(K):
                            nc.tensor.matmul(m.ps[0:P, t % 2, :], hT[:, k, tile(t)], wr2[:, k, :],
                                             start=(k == 0), stop=(k == K - 1))
                        if t == 0:
                            pe.wait_ge(g_free, e * T + (T + 2))
                        for s in range(T):
                            last = nc.tensor.matmul(m.ps[0:P, 6 + t % 2, :], m.adjT[:, s, tile(t)], g[:, s, :],
                                                    start=(s == 0), stop=(s == T - 1))
                        last.then_inc(out_summed, 1)

            @block.scalar
            def _(act):
                act.sem_inc(h_free, 4)
                act.sem_inc(g_free, 2)
                with act.Fori(0, EXPERTS) as e:
                    act.wait_ge(first_loaded, e * 48 + 48)
                    n = 0
                    for f in range(K):
                        for c0, cn in CHUNKS:
                            act.wait_ge(h_summed, e * NH + (n + 1))
                            nc.scalar.activation(hT[:, f, c0:c0 + cn], m.ps[:, n % 4, 0:cn], ACT.Relu, bias=bl1[:, f:f + 1])\
                                .then_inc(h_free, 1)
                            n += 1
                    for t in range(T):
                        act.wait_ge(g_summed, e * T + (t + 1))
                        nc.scalar.activation(g[:, t, :], m.ps[0:P, 4 + t % 2, :], ACT.Copy).then_inc(g_free, 1)

            @block.vector
            def _(vec):
                vec.sem_inc(out_free, 2)
                with vec.Fori(0, EXPERTS) as e:
                    vec.wait_ge(second_loaded, e * 48 + 48)
                    vec.wait_ge(acc_cleared, 1)
                    for t in range(T):
                        vec.wait_ge(out_summed, e * T + (t + 1))
                        if t >= 2:
                            vec.wait_ge(out_added, e * T + (t - 1))
                        else:
                            vec.wait_ge(out_added, e * T)
                        nc.vector.scalar_tensor_tensor(o[:, t % 2, :], m.ps[0:P, 6 + t % 2, :], m.inv_col[:, t:t + 1], bl2[:],
                                                       ALU.mult, ALU.add)
                        vec.drain()
                        nc.vector.tensor_tensor(o[:, t % 2, :], o[:, t % 2, :], m.ps[0:P, t % 2, :], ALU.add).then_inc(out_free, 1)
                        vec.drain()
                        nc.vector.tensor_scalar(o[:, t % 2, :], o[:, t % 2, :], 0.0, m.gate[:, bass.ds(e, 1), t],
                                                ALU.max, ALU.mult).then_inc(out_gated, 1)

            @block.gpsimd
            def _(pool):
                pool.memset(acc[:], 0.0).then_inc(acc_cleared, 1)
                pool.wait_ge(acc_cleared, 1)
                with pool.Fori(0, EXPERTS) as e:
                    for t in range(T):
                        pool.wait_ge(out_gated, e * T + (t + 1))
                        pool.tensor_tensor(acc[:, t, :], acc[:, t, :], o[:, t % 2, :], ALU.add).then_inc(out_added, 1)


def stage_mixer(nc, m, w, xn_dram):
    with ExitStack() as ctx:
        def sb(name, shape, dt=F32):
            return ctx.enter_context(nc.sbuf_tensor(name, shape, dt))

        def sem(name):
            return ctx.enter_context(nc.semaphore(name))

        xm = m.xm
        region1 = sb("region1", [128, T * D])
        yT = region1[:, 0:K * N].rearrange("p (k n) -> p k n", k=K)
        kp = region1[0:P, :].rearrange("p (t c) -> p t c", t=T)
        oT = yT
        region2 = sb("region2", [128, 2 * K * N])
        qT = region2[:, 0:K * N].rearrange("p (k n) -> p k n", k=K)
        kT = region2[:, K * N:2 * K * N].rearrange("p (k n) -> p k n", k=K)
        w2 = region2[:, 0:FT * D].rearrange("p (f n) -> p f n", f=FT)
        VW = DH + 1
        region3 = sb("region3", [128, T * HEADS * VW + T * D])
        v = region3[0:P, 0:T * HEADS * VW].rearrange("p (t h c) -> p t h c", t=T, h=HEADS)
        z = region3[0:P, T * HEADS * VW:T * HEADS * VW + T * D].rearrange("p (t d) -> p t d", t=T)
        o = z
        hT = region3[:, 0:2 * FT * FCN].rearrange("p (s f n) -> p s f n", s=2, f=FT)
        wq = sb("wq", [128, K, D])
        wo = wq
        wk = sb("wk", [128, K, D])
        wv = sb("wv", [128, K, D])
        w1 = sb("w1", [128, K, FF])
        proj = sb("proj", [128, 2, 2, DH])
        projT = sb("projT", [128, 2 * M])
        halves = sb("halves", [128, 2])
        sq = sb("sq", [128, 2, N])
        qp = sb("qp", [P, 2, 2 * M])
        qpT = sb("qpT", [128, 2, 4 * P])
        context = sb("context", [128, 4, VW])
        CW = 6 * K + FT
        col_rows = sb("col_rows", [DEPTH * CW, 128])
        all_cols = sb("all_cols", [128, DEPTH * CW])
        layer_cols = sb("layer_cols", [128, CW])
        cols = layer_cols[:, 0:4 * K].rearrange("p (a k) -> p a k", a=4)
        qk_bias = layer_cols[:, 4 * K:6 * K].rearrange("p (a k) -> p a k", a=2)
        b1 = layer_cols[:, 6 * K:CW]
        rows = sb("rows", [P, 3, D])
        st = sb("st1", [P, T, 6])
        mv = sb("mv1", [P, T, 2])
        std = sb("std1", [P, T])
        rstd = sb("rstd1", [P, T])
        k_max = sb("k_max", [P, 2, T])
        k_top = sb("k_top", [P, 2])
        k_all = sb("k_all", [P, 2])
        k_shift = sb("k_shift", [P, T, 2])
        q_max = sb("q_max", [P, 2, 2])
        q_shift = sb("q_shift", [P, 2, 2])
        rden = sb("rden", [P, 2, 2])

        x_loaded, cols_loaded, rows_loaded = sem("xm_loaded"), sem("cols_loaded"), sem("rows_loaded")
        qkv_loaded, wo_loaded, w1_loaded, w2_loaded = sem("qkv_loaded"), sem("wo_loaded"), sem("w1_loaded"), sem("w2_loaded")
        proj_loaded = sem("proj_loaded")
        var_ready, std_made, z_ready = sem("var_ready1"), sem("std_made1"), sem("z_ready")
        y_turned, y_free = sem("y_turned"), sem("y_free")
        layer_cols_ready = sem("layer_cols_ready")
        cols_turned = sem("cols_turned")
        qk_summed, qk_free = sem("qk_summed"), sem("qk_free")
        v_summed, v_free = sem("v_summed"), sem("v_free")
        projT_cleared, proj_turned, projT_ready = sem("projT_cleared"), sem("proj_turned"), sem("projT_ready")
        halves_ready = sem("halves_ready")
        squares_ready = sem("squares_ready")
        ks_summed, ks_copied = sem("ks_summed"), sem("ks_copied")
        diag_summed, k_top_ready, k_all_ready, k_shift_ready = sem("diag_summed"), sem("k_top_ready"), sem("k_all_ready"), sem("k_shift_ready")
        k_exp, kp_ready = sem("k_exp"), sem("kp_ready")
        context_summed, context_ready = sem("context_summed"), sem("context_ready")
        qs_summed, q_shift_ready, q_exp, qp_turned, qpT_ready = (
            sem("qs_summed"), sem("q_shift_ready"), sem("q_exp"), sem("qp_turned"), sem("qpT_ready"))
        o_summed, o_ready = sem("o_summed"), sem("o_ready")
        bo_added, b2_added = sem("bo_added"), sem("b2_added")
        o_turned, oT_free = sem("o_turned"), sem("oT_free")
        wo_summed, wo_added = sem("wo_summed"), sem("wo_added")
        h_summed, h_free = sem("ffh_summed"), sem("ffh_free")
        ff_summed, ff_added = sem("ff_summed"), sem("ff_added")

        G = K * len(GROUPS3)
        NQ = K * len(CHUNKS)
        NT = PAIRS * T

        with nc.Block() as block:
            @block.sync
            def _(sp):
                sp.dma_start(xm[:], xn_dram.rearrange("(t p) d -> p t d", p=P)).then_inc(x_loaded, 16)
                for n, a in enumerate(("ln1_g", "ln1_b", "ln2_g", "ln2_b", "bq", "bk")):
                    sp.dma_start(col_rows[n * DEPTH * K:(n + 1) * DEPTH * K, :], w[a].rearrange("l (k p) -> (l k) p", p=128)).then_inc(cols_loaded, 16)
                sp.dma_start(col_rows[6 * DEPTH * K:, :], w["b1"].rearrange("l (f p) -> (l f) p", p=128)).then_inc(cols_loaded, 16)
                for i in range(DEPTH):
                    def matrix(a):
                        return w[a][i].rearrange("(k p) n -> p k n", p=128)

                    if i:
                        sp.wait_ge(wo_summed, i * T)
                    sp.dma_start(wq[:], matrix("Wq")).then_inc(qkv_loaded, 16)
                    sp.dma_start(wk[:], matrix("Wk")).then_inc(qkv_loaded, 16)
                    sp.dma_start(wv[:], matrix("Wv")).then_inc(qkv_loaded, 16)
                    pv = w["proj"][i].rearrange("(a p) d -> p a d", p=128)
                    for c in range(2):
                        sp.dma_start(proj[:, :, c, :], pv).then_inc(proj_loaded, 16)
                    if i:
                        sp.wait_ge(ff_summed, i * T)
                        sp.wait_ge(ff_added, i * T)
                    for j, a in enumerate(("bv", "bo", "b2")):
                        sp.dma_start(rows[:, j], w[a][i].partition_broadcast(P)).then_inc(rows_loaded, 16)
                    sp.dma_start(w1[:], matrix("W1")).then_inc(w1_loaded, 16)
                    sp.wait_ge(qk_summed, i * 2 * NQ + 2 * NQ)
                    sp.dma_start(wo[:], matrix("Wo")).then_inc(wo_loaded, 16)
                    sp.wait_ge(qs_summed, i * NT + NT)
                    sp.wait_ge(squares_ready, i * 2 * PAIRS + 2 * PAIRS)
                    sp.dma_start(w2, matrix("W2")).then_inc(w2_loaded, 16)

            @block.tensor
            def _(pe):
                def turn_rows(i, half):
                    for n, (k, (t0, t1)) in enumerate([(k, g) for k in range(K) for g in GROUPS3]):
                        pe.wait_ge(y_free, i * 2 * G + (half * G + n + 1))
                        pe.wait_ge(z_ready, i * 2 * T + (half * T + t1))
                        for t in range(t0, t1):
                            last = nc.tensor.transpose(m.ps[:, n % 4, (t - t0) * P:(t - t0 + 1) * P], z[:, t, k * 128:(k + 1) * 128],
                                                       m.ident[0:P, 0:P])
                        last.then_inc(y_turned, 1)

                pe.wait_ge(cols_loaded, 112)
                nc.tensor.transpose(m.ps[:, 5, 0:DEPTH * CW], col_rows[:], m.ident[0:DEPTH * CW, 0:DEPTH * CW]).then_inc(cols_turned, 1)
                with pe.Fori(0, DEPTH) as i:
                    pe.wait_ge(proj_loaded, i * 32 + 32)
                    for a in range(2):
                        last = nc.tensor.transpose(m.ps[:, 4, a * 128:(a + 1) * 128], proj[:, a].rearrange("p c d -> p (c d)"), m.ident[:])
                    last.then_inc(proj_turned, 1)
                    pe.wait_ge(wo_added, i * T)
                    pe.wait_ge(ff_added, i * T)
                    turn_rows(i, 0)
                    pe.wait_ge(qkv_loaded, i * 48 + 48)
                    pe.wait_ge(y_free, i * 2 * G + (G + 4))
                    pe.wait_ge(projT_ready, i + 1)
                    n = 0
                    for wt in (wq, wk):
                        for f in range(K):
                            for c0, cn in CHUNKS:
                                pe.wait_ge(qk_free, i * 2 * NQ + (n + 1))
                                for k in range(K):
                                    last = nc.tensor.matmul(m.ps[:, 4 + n % 4, 0:cn], wt[:, k, f * 128:(f + 1) * 128], yT[:, k, c0:c0 + cn],
                                                            start=(k == 0), stop=(k == K - 1))
                                last.then_inc(qk_summed, 1)
                                n += 1
                    for t in range(T):
                        pe.wait_ge(v_free, i * T + (t + 1))
                        for k in range(K):
                            last = nc.tensor.matmul(m.ps[0:P, t % 2, :], yT[:, k, tile(t)], wv[:, k, :], start=(k == 0), stop=(k == K - 1))
                        last.then_inc(v_summed, 1)
                    pe.wait_ge(qk_free, i * 2 * NQ + (2 * NQ + 4))
                    pe.wait_ge(v_free, i * T + (T + 2))
                    for j in range(PAIRS):
                        if j:
                            pe.wait_ge(o_ready, i * NT + j * T)
                        for t in range(T):
                            pe.wait_ge(ks_copied, i * NT + (j * T + t + 1))
                            nc.tensor.matmul(m.ps[0:P, 2 + t % 2, :], kT[:, j, tile(t)], projT[:], start=True, stop=True).then_inc(ks_summed, 1)
                        pe.wait_ge(squares_ready, i * 2 * PAIRS + (2 * j + 2))
                        for a in range(2):
                            for t in range(T):
                                last = nc.tensor.matmul(m.ps[0:P, 4, (a * T + t) * 2:(a * T + t + 1) * 2], sq[:, a, tile(t)], halves[:],
                                                        start=True, stop=True)
                        last.then_inc(diag_summed, 1)
                        pe.wait_ge(kp_ready, i * NT + (j * T + T))
                        for c in range(4):
                            for t in range(T):
                                last = nc.tensor.matmul(m.ps[:, 5, c * VW:(c + 1) * VW], kp[:, t, c * 128:(c + 1) * 128], v[:, t, 2 * j + c // 2, :],
                                                        start=(t == 0), stop=(t == T - 1))
                        last.then_inc(context_summed, 1)
                        for s in range(T + 2):
                            if s < T:
                                if s >= 2:
                                    pe.wait_ge(q_exp, i * NT + (j * T + s - 1))
                                nc.tensor.matmul(m.ps[0:P, 6 + s % 2, :], qT[:, j, tile(s)], projT[:], start=True, stop=True).then_inc(qs_summed, 1)
                            t = s - 1
                            if 0 <= t < T:
                                pe.wait_ge(q_exp, i * NT + (j * T + t + 1))
                                if t >= 2:
                                    pe.wait_ge(qpT_ready, i * NT + (j * T + t - 1))
                                for c in range(4):
                                    last = nc.tensor.transpose(m.ps[:, t % 2, c * P:(c + 1) * P], qp[:, t % 2, c * 128:(c + 1) * 128],
                                                               m.ident[0:P, 0:P])
                                last.then_inc(qp_turned, 1)
                            t = s - 2
                            if 0 <= t < T:
                                if t == 0:
                                    pe.wait_ge(context_ready, i * PAIRS + (j + 1))
                                pe.wait_ge(qpT_ready, i * NT + (j * T + t + 1))
                                if t >= 2:
                                    pe.wait_ge(o_ready, i * NT + (j * T + t - 1))
                                for h in range(2):
                                    for a in range(2):
                                        last = nc.tensor.matmul(m.ps[0:P, 2 + t % 2, h * VW:(h + 1) * VW],
                                                                qpT[:, t % 2, (2 * h + a) * P:(2 * h + a + 1) * P], context[:, 2 * h + a, :],
                                                                start=(a == 0), stop=(a == 1))
                                last.then_inc(o_summed, 1)
                    pe.wait_ge(o_ready, i * NT + NT)
                    for n, (k, (t0, t1)) in enumerate([(k, g) for k in range(K) for g in GROUPS3]):
                        pe.wait_ge(oT_free, i * G + (n + 1))
                        for t in range(t0, t1):
                            last = nc.tensor.transpose(m.ps[:, n % 4, (t - t0) * P:(t - t0 + 1) * P], o[:, t, k * 128:(k + 1) * 128],
                                                       m.ident[0:P, 0:P])
                        last.then_inc(o_turned, 1)
                    pe.wait_ge(wo_loaded, i * 16 + 16)
                    pe.wait_ge(oT_free, i * G + (G + 4))
                    for t in range(T):
                        if t >= 2:
                            pe.wait_ge(wo_added, i * T + (t - 1))
                        for k in range(K):
                            last = nc.tensor.matmul(m.ps[0:P, 4 + t % 2, :], oT[:, k, tile(t)], wo[:, k, :], start=(k == 0), stop=(k == K - 1))
                        last.then_inc(wo_summed, 1)
                    turn_rows(i, 1)
                    pe.wait_ge(y_free, i * 2 * G + (2 * G + 4))
                    pe.wait_ge(w1_loaded, i * 16 + 16)
                    for s in range(FC + 1):
                        if s < FC:
                            for f in range(FT):
                                n = s * FT + f
                                pe.wait_ge(h_free, i * FC * FT + (n + 1))
                                for k in range(K):
                                    last = nc.tensor.matmul(m.ps[:, 4 + n % 4, 0:FCN], w1[:, k, f * 128:(f + 1) * 128],
                                                            yT[:, k, s * FCN:(s + 1) * FCN], start=(k == 0), stop=(k == K - 1))
                                last.then_inc(h_summed, 1)
                        if s == 1:
                            pe.wait_ge(w2_loaded, i * 16 + 16)
                        if s >= 1:
                            pe.wait_ge(h_free, i * FC * FT + (s * FT + 4))
                            for u in range(FCT):
                                t = (s - 1) * FCT + u
                                if t >= 2:
                                    pe.wait_ge(ff_added, i * T + (t - 1))
                                for f in range(FT):
                                    last = nc.tensor.matmul(m.ps[0:P, t % 2, :], hT[:, (s - 1) % 2, f, u * P:(u + 1) * P], w2[:, f, :],
                                                            start=(f == 0), stop=(f == FT - 1))
                                last.then_inc(ff_summed, 1)

            @block.scalar
            def _(act):
                act.sem_inc(y_free, 4)
                act.sem_inc(qk_free, 4)
                act.sem_inc(ks_copied, 2)
                act.sem_inc(oT_free, 4)
                act.sem_inc(h_free, 4)

                def norm_rows(i, half):
                    act.wait_ge(var_ready, i * 2 + half + 1)
                    nc.scalar.activation(std[:], mv[:, :, 1], ACT.Sqrt, bias=m.eps_col[0:P, :]).then_inc(std_made, 1)
                    for n, (k, (t0, t1)) in enumerate([(k, g) for k in range(K) for g in GROUPS3]):
                        act.wait_ge(y_turned, i * 2 * G + (half * G + n + 1))
                        nc.scalar.activation(yT[:, k, t0 * P:t1 * P], m.ps[:, n % 4, 0:(t1 - t0) * P], ACT.Identity,
                                             bias=cols[:, 2 * half + 1, k:k + 1], scale=cols[:, 2 * half, k:k + 1])\
                            .then_inc(y_free, 1)

                with act.Fori(0, DEPTH) as i:
                    act.wait_ge(layer_cols_ready, i + 1)
                    norm_rows(i, 0)
                    n = 0
                    for a, dstT in enumerate((qT, kT)):
                        for f in range(K):
                            for c0, cn in CHUNKS:
                                act.wait_ge(qk_summed, i * 2 * NQ + (n + 1))
                                nc.scalar.activation(dstT[:, f, c0:c0 + cn], m.ps[:, 4 + n % 4, 0:cn], ACT.Identity,
                                                     bias=qk_bias[:, a, f:f + 1], scale=NORM).then_inc(qk_free, 1)
                                n += 1
                    for j in range(PAIRS):
                        for t in range(T):
                            act.wait_ge(ks_summed, i * NT + (j * T + t + 1))
                            nc.scalar.activation(kp[:, t, :], m.ps[0:P, 2 + t % 2, :], ACT.Copy).then_inc(ks_copied, 1)
                        act.drain()
                        act.wait_ge(k_shift_ready, i * PAIRS + (j + 1))
                        for t in range(T):
                            for h in range(2):
                                last = nc.scalar.activation(kp[:, t, h * M:(h + 1) * M], kp[:, t, h * M:(h + 1) * M], ACT.Exp,
                                                            bias=k_shift[:, t, h:h + 1])
                            last.then_inc(k_exp, 1)
                        act.wait_ge(context_summed, i * PAIRS + (j + 1))
                        nc.scalar.activation(context[:], m.ps[:, 5, 0:4 * VW].rearrange("p (c n) -> p c n", c=4), ACT.Copy).then_inc(context_ready, 1)
                        for t in range(T):
                            act.wait_ge(q_shift_ready, i * NT + (j * T + t + 1))
                            if t >= 2:
                                act.wait_ge(qp_turned, i * NT + (j * T + t - 1))
                            for h in range(2):
                                last = nc.scalar.activation(qp[:, t % 2, h * M:(h + 1) * M], m.ps[0:P, 6 + t % 2, h * M:(h + 1) * M], ACT.Exp,
                                                            bias=q_shift[:, t % 2, h:h + 1])
                            last.then_inc(q_exp, 1)
                    for n, (k, (t0, t1)) in enumerate([(k, g) for k in range(K) for g in GROUPS3]):
                        act.wait_ge(o_turned, i * G + (n + 1))
                        nc.scalar.activation(oT[:, k, t0 * P:t1 * P], m.ps[:, n % 4, 0:(t1 - t0) * P], ACT.Copy).then_inc(oT_free, 1)
                    norm_rows(i, 1)
                    for s in range(FC):
                        for f in range(FT):
                            n = s * FT + f
                            act.wait_ge(h_summed, i * FC * FT + (n + 1))
                            if s >= 2 and f == 0:
                                act.wait_ge(ff_summed, i * T + (s - 1) * FCT)
                            nc.scalar.activation(hT[:, s % 2, f, :], m.ps[:, 4 + n % 4, 0:FCN], ACT.Gelu, bias=b1[:, f:f + 1])\
                                .then_inc(h_free, 1)

            @block.vector
            def _(vec):
                vec.sem_inc(v_free, 2)
                nc.vector.memset(projT[:], 0.0)
                nc.vector.memset(halves[:], 0.0)
                vec.drain()
                for h in range(2):
                    last = nc.vector.memset(halves[h * DH:(h + 1) * DH, h:h + 1], 0.5)
                last.then_inc(halves_ready, 1)
                vec.wait_ge(cols_turned, 1)
                nc.vector.tensor_copy(all_cols[:], m.ps[:, 5, 0:DEPTH * CW])
                vec.drain()
                vec.wait_ge(x_loaded, 16)

                def norm_rows(i, half):
                    emit_norm_stats(nc, vec, std_made, var_ready, i * 2 + half + 1, xm, st, mv, rstd, std)
                    for t in range(T):
                        nc.vector.tensor_scalar(z[:, t, :], xm[:, t, :], mv[:, t, 0:1], rstd[:, t:t + 1],
                                                ALU.subtract, ALU.mult).then_inc(z_ready, 1)

                with vec.Fori(0, DEPTH) as i:
                    nc.vector.tensor_copy(layer_cols[:, 0:6 * K].rearrange("p (a k) -> p a k", a=6),
                                          all_cols[:, 0:6 * DEPTH * K].rearrange("p (a l k) -> p l a k", a=6, l=DEPTH)[:, bass.ds(i, 1)]
                                          .rearrange("p o a k -> p (o a) k"))
                    nc.vector.tensor_copy(b1, all_cols[:, 6 * DEPTH * K:].rearrange("p (l f) -> p l f", l=DEPTH)[:, bass.ds(i, 1)]
                                          .rearrange("p o f -> p (o f)"))
                    vec.drain()
                    nc.vector.tensor_scalar(qk_bias, qk_bias, NORM, None, ALU.mult).then_inc(layer_cols_ready, 1)
                    norm_rows(i, 0)
                    vec.wait_ge(proj_turned, i + 1)
                    for h in range(2):
                        last = nc.vector.tensor_copy(projT[h * DH:(h + 1) * DH, h * M:(h + 1) * M], m.ps[h * DH:(h + 1) * DH, 4, 0:M])
                    last.then_inc(projT_ready, 1)
                    vec.wait_ge(rows_loaded, i * 48 + 48)
                    for t in range(T):
                        vec.wait_ge(v_summed, i * T + (t + 1))
                        if t == 0:
                            nc.vector.memset(v[:, :, :, DH:VW], 1.0)
                        nc.vector.tensor_tensor(v[:, t, :, 0:DH], m.ps[0:P, t % 2, :].rearrange("p (h c) -> p h c", h=HEADS),
                                                rows[:, 0, :].rearrange("p (h c) -> p h c", h=HEADS), ALU.add).then_inc(v_free, 1)
                    for j in range(PAIRS):
                        for t in range(T):
                            vec.wait_ge(ks_copied, i * NT + (j * T + t + 3))
                            nc.vector.tensor_reduce(k_max[:, :, t], kp[:, t, :].rearrange("p (h c) -> p h c", h=2), X, ALU.max)
                        vec.drain()
                        nc.vector.tensor_reduce(k_top[:], k_max[:], X, ALU.max).then_inc(k_top_ready, 1)
                        vec.wait_ge(diag_summed, i * PAIRS + (j + 1))
                        vec.wait_ge(k_all_ready, i * PAIRS + (j + 1))
                        for h in range(2):
                            last = nc.vector.tensor_scalar(k_shift[:, :, h], m.ps[0:P, 4, 0:2 * T].rearrange("p (t h) -> p t h", h=2)[:, :, h],
                                                           k_all[:, h:h + 1], -1.0, ALU.add, ALU.mult)
                        last.then_inc(k_shift_ready, 1)
                        for s in range(T + 2):
                            if s < T:
                                vec.wait_ge(qs_summed, i * NT + (j * T + s + 1))
                                nc.vector.tensor_reduce(q_max[:, s % 2, :], m.ps[0:P, 6 + s % 2, :].rearrange("p (h c) -> p h c", h=2), X, ALU.max)
                                vec.drain()
                                if s >= 2:
                                    vec.wait_ge(q_exp, i * NT + (j * T + s - 1))
                                nc.vector.scalar_tensor_tensor(q_shift[:, s % 2, :], q_max[:, s % 2, :], -1.0,
                                                               m.ps[0:P, 4, (T + s) * 2:(T + s + 1) * 2], ALU.mult, ALU.subtract)\
                                    .then_inc(q_shift_ready, 1)
                            t = s - 1
                            if 0 <= t < T:
                                vec.wait_ge(qp_turned, i * NT + (j * T + t + 1))
                                if t >= 2:
                                    vec.wait_ge(o_summed, i * NT + (j * T + t - 1))
                                nc.vector.tensor_scalar(qpT[:, t % 2, :], m.ps[:, t % 2, 0:4 * P], FEATURE_EPS, None, ALU.add).then_inc(qpT_ready, 1)
                            t = s - 2
                            if 0 <= t < T:
                                vec.wait_ge(o_summed, i * NT + (j * T + t + 1))
                                ov = m.ps[0:P, 2 + t % 2, 0:2 * VW].rearrange("p (h c) -> p h c", h=2)
                                nc.vector.reciprocal(rden[:, t % 2, :], ov[:, :, DH])
                                vec.drain()
                                for h in range(2):
                                    last = nc.vector.tensor_scalar(o[:, t, (2 * j + h) * DH:(2 * j + h + 1) * DH], ov[:, h, 0:DH],
                                                                   rden[:, t % 2, h:h + 1], None, ALU.mult)
                                last.then_inc(o_ready, 1)
                    vec.wait_ge(bo_added, i * T + T)
                    for t in range(T):
                        vec.wait_ge(wo_summed, i * T + (t + 1))
                        nc.vector.tensor_tensor(xm[:, t, :], xm[:, t, :], m.ps[0:P, 4 + t % 2, :], ALU.add).then_inc(wo_added, 1)
                    vec.drain()
                    vec.wait_ge(o_turned, i * G + G)
                    norm_rows(i, 1)
                    vec.wait_ge(b2_added, i * T + T)
                    for t in range(T):
                        vec.wait_ge(ff_summed, i * T + (t + 1))
                        nc.vector.tensor_tensor(xm[:, t, :], xm[:, t, :], m.ps[0:P, t % 2, :], ALU.add).then_inc(ff_added, 1)
                    vec.drain()

            @block.gpsimd
            def _(pool):
                pool.wait_ge(x_loaded, 16)
                for i in range(DEPTH):
                    pool.wait_ge(rows_loaded, i * 48 + 48)
                    for j in range(PAIRS):
                        pool.wait_ge(qk_free, i * 2 * NQ + (2 * NQ + 4))
                        if j:
                            pool.wait_ge(diag_summed, i * PAIRS + j)
                        for a, srcT in enumerate((kT, qT)):
                            pool.tensor_tensor(sq[:, a, :], srcT[:, j, :], srcT[:, j, :], ALU.mult).then_inc(squares_ready, 1)
                        pool.wait_ge(k_top_ready, i * PAIRS + (j + 1))
                        pool.partition_all_reduce(k_all[:], k_top[:], P, MAX_REDUCE).then_inc(k_all_ready, 1)
                        for t in range(T):
                            pool.wait_ge(k_exp, i * NT + (j * T + t + 1))
                            pool.tensor_scalar(kp[:, t, :], kp[:, t, :], FEATURE_EPS, 1.0, ALU.add, ALU.mult).then_inc(kp_ready, 1)
                    pool.wait_ge(z_ready, i * 2 * T + T)
                    for t in range(T):
                        pool.tensor_tensor(xm[:, t, :], xm[:, t, :], rows[:, 1, :], ALU.add).then_inc(bo_added, 1)
                    pool.wait_ge(z_ready, i * 2 * T + 2 * T)
                    for t in range(T):
                        pool.tensor_tensor(xm[:, t, :], xm[:, t, :], rows[:, 2, :], ALU.add).then_inc(b2_added, 1)


def stage_shift_unit(nc, m, x, gnn_dram, out):
    MARK, SHL, SHR, LO, DIGITS, OUT = 0, 39, 40, 64, 16, 128
    with ExitStack() as ctx:
        def sb(name, shape, dt=F32):
            return ctx.enter_context(nc.sbuf_tensor(name, shape, dt))

        def sem(name):
            return ctx.enter_context(nc.semaphore(name))

        y = sb("y", [P, T, D])
        gnn = sb("gnn", [P, T, D])
        ln = sb("ln", [P, T, D])
        st = sb("st2", [P, T, 6])
        mv = sb("mv2", [P, T, 2])
        std = sb("std2", [P, T])
        rstd = sb("rstd2", [P, T])
        count_i = sb("count_i", [P, 2, DIGITS], I32)
        down = sb("down", [P, DIGITS])
        up = sb("up", [P, DIGITS])
        first = sb("first", [P, T, 3, DIGITS])
        best = sb("best", [P, T, 3])
        found = sb("found", [P, T, 3])
        digit = sb("digit", [P, T, 3])
        flag = sb("flag", [P, 5, T])
        value = sb("value", [P, T])
        value_i = sb("value_i", [P, 2, T], I32)
        shift_i = sb("amount_i", [P, T], I32)
        shifted_i = sb("shifted_i", [P, 2, T], I32)
        shifted = sb("shifted", [P, 2, T])
        result = sb("result", [P, T])
        result_i = sb("result_i", [P, T], I32)
        nibble_i = sb("nibble_i", [P, 2, T], I32)
        nibble = sb("nibble", [P, 2, T])
        amp = sb("amp", [P, T])
        hot = sb("hot2", [P, T, 2, DIGITS])

        x_loaded, gnn_loaded = sem("y_loaded"), sem("gnn_loaded")
        counts_made, var_ready, std_made = sem("counts_made"), sem("var_ready2"), sem("std_made2")
        out_ready, out_stored = sem("out_ready"), sem("out_stored")
        xv = x.rearrange("(t p) d -> p t d", p=P)
        ov = out.rearrange("(t p) d -> p t d", p=P)

        with nc.Block() as block:
            @block.sync
            def _(sp):
                sp.dma_start(y[:], xv).then_inc(x_loaded, 16)
                sp.dma_start(gnn[:], gnn_dram.rearrange("(t p) d -> p t d", p=P)).then_inc(gnn_loaded, 16)
                for h in range(2):
                    a, b = h * T // 2, (h + 1) * T // 2
                    sp.wait_ge(out_ready, b)
                    sp.dma_start(ov[:, a:b, :], ln[:, a:b, :]).then_inc(out_stored, 16)
                sp.wait_ge(out_stored, 32)

            @block.gpsimd
            def _(pool):
                pool.iota(count_i[:, 0], pattern=[[-1, DIGITS]], base=DIGITS, channel_multiplier=0).then_inc(counts_made, 1)
                pool.iota(count_i[:, 1], pattern=[[1, DIGITS]], base=0, channel_multiplier=0).then_inc(counts_made, 1)

            @block.scalar
            def _(act):
                act.wait_ge(var_ready, 1)
                nc.scalar.activation(std[:], mv[:, :, 1], ACT.Sqrt, bias=m.eps_col[0:P, :]).then_inc(std_made, 1)

            @block.vector
            def _(vec):
                v = nc.vector
                vec.wait_ge(counts_made, 2)
                v.tensor_copy(down[:], count_i[:, 0])
                v.tensor_copy(up[:], count_i[:, 1])
                vec.wait_ge(x_loaded, 16)
                vec.wait_ge(gnn_loaded, 16)
                for t in range(T):
                    v.tensor_tensor(y[:, t, :], y[:, t, :], gnn[:, t, :], ALU.add)
                vec.drain()
                for t in range(T):
                    v.tensor_tensor(y[:, t, :], y[:, t, :], m.xm[:, t, :], ALU.add)
                vec.drain()
                emit_norm_stats(nc, vec, std_made, var_ready, 1, y, st, mv, rstd, std)
                for t in range(T):
                    v.tensor_scalar(ln[:, t, :], y[:, t, :], mv[:, t, 0:1], rstd[:, t:t + 1], ALU.subtract, ALU.mult)
                vec.drain()
                v.scalar_tensor_tensor(first[:].rearrange("p t a d -> p t (a d)"), ln[:, :, LO:LO + 3 * DIGITS], 0.5,
                                       ln[:, :, LO:LO + 3 * DIGITS], ALU.is_gt, ALU.bypass)
                for n, c in enumerate((MARK, SHL, SHR)):
                    v.tensor_scalar(flag[:, n, :], ln[:, :, c], 0.5, None, ALU.is_gt)
                vec.drain()
                for a in range(3):
                    v.tensor_tensor(first[:, :, a, :], first[:, :, a, :], down[:].unsqueeze(1).to_broadcast([P, T, DIGITS]), ALU.mult)
                vec.drain()
                v.tensor_reduce(best[:], first[:], X, ALU.max)
                vec.drain()
                v.tensor_scalar(found[:], best[:], 0.0, None, ALU.is_gt)
                v.tensor_scalar(digit[:], best[:], -1.0, float(DIGITS), ALU.mult, ALU.add)
                vec.drain()
                v.tensor_tensor(digit[:], digit[:], found[:], ALU.mult)
                vec.drain()
                v.scalar_tensor_tensor(value[:], digit[:, :, 1], float(DIGITS), digit[:, :, 0], ALU.mult, ALU.add)
                v.tensor_copy(shift_i[:], digit[:, :, 2])
                vec.drain()
                v.tensor_copy(value_i[:, 0], value[:])
                vec.drain()
                v.tensor_tensor(shifted_i[:, 0], value_i[:, 0], shift_i[:], ALU.logical_shift_left)
                v.tensor_tensor(shifted_i[:, 1], value_i[:, 0], shift_i[:], ALU.logical_shift_right)
                v.tensor_tensor(flag[:, 3, :], flag[:, 0, :], flag[:, 1, :], ALU.mult)
                v.tensor_tensor(flag[:, 4, :], flag[:, 0, :], flag[:, 2, :], ALU.mult)
                vec.drain()
                v.tensor_scalar(shifted_i[:, 0], shifted_i[:, 0], 255, None, ALU.bitwise_and)
                v.tensor_tensor(flag[:, 4, :], flag[:, 4, :], flag[:, 3, :], ALU.is_gt)
                vec.drain()
                v.tensor_copy(shifted[:], shifted_i[:])
                v.tensor_tensor(amp[:], flag[:, 3, :], flag[:, 4, :], ALU.add)
                vec.drain()
                v.tensor_tensor(shifted[:], shifted[:], flag[:, 3:5, :], ALU.mult)
                v.tensor_scalar(amp[:], amp[:], 2.0, None, ALU.mult)
                vec.drain()
                v.tensor_tensor(result[:], shifted[:, 0], shifted[:, 1], ALU.add)
                vec.drain()
                v.tensor_copy(result_i[:], result[:])
                vec.drain()
                v.tensor_scalar(nibble_i[:, 0], result_i[:], 15, None, ALU.bitwise_and)
                v.tensor_scalar(nibble_i[:, 1], result_i[:], 4, None, ALU.logical_shift_right)
                vec.drain()
                v.tensor_copy(nibble[:], nibble_i[:])
                vec.drain()
                for a in range(2):
                    v.tensor_tensor(hot[:, :, a, :], up[:].unsqueeze(1).to_broadcast([P, T, DIGITS]),
                                    nibble[:, a, :].unsqueeze(2).to_broadcast([P, T, DIGITS]), ALU.is_equal)
                vec.drain()
                for a in range(2):
                    v.tensor_tensor(hot[:, :, a, :], hot[:, :, a, :], amp[:].unsqueeze(2).to_broadcast([P, T, DIGITS]), ALU.mult)
                vec.drain()
                v.tensor_tensor(ln[:, :, OUT:OUT + 2 * DIGITS], ln[:, :, OUT:OUT + 2 * DIGITS],
                                hot[:].rearrange("p t a d -> p t (a d)"), ALU.add)
                vec.drain()
                for t in range(T):
                    v.tensor_tensor(ln[:, t, :], ln[:, t, :], y[:, t, :], ALU.add).then_inc(out_ready, 1)


def gps_block(nc, a, out):
    xn_dram = nc.dram_tensor("xn_dram", [N, D], F32, kind="Internal").ap()
    gnn_dram = nc.dram_tensor("gnn_dram", [N, D], F32, kind="Internal").ap()
    with ExitStack() as ctx:
        ctx.enter_context(nc.allow_non_contiguous_dma(reason="bias vectors, one feature per partition"))

        def sb(name, shape, dt=F32):
            return ctx.enter_context(nc.sbuf_tensor(name, shape, dt))

        m = OnChip()
        m.ps = ctx.enter_context(nc.psum_tensor("ps", [128, 8, 512], F32))
        m.ident = sb("ident", [128, 128])
        m.ones = sb("ones", [128, 128])
        m.eps_col = sb("eps_col", [128, 1])
        with ExitStack() as graph:
            def gsb(name, shape, dt=F32):
                return graph.enter_context(nc.sbuf_tensor(name, shape, dt))

            m.adjT = gsb("adjT", [P, T, NPAD])
            m.xnT = gsb("xnT", [128, K, N])
            m.meanT = gsb("meanT", [128, K, N])
            m.inv_col = gsb("inv_col", [P, T])
            m.gate = gsb("gate", [P, EXPERTS, T])
            with ExitStack() as counting:
                def csb(name, shape, dt=F32):
                    return counting.enter_context(nc.sbuf_tensor(name, shape, dt))

                m.xn = csb("xn", [P, T, D])
                m.src_rowT = csb("src_rowT", [CE, NC])
                m.keyT = csb("keyT", [CE, NC])
                m.shift = csb("shift", [P, NG])
                m.hot = csb("hot", [P, GW], F16)
                m.ranges = csb("ranges", [1, 3, NG], I32)
                stage_normalise_and_index(nc, m, a["x"], a["src"], a["dst"], xn_dram)
                stage_count_edges(nc, m)
                stage_gates_and_first_sum(nc, m, a["L0_gnn_gate_W"], a["L0_gnn_gate_b"])
            stage_experts(nc, m, a["L0_gnn_Wl"], a["L0_gnn_bl"], a["L0_gnn_Wr"], gnn_dram)
        m.xm = sb("xm", [P, T, D])
        stage_mixer(nc, m, {k[len("L0_mix_"):]: v for k, v in a.items() if k.startswith("L0_mix_")}, xn_dram)
        stage_shift_unit(nc, m, a["x"], gnn_dram, out)


_INS = ["x", "src", "dst", "L0_gnn_gate_W", "L0_gnn_gate_b", "L0_gnn_Wl", "L0_gnn_bl", "L0_gnn_Wr", "L0_mix_ln1_g", "L0_mix_ln1_b",
        "L0_mix_ln2_g", "L0_mix_ln2_b", "L0_mix_Wq", "L0_mix_bq", "L0_mix_Wk", "L0_mix_bk", "L0_mix_Wv", "L0_mix_bv",
        "L0_mix_Wo", "L0_mix_bo", "L0_mix_proj", "L0_mix_W1", "L0_mix_b1", "L0_mix_W2", "L0_mix_b2"]


def kernel(**inputs):
    import concourse.bacc as bacc
    from concourse.bass_utils import run_bass_kernel_spmd

    nc = bacc.Bacc("TRN2", target_bir_lowering=False, num_devices=1)
    arrays, args = {}, {}
    for name in _INS:
        arr = np.ascontiguousarray(inputs[name])
        arrays["in_" + name] = arr
        args[name] = nc.dram_tensor("in_" + name, arr.shape, mybir.dt.from_np(arr.dtype), kind="ExternalInput").ap()
    out = nc.dram_tensor("out", (N, D), F32, kind="ExternalOutput").ap()
    gps_block(nc, args, out)
    r = run_bass_kernel_spmd(nc, [arrays], core_ids=[0])
    return r.results[0]["out"]
```

```python
from contextlib import ExitStack

import numpy as np

import concourse.bass as bass
from concourse import mybir

F32 = mybir.dt.float32
F32R = mybir.dt.float32r
F16 = mybir.dt.float16
BF16 = mybir.dt.bfloat16
I32 = mybir.dt.int32
ACT = mybir.ActivationFunctionType
ALU = mybir.AluOpType
X = mybir.AxisListType.X
MAX_REDUCE = bass.bass_isa.ReduceOp.max

N, D, E = 1250, 512, 40000
T = 10
P = N // T
K = D // 128
CHUNKS = ((0, 500), (500, 500), (1000, 250))
GROUPS3 = ((0, 4), (4, 8), (8, 10))

CE = 125
NC = E // CE
CQ, CR = 4, NC // 4
B = 5
NB = NC // B
DG = 32
NG = -(-N // DG)
GW = DG * T
NPAD = NG * DG
SLOTS = 4

EXPERTS = 4
DEPTH, HEADS, DH, M = 2, 8, 64, 256
PAIRS = HEADS // 2
FF = 2048
FT = FF // 128
NORM = float(DH) ** -0.25
FEATURE_EPS = 1e-4
LN_EPS = 1e-5
FC, FCN = 5, 250
FCT = FCN // P


class OnChip:
    pass


def tile(t):
    return slice(t * P, (t + 1) * P)


def emit_norm_stats(nc, vec, act_done, std_ready, seen, src, st, mv, rstd, std):
    for t in range(T):
        last = nc.vector.bn_stats(st[:, t, :], src[:, t, :])
    vec.drain()
    for t in range(T):
        last = nc.vector.bn_aggr(mv[:, t, :], st[:, t, :])
    last.then_inc(std_ready, 1)
    vec.wait_ge(act_done, seen)
    nc.vector.reciprocal(rstd[:], std[:])
    vec.drain()


def stage_normalise_and_index(nc, m, x, src, dst, xn_dram):
    with ExitStack() as ctx:
        def sb(name, shape, dt=F32):
            return ctx.enter_context(nc.sbuf_tensor(name, shape, dt))

        def sem(name):
            return ctx.enter_context(nc.semaphore(name))

        x_in = sb("x_in", [P, T, D])
        st = sb("st0", [P, T, 6])
        mv = sb("mv0", [P, T, 2])
        std = sb("std0", [P, T])
        rstd = sb("rstd0", [P, T])
        edge_i = sb("edge_i", [CR, 2, CQ, CE], I32)
        edge_f = sb("edge_f", [CR, 2, CQ, CE])
        src_tile = sb("src_tile", [CR, CQ, CE])
        src_row = sb("src_row", [CR, CQ, CE])
        key = sb("key", [CR, CQ, CE])
        chunk_min = sb("chunk_min", [CR, CQ])
        chunk_max = sb("chunk_max", [CR, CQ])
        step_i = sb("step_i", [CR, CQ, CR // B], I32)
        step_f = sb("step_f", [CR, CQ, CR // B])
        step_of = sb("step_of", [CR, CQ])
        step_up = sb("step_up", [CR, CQ])
        step_down = sb("step_down", [CR, CQ])
        group_i = sb("group_i", [CR, NG], I32)
        group_lo = sb("group_lo", [CR, NG])
        group_hi = sb("group_hi", [CR, NG])
        cand = sb("cand", [CR, 2, CQ, NG])
        ends = sb("ends", [CR, 2, NG])
        ends_all = sb("ends_all", [CR, 2, NG])
        rng = sb("rng", [1, 6, NG])
        shift_i = sb("shift_i", [P, NG], I32)
        hot_i = sb("hot_i", [P, GW], I32)

        x_loaded = [sem("x_loaded0"), sem("x_loaded1")]
        edges_loaded = sem("edges_loaded")
        consts_made = sem("consts_made")
        ident_cleared = sem("ident_cleared")
        var_ready = sem("var_ready")
        std_made = sem("std_made")
        xn_ready = sem("xn_ready")
        xn_turned = sem("xn_turned")
        xnT_copied = sem("xnT_copied")
        keys_ready = sem("keys_ready")
        keys_turned = sem("keys_turned")
        ends_local = sem("ends_local")
        ends_global = sem("ends_global")
        xn_stored = sem("xn_stored")

        xv = x.rearrange("(t p) d -> p t d", p=P)
        H = T // 2
        with nc.Block() as block:
            @block.sync
            def _(sp):
                for h in range(2):
                    sp.dma_start(x_in[:, h * H:(h + 1) * H, :], xv[:, h * H:(h + 1) * H, :]).then_inc(x_loaded[h], 16)
                for n, a in enumerate((src, dst)):
                    sp.dma_start(edge_i[:, n], a.rearrange("(q r e) -> r q e", q=CQ, e=CE)).then_inc(edges_loaded, 16)
                sp.wait_ge(xn_ready, T)
                sp.dma_start(xn_dram.rearrange("(t p) d -> p t d", p=P), m.xn[:]).then_inc(xn_stored, 16)
                sp.wait_ge(xn_stored, 16)

            @block.gpsimd
            def _(pool):
                pool.memset(m.ident[:], 0.0).then_inc(ident_cleared, 1)
                pool.wait_ge(ident_cleared, 1)
                pool.affine_select(out=m.ident[:], in_=m.ident[:], compare_op=ALU.not_equal, fill=1.0,
                                   base=0, pattern=[[-1, 128]], channel_multiplier=1).then_inc(consts_made, 1)
                pool.memset(m.ones[:], 1.0).then_inc(consts_made, 1)
                pool.memset(m.eps_col[:], LN_EPS).then_inc(consts_made, 1)
                pool.iota(step_i[:], pattern=[[0, CQ], [-B, CR // B]], base=-B, channel_multiplier=1).then_inc(consts_made, 1)
                pool.iota(group_i[:], pattern=[[DG, NG]], base=0, channel_multiplier=0).then_inc(consts_made, 1)
                pool.iota(shift_i[:], pattern=[[-GW, NG]], base=0, channel_multiplier=0).then_inc(consts_made, 1)
                pool.iota(hot_i[:], pattern=[[1, GW]], base=0, channel_multiplier=0).then_inc(consts_made, 1)
                pool.wait_ge(ends_local, 1)
                pool.partition_all_reduce(ends_all[:], ends[:], CR, MAX_REDUCE).then_inc(ends_global, 1)

            @block.scalar
            def _(act):
                act.wait_ge(consts_made, 7)
                act.wait_ge(var_ready, 1)
                nc.scalar.activation(std[:], mv[:, :, 1], ACT.Sqrt, bias=m.eps_col[0:P, :]).then_inc(std_made, 1)
                for t in range(T):
                    act.wait_ge(xn_turned, t + 1)
                    nc.scalar.activation(m.xnT[:, :, tile(t)],
                                         m.ps[:, t % 4, 0:D // 128 * P].rearrange("p (k n) -> p k n", k=K),
                                         ACT.Copy).then_inc(xnT_copied, 1)

            @block.vector
            def _(vec):
                vec.wait_ge(consts_made, 7)
                for h in range(2):
                    vec.wait_ge(x_loaded[h], 16)
                emit_norm_stats(nc, vec, std_made, var_ready, 1, x_in, st, mv, rstd, std)
                for t in range(T):
                    nc.vector.tensor_scalar(m.xn[:, t, :], x_in[:, t, :], mv[:, t, 0:1], rstd[:, t:t + 1],
                                            ALU.subtract, ALU.mult).then_inc(xn_ready, 1)

                vec.wait_ge(edges_loaded, 32)
                nc.vector.tensor_copy(edge_f[:], edge_i[:])
                vec.drain()
                nc.vector.tensor_scalar(src_tile[:], edge_f[:, 0], float(P), None, ALU.is_ge)
                for k in range(2, T):
                    vec.drain()
                    nc.vector.scalar_tensor_tensor(src_tile[:], edge_f[:, 0], float(k * P), src_tile[:], ALU.is_ge, ALU.add)
                vec.drain()
                nc.vector.scalar_tensor_tensor(src_row[:], src_tile[:], -float(P), edge_f[:, 0], ALU.mult, ALU.add)
                nc.vector.scalar_tensor_tensor(key[:], edge_f[:, 1], float(T), src_tile[:], ALU.mult, ALU.add)\
                    .then_inc(keys_ready, 1)

                nc.vector.tensor_reduce(chunk_min[:], edge_f[:, 1], X, ALU.min)
                nc.vector.tensor_reduce(chunk_max[:], edge_f[:, 1], X, ALU.max)
                nc.vector.tensor_copy(step_f[:], step_i[:])
                nc.vector.tensor_copy(group_lo[:], group_i[:])
                vec.drain()
                nc.vector.tensor_scalar(step_f[:], step_f[:], 0.0, None, ALU.is_ge)
                nc.vector.tensor_scalar(group_hi[:], group_lo[:], float(DG), None, ALU.add)
                vec.drain()
                nc.vector.tensor_reduce(step_of[:], step_f[:], X, ALU.add)
                vec.drain()
                for q in range(CQ):
                    nc.vector.tensor_scalar(step_up[:, q:q + 1], step_of[:, q:q + 1], float(q * CR // B + 1), None, ALU.add)
                vec.drain()
                nc.vector.tensor_scalar(step_down[:], step_up[:], -1.0, float(NB + 1), ALU.mult, ALU.add)
                vec.drain()
                for q in range(CQ):
                    nc.vector.tensor_scalar(cand[:, 0, q, :], group_lo[:], chunk_max[:, q:q + 1], step_down[:, q:q + 1],
                                            ALU.is_le, ALU.mult)
                    nc.vector.tensor_scalar(cand[:, 1, q, :], group_hi[:], chunk_min[:, q:q + 1], step_up[:, q:q + 1],
                                            ALU.is_gt, ALU.mult)
                vec.drain()
                for n in range(2):
                    nc.vector.tensor_reduce(ends[:, n, :], cand[:, n].rearrange("p q g -> p g q"), X, ALU.max)\
                        .then_inc(ends_local, 1) if n else \
                        nc.vector.tensor_reduce(ends[:, n, :], cand[:, n].rearrange("p q g -> p g q"), X, ALU.max)
                nc.vector.tensor_copy(m.shift[:], shift_i[:])
                nc.vector.tensor_copy(m.hot[:], hot_i[:])
                vec.wait_ge(ends_global, 1)
                nc.vector.tensor_scalar(rng[:, 0], ends_all[0:1, 0], -1.0, float(NB), ALU.mult, ALU.add)
                vec.drain()
                nc.vector.tensor_scalar(rng[:, 0], rng[:, 0], float(NB - 1), None, ALU.min)
                vec.drain()
                nc.vector.tensor_tensor(rng[:, 1], ends_all[0:1, 1], rng[:, 0], ALU.subtract)
                vec.drain()
                nc.vector.tensor_scalar(rng[:, 1], rng[:, 1], 1.0, None, ALU.max)
                vec.drain()
                at, width = 1, 1
                while width < NG:
                    to = 2 if at != 2 else 3
                    nc.vector.tensor_copy(rng[:, to, 0:width], rng[:, at, 0:width])
                    nc.vector.tensor_tensor(rng[:, to, width:NG], rng[:, at, width:NG], rng[:, at, 0:NG - width], ALU.add)
                    vec.drain()
                    at, width = to, 2 * width
                nc.vector.tensor_tensor(rng[:, 4], rng[:, at], rng[:, 1], ALU.subtract)
                vec.drain()
                nc.vector.tensor_copy(m.ranges[:, 0], rng[:, 0])
                nc.vector.tensor_copy(m.ranges[:, 1], rng[:, 1])
                nc.vector.tensor_copy(m.ranges[:, 2], rng[:, 4])
                vec.wait_ge(keys_turned, 1)
                nc.vector.tensor_copy(m.src_rowT[:], m.ps[0:CE, 4, 0:NC])
                nc.vector.tensor_copy(m.keyT[:], m.ps[0:CE, 5, 0:NC])

            @block.tensor
            def _(pe):
                pe.wait_ge(consts_made, 7)
                for t in range(T):
                    pe.wait_ge(xn_ready, t + 1)
                    if t >= 4:
                        pe.wait_ge(xnT_copied, t - 3)
                    for k in range(K):
                        last = nc.tensor.transpose(m.ps[:, t % 4, k * P:(k + 1) * P], m.xn[:, t, k * 128:(k + 1) * 128],
                                                   m.ident[0:P, 0:P])
                    last.then_inc(xn_turned, 1)
                pe.wait_ge(keys_ready, 1)
                for n, a in enumerate((src_row, key)):
                    for q in range(CQ):
                        last = nc.tensor.transpose(m.ps[0:CE, 4 + n, q * CR:(q + 1) * CR], a[:, q, :], m.ident[0:CR, 0:CR])
                last.then_inc(keys_turned, 1)


def stage_count_edges(nc, m):
    with ExitStack() as ctx:
        def sem(name):
            return ctx.enter_context(nc.semaphore(name))

        row_hot = ctx.enter_context(nc.sbuf_tensor("row_hot", [CE, SLOTS, B, P], BF16))
        key_hot = ctx.enter_context(nc.sbuf_tensor("key_hot", [CE, SLOTS, B, GW], BF16))
        zeros = ctx.enter_context(nc.sbuf_tensor("zeros", [CE, GW], BF16))
        hots_ready = sem("hots_ready")
        slots_free = sem("slots_free")
        group_counted = sem("group_counted")
        banks_free = sem("banks_free")
        zeroed = sem("zeroed")

        with nc.Block() as block:
            @block.vector
            def _(vec):
                nc.vector.memset(zeros[:], 0.0).then_inc(zeroed, 1)
                with vec.Fori(0, NG) as g:
                    lo = vec.value_load(m.ranges[0:1, 0, bass.ds(g, 1)], min_val=0, max_val=NB - 1)
                    steps = vec.value_load(m.ranges[0:1, 1, bass.ds(g, 1)], min_val=1, max_val=NB)
                    before = vec.value_load(m.ranges[0:1, 2, bass.ds(g, 1)], min_val=0, max_val=NB * NG)
                    with vec.Fori(0, steps) as j:
                        vec.wait_ge(slots_free, before + j + 1)
                        slot = (before + j) & (SLOTS - 1)
                        step = nc.s_assert_within(lo + j, 0, NB - 1, skip_runtime_bounds_check_because="lo + steps <= NB")
                        for b in range(B):
                            c = step * B + b
                            nc.vector.tensor_scalar(row_hot[:, bass.ds(slot, 1), b, :], m.hot[0:CE, 0:P],
                                                    m.src_rowT[:, bass.ds(c, 1)], None, ALU.is_equal)
                            last = nc.vector.tensor_scalar(key_hot[:, bass.ds(slot, 1), b, :], m.hot[0:CE, :],
                                                           m.keyT[:, bass.ds(c, 1)], m.shift[0:CE, bass.ds(g, 1)],
                                                           ALU.subtract, ALU.is_equal)
                        last.then_inc(hots_ready, 1)

            @block.tensor
            def _(pe):
                pe.sem_inc(slots_free, SLOTS)
                pe.wait_ge(zeroed, 1)
                with pe.Fori(0, NG // 2) as pair:
                    for half in range(2):
                        g = pair * 2 + half
                        acc = m.ps[0:P, half, 0:GW]
                        lo = pe.value_load(m.ranges[0:1, 1, bass.ds(g, 1)], min_val=1, max_val=NB)
                        before = pe.value_load(m.ranges[0:1, 2, bass.ds(g, 1)], min_val=0, max_val=NB * NG)
                        pe.wait_ge(banks_free, g + 1)
                        nc.tensor.matmul(acc, zeros[:, 0:P], zeros[:], start=True, stop=False)
                        with pe.Fori(0, lo) as j:
                            pe.wait_ge(hots_ready, before + j + 1)
                            slot = (before + j) & (SLOTS - 1)
                            for b in range(B):
                                last = nc.tensor.matmul(acc, row_hot[:, bass.ds(slot, 1), b, :].rearrange("p o n -> p (o n)"),
                                                        key_hot[:, bass.ds(slot, 1), b, :].rearrange("p o n -> p (o n)"),
                                                        start=False, stop=False)
                            last.then_inc(slots_free, 1)
                        nc.tensor.matmul(acc, zeros[:, 0:P], zeros[:], start=False, stop=True).then_inc(group_counted, 1)

            @block.scalar
            def _(act):
                act.sem_inc(banks_free, 2)
                with act.Fori(0, NG // 2) as pair:
                    for half in range(2):
                        g = pair * 2 + half
                        act.wait_ge(group_counted, g + 1)
                        act.wait_ge(group_counted, 1)
                        nc.scalar.activation(m.adjT[:, :, bass.ds(g * DG, DG)],
                                             m.ps[0:P, half, 0:GW].rearrange("p (d s) -> p s d", s=T),
                                             ACT.Copy).then_inc(banks_free, 1)


def stage_gates_and_first_sum(nc, m, gate_W, gate_b):
    with ExitStack() as ctx:
        def sb(name, shape, dt=F32):
            return ctx.enter_context(nc.sbuf_tensor(name, shape, dt))

        def sem(name):
            return ctx.enter_context(nc.semaphore(name))

        gw = sb("gw", [128, K, EXPERTS])
        gb = sb("gb", [P, EXPERTS])
        lg = sb("lg", [P, T, EXPERTS])
        top = sb("top", [P, T])
        total = sb("total", [P, T])
        gates = sb("gates", [P, EXPERTS, T])
        rank = sb("rank", [P, EXPERTS, T])
        beats = sb("beats", [P, EXPERTS, T])
        deg_part = sb("deg_part", [P, N])
        inv_row = sb("inv_row", [128, N])
        inv_tmp = sb("inv_tmp", [128, N])
        inv_ctmp = sb("inv_ctmp", [P, T])

        gate_loaded = sem("gate_loaded")
        gate_summed = sem("gate_summed")
        gate_shifted = sem("gate_shifted")
        gate_exp = sem("gate_exp")
        deg_part_ready = sem("deg_part_ready")
        deg_summed = sem("deg_summed")
        sums_ready = sem("sums_ready")
        sums_copied = sem("sums_copied")

        RING = 3
        with nc.Block() as block:
            @block.sync
            def _(sp):
                sp.dma_start(gw[:], gate_W.rearrange("(k p) e -> p k e", p=128)).then_inc(gate_loaded, 16)
                sp.dma_start(gb[:], gate_b.partition_broadcast(P)).then_inc(gate_loaded, 16)

            @block.tensor
            def _(pe):
                pe.wait_ge(gate_loaded, 32)
                for t in range(T):
                    for k in range(K):
                        last = nc.tensor.matmul(m.ps[0:P, 7, t * EXPERTS:(t + 1) * EXPERTS], m.xnT[:, k, tile(t)], gw[:, k, :],
                                                start=(k == 0), stop=(k == K - 1))
                last.then_inc(gate_summed, 1)
                n = 0
                for f in range(K):
                    for c0, cn in CHUNKS:
                        if n == 3:
                            pe.wait_ge(deg_part_ready, 1)
                            for i, (d0, dn) in enumerate(CHUNKS):
                                nc.tensor.matmul(m.ps[:, i, 0:dn], m.ones[0:P, :], deg_part[:, d0:d0 + dn], start=True, stop=True)
                            for t in range(T):
                                last = nc.tensor.matmul(m.ps[0:P, 3, t:t + 1], deg_part[:, tile(t)], m.ones[0:P, 0:1],
                                                        start=True, stop=True)
                            last.then_inc(deg_summed, 1)
                        if n >= RING:
                            pe.wait_ge(sums_copied, n - RING + 1)
                        for s in range(T):
                            last = nc.tensor.matmul(m.ps[:, 4 + n % RING, 0:cn], m.xn[:, s, f * 128:(f + 1) * 128],
                                                    m.adjT[:, s, c0:c0 + cn], start=(s == 0), stop=(s == T - 1))
                        last.then_inc(sums_ready, 1)
                        n += 1

            @block.scalar
            def _(act):
                act.wait_ge(gate_shifted, 1)
                nc.scalar.activation(lg[:], lg[:], ACT.Exp).then_inc(gate_exp, 1)

            @block.vector
            def _(vec):
                nc.vector.tensor_reduce(deg_part[:], m.adjT[:, :, 0:N].rearrange("p s d -> p d s"), X, ALU.add)\
                    .then_inc(deg_part_ready, 1)
                vec.wait_ge(gate_loaded, 32)
                vec.wait_ge(gate_summed, 1)
                nc.vector.tensor_tensor(lg[:], m.ps[0:P, 7, 0:T * EXPERTS].rearrange("p (t e) -> p t e", e=EXPERTS),
                                        gb[:].unsqueeze(1).to_broadcast([P, T, EXPERTS]), ALU.add)
                vec.drain()
                nc.vector.tensor_reduce(top[:], lg[:], X, ALU.max)
                vec.drain()
                nc.vector.tensor_tensor(lg[:], lg[:], top[:].unsqueeze(2).to_broadcast([P, T, EXPERTS]), ALU.subtract)\
                    .then_inc(gate_shifted, 1)
                vec.wait_ge(deg_summed, 1)
                for i, (d0, dn) in enumerate(CHUNKS):
                    nc.vector.tensor_scalar(inv_tmp[:, d0:d0 + dn], m.ps[:, i, 0:dn], 1.0, None, ALU.max)
                nc.vector.tensor_scalar(inv_ctmp[:], m.ps[0:P, 3, 0:T], 1.0, None, ALU.max)
                vec.drain()
                nc.vector.reciprocal(inv_tmp[:], inv_tmp[:])
                nc.vector.reciprocal(inv_ctmp[:], inv_ctmp[:])
                vec.drain()
                for i, (d0, dn) in enumerate(CHUNKS):
                    nc.vector.scalar_tensor_tensor(inv_row[:, d0:d0 + dn], m.ps[:, i, 0:dn], 0.0, inv_tmp[:, d0:d0 + dn],
                                                   ALU.is_gt, ALU.mult)
                nc.vector.scalar_tensor_tensor(m.inv_col[:], m.ps[0:P, 3, 0:T], 0.0, inv_ctmp[:], ALU.is_gt, ALU.mult)
                vec.drain()
                n = 0
                for f in range(K):
                    for c0, cn in CHUNKS:
                        vec.wait_ge(sums_ready, n + 1)
                        nc.vector.tensor_tensor(m.meanT[:, f, c0:c0 + cn], m.ps[:, 4 + n % RING, 0:cn], inv_row[:, c0:c0 + cn],
                                                ALU.mult).then_inc(sums_copied, 1)
                        n += 1
                vec.wait_ge(gate_exp, 1)
                nc.vector.tensor_reduce(total[:], lg[:], X, ALU.add)
                vec.drain()
                nc.vector.reciprocal(total[:], total[:])
                vec.drain()
                for e in range(EXPERTS):
                    nc.vector.tensor_tensor(gates[:, e, :], lg[:, :, e], total[:], ALU.mult)
                vec.drain()
                for e in range(EXPERTS):
                    rest = [f for f in range(EXPERTS) if f != e]
                    for f in rest:
                        nc.vector.tensor_tensor(beats[:, f, :], gates[:, f, :], gates[:, e, :], ALU.is_ge if f < e else ALU.is_gt)
                    vec.drain()
                    nc.vector.tensor_tensor(rank[:, e, :], beats[:, rest[0], :], beats[:, rest[1], :], ALU.add)
                    vec.drain()
                    nc.vector.tensor_tensor(rank[:, e, :], rank[:, e, :], beats[:, rest[2], :], ALU.add)
                    vec.drain()
                    nc.vector.scalar_tensor_tensor(m.gate[:, e, :], rank[:, e, :], 1.5, gates[:, e, :], ALU.is_lt, ALU.mult)


def stage_experts(nc, m, Wl, bl, Wr, gnn_dram):
    with ExitStack() as ctx:
        def sb(name, shape, dt=F32):
            return ctx.enter_context(nc.sbuf_tensor(name, shape, dt))

        def sem(name):
            return ctx.enter_context(nc.semaphore(name))

        wl1 = sb("wl1", [128, K, D])
        wr1 = sb("wr1", [128, K, D])
        wl2 = sb("wl2", [128, K, D])
        wr2 = sb("wr2", [128, K, D])
        bl1 = sb("bl1", [128, K])
        bl2 = sb("bl2", [P, D])
        hT = sb("hT", [128, K, N])
        g = sb("g", [P, T, D])
        acc = sb("acc", [P, T, D])
        o = sb("o", [P, 2, D])

        first_loaded = sem("first_loaded")
        second_loaded = sem("second_loaded")
        h_summed = sem("h_summed")
        h_free = sem("h_free")
        g_summed = sem("g_summed")
        g_free = sem("g_free")
        out_summed = sem("out_summed")
        out_free = sem("out_free")
        out_gated = sem("out_gated")
        out_added = sem("out_added")
        acc_cleared = sem("acc_cleared")
        gnn_stored = sem("gnn_stored")
        NH = K * len(CHUNKS)

        with nc.Block() as block:
            @block.sync
            def _(sp):
                for e in range(EXPERTS):
                    def matrix(W, layer):
                        return W[e, layer].rearrange("(k p) n -> p k n", p=128)

                    if e:
                        sp.wait_ge(h_summed, e * NH)
                        sp.wait_ge(h_free, e * NH + 4)
                    sp.dma_start(wl1[:], matrix(Wl, 0)).then_inc(first_loaded, 16)
                    sp.dma_start(wr1[:], matrix(Wr, 0)).then_inc(first_loaded, 16)
                    sp.dma_start(bl1[:], bl[e, 0].rearrange("(k p) -> p k", p=128)).then_inc(first_loaded, 16)
                    if e:
                        sp.wait_ge(out_summed, e * T)
                        sp.wait_ge(out_added, e * T)
                    sp.dma_start(wl2[:], matrix(Wl, 1)).then_inc(second_loaded, 16)
                    sp.dma_start(wr2[:], matrix(Wr, 1)).then_inc(second_loaded, 16)
                    sp.dma_start(bl2[:], bl[e, 1].partition_broadcast(P)).then_inc(second_loaded, 16)
                sp.wait_ge(out_added, EXPERTS * T)
                sp.dma_start(gnn_dram.rearrange("(t p) d -> p t d", p=P), acc[:]).then_inc(gnn_stored, 16)
                sp.wait_ge(gnn_stored, 16)

            @block.tensor
            def _(pe):
                with pe.Fori(0, EXPERTS) as e:
                    pe.wait_ge(first_loaded, e * 48 + 48)
                    pe.wait_ge(out_free, e * T + 2)
                    n = 0
                    for f in range(K):
                        for c0, cn in CHUNKS:
                            pe.wait_ge(h_free, e * NH + (n + 1))
                            for k in range(K):
                                nc.tensor.matmul(m.ps[:, n % 4, 0:cn], wl1[:, k, f * 128:(f + 1) * 128], m.meanT[:, k, c0:c0 + cn],
                                                 start=(k == 0), stop=False)
                            for k in range(K):
                                last = nc.tensor.matmul(m.ps[:, n % 4, 0:cn], wr1[:, k, f * 128:(f + 1) * 128],
                                                        m.xnT[:, k, c0:c0 + cn], start=False, stop=(k == K - 1))
                            last.then_inc(h_summed, 1)
                            n += 1
                    pe.wait_ge(second_loaded, e * 48 + 48)
                    pe.wait_ge(h_free, e * NH + (NH + 4))
                    for t in range(T):
                        pe.wait_ge(g_free, e * T + (t + 1))
                        for k in range(K):
                            last = nc.tensor.matmul(m.ps[0:P, 4 + t % 2, :], hT[:, k, tile(t)], wl2[:, k, :],
                                                    start=(k == 0), stop=(k == K - 1))
                        last.then_inc(g_summed, 1)
                    for t in range(T):
                        pe.wait_ge(out_free, e * T + (t + 1))
                        for k in range(K):
                            nc.tensor.matmul(m.ps[0:P, t % 2, :], hT[:, k, tile(t)], wr2[:, k, :],
                                             start=(k == 0), stop=(k == K - 1))
                        if t == 0:
                            pe.wait_ge(g_free, e * T + (T + 2))
                        for s in range(T):
                            last = nc.tensor.matmul(m.ps[0:P, 6 + t % 2, :], m.adjT[:, s, tile(t)], g[:, s, :],
                                                    start=(s == 0), stop=(s == T - 1))
                        last.then_inc(out_summed, 1)

            @block.scalar
            def _(act):
                act.sem_inc(h_free, 4)
                act.sem_inc(g_free, 2)
                with act.Fori(0, EXPERTS) as e:
                    act.wait_ge(first_loaded, e * 48 + 48)
                    n = 0
                    for f in range(K):
                        for c0, cn in CHUNKS:
                            act.wait_ge(h_summed, e * NH + (n + 1))
                            nc.scalar.activation(hT[:, f, c0:c0 + cn], m.ps[:, n % 4, 0:cn], ACT.Relu, bias=bl1[:, f:f + 1])\
                                .then_inc(h_free, 1)
                            n += 1
                    for t in range(T):
                        act.wait_ge(g_summed, e * T + (t + 1))
                        nc.scalar.activation(g[:, t, :], m.ps[0:P, 4 + t % 2, :], ACT.Copy).then_inc(g_free, 1)

            @block.vector
            def _(vec):
                vec.sem_inc(out_free, 2)
                with vec.Fori(0, EXPERTS) as e:
                    vec.wait_ge(second_loaded, e * 48 + 48)
                    vec.wait_ge(acc_cleared, 1)
                    for t in range(T):
                        vec.wait_ge(out_summed, e * T + (t + 1))
                        if t >= 2:
                            vec.wait_ge(out_added, e * T + (t - 1))
                        else:
                            vec.wait_ge(out_added, e * T)
                        nc.vector.scalar_tensor_tensor(o[:, t % 2, :], m.ps[0:P, 6 + t % 2, :], m.inv_col[:, t:t + 1], bl2[:],
                                                       ALU.mult, ALU.add)
                        vec.drain()
                        nc.vector.tensor_tensor(o[:, t % 2, :], o[:, t % 2, :], m.ps[0:P, t % 2, :], ALU.add).then_inc(out_free, 1)
                        vec.drain()
                        nc.vector.tensor_scalar(o[:, t % 2, :], o[:, t % 2, :], 0.0, m.gate[:, bass.ds(e, 1), t],
                                                ALU.max, ALU.mult).then_inc(out_gated, 1)

            @block.gpsimd
            def _(pool):
                pool.memset(acc[:], 0.0).then_inc(acc_cleared, 1)
                pool.wait_ge(acc_cleared, 1)
                with pool.Fori(0, EXPERTS) as e:
                    for t in range(T):
                        pool.wait_ge(out_gated, e * T + (t + 1))
                        pool.tensor_tensor(acc[:, t, :], acc[:, t, :], o[:, t % 2, :], ALU.add).then_inc(out_added, 1)


def emit_split_product(nc, out, lhs, rhs, first, last):
    lhs_high, lhs_low = lhs
    rhs_high, rhs_low = rhs
    nc.tensor.matmul(out, lhs_high, rhs_high, start=first, stop=False)
    nc.tensor.matmul(out, lhs_high, rhs_low, start=False, stop=False)
    return nc.tensor.matmul(out, lhs_low, rhs_high, start=False, stop=last)


def stage_mixer(nc, m, w, xn_dram):
    WQ, WK, WV, WO = range(4)
    QUARTERS = FF // D
    BLOCKS = 4 + 2 * QUARTERS
    W1 = [4 + 2 * b for b in range(QUARTERS)]
    W2 = [5 + 2 * b for b in range(QUARTERS)]
    SLOT = [0, 1, 0, 1] + [0, 1, 2, 3] * (QUARTERS // 2)
    VW = DH + 1
    CW = 6 * K + FT
    xm = m.xm
    with ExitStack() as ctx:
        def sb(name, shape, dt=F32):
            return ctx.enter_context(nc.sbuf_tensor(name, shape, dt))

        def sem(name):
            return ctx.enter_context(nc.semaphore(name))

        qp = sb("qp", [P, 2, 2 * M])
        qpT = sb("qpT", [128, 2, 4 * P])
        tmp = qpT
        context = sb("context", [128, 2, 4, VW])
        squares = sb("squares", [128, N])
        proj = sb("proj", [128, 2, 2, DH])
        projT = sb("projT", [128, 2 * M])
        halves = sb("halves", [128, 2])
        col_rows = sb("col_rows", [DEPTH * CW, 128])
        all_cols = sb("all_cols", [128, DEPTH * CW])
        layer_cols = sb("layer_cols", [128, CW])
        cols = layer_cols[:, 0:4 * K].rearrange("p (a k) -> p a k", a=4)
        qk_bias = layer_cols[:, 4 * K:6 * K].rearrange("p (a k) -> p a k", a=2)
        b1 = layer_cols[:, 6 * K:CW]
        rows = sb("rows", [P, 3, D])
        st = sb("st1", [P, T, 6])
        mv = sb("mv1", [P, T, 2])
        std = sb("std1", [P, T])
        rstd = sb("rstd1", [P, T])
        k_max = sb("k_max", [P, 2, T])
        k_top = sb("k_top", [P, 2])
        k_all = sb("k_all", [P, 2])
        k_diag = sb("k_diag", [P, 2, T, 2])
        q_diag = sb("q_diag", [P, 2, T, 2])
        k_shift = sb("k_shift", [P, T, 2])
        q_max = sb("q_max", [P, 2, 2])
        q_shift = sb("q_shift", [P, 2, 2])
        rden = sb("rden", [P, 2, 2])

        SLOT_BYTES, KP_BYTES, V_BYTES = 2 * K * D * 4, T * D * 4, T * HEADS * VW * 4
        at_y = -(-nc.sbuf_base // 64) * 64
        at_qk = at_y + 2 * K * N * 4
        at_kp = at_qk + 2 * K * N * 4
        at_v = at_kp + 2 * KP_BYTES
        at_o = at_v + V_BYTES
        assert 2 * SLOT_BYTES + K * D * 4 <= 2 * KP_BYTES and 2 * SLOT_BYTES <= V_BYTES + KP_BYTES and SLOT_BYTES <= V_BYTES

        def place(name, shape, dt, offset):
            return nc.alloc_sbuf_tensor_at(name, shape, dt, offset=offset)

        yT = place("yT", [128, 2, K, N], F32R, at_y)
        qT = place("qT", [128, K, N], F32, at_qk)
        kT = place("kT", [128, K, N], F32, at_qk + K * N * 4)
        hT = place("hidT", [128, 2, K, N], F32R, at_qk)
        kp = place("kp", [P, 2, T, D], F32, at_kp)
        landing = place("landing", [128, K, D], F32, at_kp + 2 * SLOT_BYTES)
        v = place("v", [P, T, HEADS, VW], F32, at_v)
        o = place("o", [P, T, D], F32, at_o)
        z = o
        slots = [place(f"wslot{n}", [128, 2, K, D], F32R, (at_kp if n < 2 else at_v) + n % 2 * SLOT_BYTES) for n in range(4)]

        x_loaded, cols_loaded, rows_loaded, proj_loaded = sem("xm_loaded"), sem("cols_loaded"), sem("rows_loaded"), sem("proj_loaded")
        w_landed, w_high, w_split = sem("w_landed"), sem("w_high"), sem("w_split")
        cols_turned, layer_cols_ready = sem("cols_turned"), sem("layer_cols_ready")
        proj_turned, projT_ready, halves_ready = sem("proj_turned"), sem("projT_ready"), sem("halves_ready")
        var_ready, std_made, z_ready, y_turned = sem("var_ready1"), sem("std_made1"), sem("z_ready"), sem("y_turned")
        exact_ready, high_ready, low_ready = sem("exact_ready"), sem("high_ready"), sem("low_ready")
        qk_summed, qk_copied, v_summed, v_ready = sem("qk_summed"), sem("qk_copied"), sem("v_summed"), sem("v_ready")
        squares_ready, diag_summed, diag_copied = sem("squares_ready"), sem("diag_summed"), sem("diag_copied")
        ks_summed, ks_copied, k_top_ready, k_all_ready = sem("ks_summed"), sem("ks_copied"), sem("k_top_ready"), sem("k_all_ready")
        k_shift_ready, k_exp, kp_ready = sem("k_shift_ready"), sem("k_exp"), sem("kp_ready")
        context_summed, context_ready = sem("context_summed"), sem("context_ready")
        qs_summed, q_shift_ready, q_exp = sem("qs_summed"), sem("q_shift_ready"), sem("q_exp")
        qp_turned, qpT_ready, o_summed, o_ready = sem("qp_turned"), sem("qpT_ready"), sem("o_summed"), sem("o_ready")
        bo_added, b2_added, o_turned, oT_high, oT_low = sem("bo_added"), sem("b2_added"), sem("o_turned"), sem("oT_high"), sem("oT_low")
        wo_summed, wo_added, h_summed, ff_summed, ff_added = (
            sem("wo_summed"), sem("wo_added"), sem("ffh_summed"), sem("ff_summed"), sem("ff_added"))

        TURNS = [(k, g) for k in range(K) for g in GROUPS3]
        G = len(TURNS)
        NQ = K * len(CHUNKS)
        NT = PAIRS * T
        HQ = K * len(CHUNKS)
        SPLITS = 2 * G + QUARTERS * HQ
        FT_ALL = QUARTERS * T
        DIAGS = 2 * PAIRS
        ATTENTION = range(-2, PAIRS)

        def keys_of(b):
            return b + 2 if b + 2 < PAIRS else None

        def features_of(b):
            return b + 1 if 0 <= b + 1 < PAIRS else None

        def diag_order():
            order = []
            for b in ATTENTION:
                order += [("k", keys_of(b))] * (keys_of(b) is not None) + [("q", features_of(b))] * (features_of(b) is not None)
            return order

        DIAG_AT = {key: n for n, key in enumerate(diag_order())}
        K_DIAG_STEP, Q_DIAG_STEP = 3, 8

        with nc.Block() as block:
            @block.sync
            def _(sp):
                sp.dma_start(xm[:], xn_dram.rearrange("(t p) d -> p t d", p=P)).then_inc(x_loaded, 16)
                for n, a in enumerate(("ln1_g", "ln1_b", "ln2_g", "ln2_b", "bq", "bk")):
                    sp.dma_start(col_rows[n * DEPTH * K:(n + 1) * DEPTH * K, :], w[a].rearrange("l (k p) -> (l k) p", p=128)).then_inc(cols_loaded, 16)
                sp.dma_start(col_rows[6 * DEPTH * K:, :], w["b1"].rearrange("l (f p) -> (l f) p", p=128)).then_inc(cols_loaded, 16)
                for i in range(DEPTH):
                    blocks = [w[a][i] for a in ("Wq", "Wk", "Wv", "Wo")]
                    for b in range(QUARTERS):
                        blocks += [w["W1"][i, :, b * D:(b + 1) * D], w["W2"][i, b * D:(b + 1) * D, :]]
                    for n, a in enumerate(blocks):
                        if i * BLOCKS + n:
                            sp.wait_ge(w_split, i * BLOCKS + n)
                        if n == WO:
                            sp.wait_ge(context_summed, i * PAIRS + PAIRS)
                        sp.dma_start(landing[:], a.rearrange("(k p) n -> p k n", p=128)).then_inc(w_landed, 16)
                        if n == WQ:
                            pv = w["proj"][i].rearrange("(a p) d -> p a d", p=128)
                            if i:
                                sp.wait_ge(proj_turned, i)
                            for c in range(2):
                                sp.dma_start(proj[:, :, c, :], pv).then_inc(proj_loaded, 16)
                            if i:
                                sp.wait_ge(b2_added, i * T)
                            for j, r in enumerate(("bv", "bo", "b2")):
                                sp.dma_start(rows[:, j], w[r][i].partition_broadcast(P)).then_inc(rows_loaded, 16)

            @block.tensor
            def _(pe):
                def parts(n):
                    return slots[SLOT[n]]

                def turn_rows(i, half):
                    for n, (k, (t0, t1)) in enumerate(TURNS):
                        pe.wait_ge(z_ready, i * 2 * T + (half * T + t1))
                        if n >= 4:
                            pe.wait_ge(exact_ready, i * SPLITS + (half * G + n - 3))
                        for t in range(t0, t1):
                            last = nc.tensor.transpose(m.ps[:, n % 4, (t - t0) * P:(t - t0 + 1) * P], z[:, t, k * 128:(k + 1) * 128],
                                                       m.ident[0:P, 0:P])
                        last.then_inc(y_turned, 1)
                    pe.wait_ge(low_ready, i * SPLITS + (half * G + G))

                def diagonal(i, kind, j):
                    d = DIAG_AT[kind, j]
                    pe.wait_ge(squares_ready, i * DIAGS + (d + 1))
                    if d:
                        pe.wait_ge(diag_copied, i * DIAGS + d)
                    for t in range(T):
                        last = nc.tensor.matmul(m.ps[0:P, 5, 2 * t:2 * t + 2], squares[:, tile(t)], halves[:], start=True, stop=True)
                    last.then_inc(diag_summed, 1)

                def attention_block(i, b):
                    jk, jf = keys_of(b), features_of(b)
                    for s in range(T + 2):
                        if b >= 0 and s < T:
                            if b * T + s >= 2:
                                pe.wait_ge(q_exp, i * NT + (b * T + s - 1))
                            nc.tensor.matmul(m.ps[0:P, 6 + s % 2, :], qT[:, b, tile(s)], projT[:], start=True, stop=True).then_inc(qs_summed, 1)
                        if jk is not None and s < T:
                            if jk * T + s >= 2:
                                pe.wait_ge(ks_copied, i * NT + (jk * T + s - 1))
                            nc.tensor.matmul(m.ps[0:P, 2 + s % 2, :], kT[:, jk, tile(s)], projT[:], start=True, stop=True).then_inc(ks_summed, 1)
                        if s == K_DIAG_STEP and jk is not None:
                            if jf:
                                pe.wait_ge(context_ready, i * PAIRS + jf)
                            diagonal(i, "k", jk)
                        if s == Q_DIAG_STEP and jf is not None:
                            if jf:
                                pe.wait_ge(context_ready, i * PAIRS + jf)
                            diagonal(i, "q", jf)
                        t = s - 1
                        if b >= 0 and 0 <= t < T:
                            pe.wait_ge(q_exp, i * NT + (b * T + t + 1))
                            if b * T + t >= 2:
                                pe.wait_ge(qpT_ready, i * NT + (b * T + t - 1))
                            for c in range(4):
                                last = nc.tensor.transpose(m.ps[:, t % 2, c * P:(c + 1) * P], qp[:, t % 2, c * 128:(c + 1) * 128],
                                                           m.ident[0:P, 0:P])
                            last.then_inc(qp_turned, 1)
                        t = s - 2
                        if b >= 0 and 0 <= t < T:
                            if t == 0:
                                pe.wait_ge(context_ready, i * PAIRS + (b + 1))
                            pe.wait_ge(qpT_ready, i * NT + (b * T + t + 1))
                            if b * T + t:
                                pe.wait_ge(o_ready, i * NT + (b * T + t))
                            for h in range(2):
                                for a in range(2):
                                    last = nc.tensor.matmul(m.ps[0:P, 4, h * VW:(h + 1) * VW],
                                                            qpT[:, t % 2, (2 * h + a) * P:(2 * h + a + 1) * P], context[:, b % 2, 2 * h + a, :],
                                                            start=(a == 0), stop=(a == 1))
                            last.then_inc(o_summed, 1)
                    if jf is not None:
                        pe.wait_ge(kp_ready, i * NT + (jf * T + T))
                        pe.wait_ge(diag_copied, i * DIAGS + (DIAG_AT["q", jf] + 1))
                        for c in range(4):
                            for t in range(T):
                                last = nc.tensor.matmul(m.ps[:, 5, c * VW:(c + 1) * VW], kp[:, jf % 2, t, c * 128:(c + 1) * 128],
                                                        v[:, t, 2 * jf + c // 2, :], start=(t == 0), stop=(t == T - 1))
                        last.then_inc(context_summed, 1)

                pe.wait_ge(cols_loaded, 112)
                nc.tensor.transpose(m.ps[:, 6, 0:DEPTH * CW], col_rows[:], m.ident[0:DEPTH * CW, 0:DEPTH * CW]).then_inc(cols_turned, 1)
                with pe.Fori(0, DEPTH) as i:
                    pe.wait_ge(proj_loaded, i * 32 + 32)
                    for a in range(2):
                        last = nc.tensor.transpose(m.ps[:, 4, a * 128:(a + 1) * 128], proj[:, a].rearrange("p c d -> p (c d)"), m.ident[:])
                    last.then_inc(proj_turned, 1)
                    turn_rows(i, 0)
                    pe.wait_ge(projT_ready, i + 1)
                    pe.wait_ge(layer_cols_ready, i + 1)
                    n = 0
                    for block_n in (WQ, WK):
                        pe.wait_ge(w_split, i * BLOCKS + (block_n + 1))
                        wt = parts(block_n)
                        for f in range(K):
                            for c0, cn in CHUNKS:
                                if n >= 4:
                                    pe.wait_ge(qk_copied, i * 2 * NQ + (n - 3))
                                for k in range(K):
                                    last = emit_split_product(nc, m.ps[:, 4 + n % 4, 0:cn],
                                                              [wt[:, h, k, f * 128:(f + 1) * 128] for h in range(2)],
                                                              [yT[:, h, k, c0:c0 + cn] for h in range(2)], k == 0, k == K - 1)
                                last.then_inc(qk_summed, 1)
                                n += 1
                    pe.wait_ge(w_split, i * BLOCKS + (WV + 1))
                    wt = parts(WV)
                    for t in range(T):
                        if t >= 2:
                            pe.wait_ge(v_ready, i * T + (t - 1))
                        for k in range(K):
                            last = emit_split_product(nc, m.ps[0:P, t % 2, :], [yT[:, h, k, tile(t)] for h in range(2)],
                                                      [wt[:, h, k, :] for h in range(2)], k == 0, k == K - 1)
                        last.then_inc(v_summed, 1)
                    pe.wait_ge(qk_copied, i * 2 * NQ + 2 * NQ)
                    pe.wait_ge(v_ready, i * T + T)
                    pe.wait_ge(halves_ready, 1)
                    for b in ATTENTION:
                        attention_block(i, b)
                    pe.wait_ge(o_ready, i * NT + NT)
                    for n, (k, (t0, t1)) in enumerate(TURNS):
                        if n >= 4:
                            pe.wait_ge(oT_low, i * G + (n - 3))
                        for t in range(t0, t1):
                            last = nc.tensor.transpose(m.ps[:, n % 4, (t - t0) * P:(t - t0 + 1) * P], o[:, t, k * 128:(k + 1) * 128],
                                                       m.ident[0:P, 0:P])
                        last.then_inc(o_turned, 1)
                    pe.wait_ge(w_split, i * BLOCKS + (WO + 1))
                    pe.wait_ge(oT_low, i * G + G)
                    wt = parts(WO)
                    for t in range(T):
                        if t >= 2:
                            pe.wait_ge(wo_added, i * T + (t - 1))
                        for k in range(K):
                            last = emit_split_product(nc, m.ps[0:P, 6 + t % 2, :], [yT[:, h, k, tile(t)] for h in range(2)],
                                                      [wt[:, h, k, :] for h in range(2)], k == 0, k == K - 1)
                        last.then_inc(wo_summed, 1)
                    turn_rows(i, 1)
                    for b in range(QUARTERS):
                        pe.wait_ge(w_split, i * BLOCKS + (W1[b] + 1))
                        wt = parts(W1[b])
                        for c, (c0, cn) in enumerate(CHUNKS):
                            for f in range(K):
                                n = b * HQ + c * K + f
                                if n >= 4:
                                    pe.wait_ge(exact_ready, i * SPLITS + (2 * G + n - 3))
                                for k in range(K):
                                    last = emit_split_product(nc, m.ps[:, 4 + n % 4, 0:cn],
                                                              [wt[:, h, k, f * 128:(f + 1) * 128] for h in range(2)],
                                                              [yT[:, h, k, c0:c0 + cn] for h in range(2)], k == 0, k == K - 1)
                                last.then_inc(h_summed, 1)
                        pe.wait_ge(w_split, i * BLOCKS + (W2[b] + 1))
                        wt = parts(W2[b])
                        for c, (t0, t1) in enumerate(GROUPS3):
                            pe.wait_ge(low_ready, i * SPLITS + (2 * G + b * HQ + (c + 1) * K))
                            for t in range(t0, t1):
                                if b * T + t >= 2:
                                    pe.wait_ge(ff_added, i * FT_ALL + (b * T + t - 1))
                                for k in range(K):
                                    last = emit_split_product(nc, m.ps[0:P, t % 2, :], [hT[:, h, k, tile(t)] for h in range(2)],
                                                              [wt[:, h, k, :] for h in range(2)], k == 0, k == K - 1)
                                last.then_inc(ff_summed, 1)

            @block.scalar
            def _(act):
                def weight_high(i, n):
                    act.wait_ge(w_landed, i * 16 * BLOCKS + 16 * (n + 1))
                    nc.scalar.activation(slots[SLOT[n]][:, 0], landing[:], ACT.Copy).then_inc(w_high, 1)

                def norm_rows(i, half):
                    for g, (t0, t1) in enumerate(GROUPS3):
                        act.wait_ge(var_ready, i * 6 + (half * 3 + g + 1))
                        nc.scalar.activation(std[:, t0:t1], mv[:, t0:t1, 1], ACT.Sqrt, bias=m.eps_col[0:P, :]).then_inc(std_made, 1)
                    for n, (k, (t0, t1)) in enumerate(TURNS):
                        act.wait_ge(y_turned, i * 2 * G + (half * G + n + 1))
                        if n >= 2:
                            act.wait_ge(low_ready, i * SPLITS + (half * G + n - 1))
                        nc.scalar.activation(tmp[:, n % 2, 0:(t1 - t0) * P], m.ps[:, n % 4, 0:(t1 - t0) * P], ACT.Identity,
                                             bias=cols[:, 2 * half + 1, k:k + 1], scale=cols[:, 2 * half, k:k + 1])\
                            .then_inc(exact_ready, 1)

                with act.Fori(0, DEPTH) as i:
                    act.wait_ge(ff_summed, i * FT_ALL)
                    weight_high(i, WQ)
                    act.wait_ge(layer_cols_ready, i + 1)
                    norm_rows(i, 0)
                    weight_high(i, WK)
                    n = 0
                    for a, dstT in enumerate((qT, kT)):
                        for f in range(K):
                            for c0, cn in CHUNKS:
                                act.wait_ge(qk_summed, i * 2 * NQ + (n + 1))
                                nc.scalar.activation(dstT[:, f, c0:c0 + cn], m.ps[:, 4 + n % 4, 0:cn], ACT.Identity,
                                                     bias=qk_bias[:, a, f:f + 1], scale=NORM).then_inc(qk_copied, 1)
                                n += 1
                        if a == 0:
                            weight_high(i, WV)
                    for b in ATTENTION:
                        jk, jf = keys_of(b), features_of(b)
                        for s in range(T + 2):
                            if b >= 0 and s < T:
                                act.wait_ge(q_shift_ready, i * NT + (b * T + s + 1))
                                if b * T + s >= 2:
                                    act.wait_ge(qp_turned, i * NT + (b * T + s - 1))
                                for h in range(2):
                                    last = nc.scalar.activation(qp[:, s % 2, h * M:(h + 1) * M], m.ps[0:P, 6 + s % 2, h * M:(h + 1) * M], ACT.Exp,
                                                                bias=q_shift[:, s % 2, h:h + 1])
                                last.then_inc(q_exp, 1)
                            if jk is not None and s < T:
                                act.wait_ge(ks_summed, i * NT + (jk * T + s + 1))
                                nc.scalar.activation(kp[:, jk % 2, s, :], m.ps[0:P, 2 + s % 2, :], ACT.Copy).then_inc(ks_copied, 1)
                            t = s - 2
                            if jf is not None and 0 <= t < T:
                                if t == 0:
                                    act.wait_ge(k_shift_ready, i * PAIRS + (jf + 1))
                                for h in range(2):
                                    scores = kp[:, jf % 2, t, h * M:(h + 1) * M]
                                    last = nc.scalar.activation(scores, scores, ACT.Exp, bias=k_shift[:, t, h:h + 1])
                                last.then_inc(k_exp, 1)
                            if b == PAIRS - 1 and s == 4:
                                weight_high(i, WO)
                            if b == PAIRS - 1 and s == 9:
                                weight_high(i, W1[0])
                        if jf is not None:
                            act.wait_ge(context_summed, i * PAIRS + (jf + 1))
                            nc.scalar.activation(context[:, jf % 2], m.ps[:, 5, 0:4 * VW].rearrange("p (c n) -> p c n", c=4), ACT.Copy)\
                                .then_inc(context_ready, 1)
                    for n, (k, (t0, t1)) in enumerate(TURNS):
                        act.wait_ge(o_turned, i * G + (n + 1))
                        nc.scalar.activation(yT[:, 0, k, t0 * P:t1 * P], m.ps[:, n % 4, 0:(t1 - t0) * P], ACT.Copy).then_inc(oT_high, 1)
                    norm_rows(i, 1)
                    for b in range(QUARTERS):
                        for c, (c0, cn) in enumerate(CHUNKS):
                            for f in range(K):
                                n = b * HQ + c * K + f
                                act.wait_ge(h_summed, i * QUARTERS * HQ + (n + 1))
                                if n >= 2:
                                    act.wait_ge(low_ready, i * SPLITS + (2 * G + n - 1))
                                nc.scalar.activation(tmp[:, n % 2, 0:cn], m.ps[:, 4 + n % 4, 0:cn], ACT.Gelu, bias=b1[:, b * K + f:b * K + f + 1])\
                                    .then_inc(exact_ready, 1)
                            if c == 0:
                                if b >= 2:
                                    act.wait_ge(ff_summed, i * FT_ALL + (b - 1) * T)
                                weight_high(i, W2[b])
                            if c == 2 and b + 1 < QUARTERS:
                                weight_high(i, W1[b + 1])

            @block.vector
            def _(vec):
                nc.vector.memset(projT[:], 0.0)
                nc.vector.memset(halves[:], 0.0)
                vec.drain()
                for h in range(2):
                    last = nc.vector.memset(halves[h * DH:(h + 1) * DH, h:h + 1], 0.5)
                last.then_inc(halves_ready, 1)
                vec.wait_ge(cols_turned, 1)
                nc.vector.tensor_copy(all_cols[:], m.ps[:, 6, 0:DEPTH * CW])
                vec.drain()
                vec.wait_ge(x_loaded, 16)

                def norm_group(i, half, g):
                    t0, t1 = GROUPS3[g]
                    for t in range(t0, t1):
                        nc.vector.bn_stats(st[:, t, :], xm[:, t, :])
                    vec.drain()
                    for t in range(t0, t1):
                        last = nc.vector.bn_aggr(mv[:, t, :], st[:, t, :])
                    last.then_inc(var_ready, 1)
                    vec.wait_ge(std_made, i * 6 + (half * 3 + g + 1))
                    nc.vector.reciprocal(rstd[:, t0:t1], std[:, t0:t1])
                    vec.drain()
                    for t in range(t0, t1):
                        nc.vector.tensor_scalar(z[:, t, :], xm[:, t, :], mv[:, t, 0:1], rstd[:, t:t + 1],
                                                ALU.subtract, ALU.mult).then_inc(z_ready, 1)

                def split_high(i, n, dst, width):
                    vec.wait_ge(exact_ready, i * SPLITS + (n + 1))
                    nc.vector.tensor_copy(dst, tmp[:, n % 2, 0:width]).then_inc(high_ready, 1)

                with vec.Fori(0, DEPTH) as i:
                    nc.vector.tensor_copy(layer_cols[:, 0:6 * K].rearrange("p (a k) -> p a k", a=6),
                                          all_cols[:, 0:6 * DEPTH * K].rearrange("p (a l k) -> p l a k", a=6, l=DEPTH)[:, bass.ds(i, 1)]
                                          .rearrange("p o a k -> p (o a) k"))
                    nc.vector.tensor_copy(b1, all_cols[:, 6 * DEPTH * K:].rearrange("p (l f) -> p l f", l=DEPTH)[:, bass.ds(i, 1)]
                                          .rearrange("p o f -> p (o f)"))
                    vec.drain()
                    nc.vector.tensor_scalar(qk_bias, qk_bias, NORM, None, ALU.mult).then_inc(layer_cols_ready, 1)
                    for g in range(len(GROUPS3)):
                        norm_group(i, 0, g)
                    for n, (k, (t0, t1)) in enumerate(TURNS):
                        split_high(i, n, yT[:, 0, k, t0 * P:t1 * P], (t1 - t0) * P)
                    vec.wait_ge(proj_turned, i + 1)
                    for h in range(2):
                        last = nc.vector.tensor_copy(projT[h * DH:(h + 1) * DH, h * M:(h + 1) * M], m.ps[h * DH:(h + 1) * DH, 4, 0:M])
                    last.then_inc(projT_ready, 1)
                    vec.wait_ge(rows_loaded, i * 48 + 48)
                    for t in range(T):
                        vec.wait_ge(v_summed, i * T + (t + 1))
                        if t == 0:
                            nc.vector.memset(v[:, :, :, DH:VW], 1.0)
                        nc.vector.tensor_tensor(v[:, t, :, 0:DH], m.ps[0:P, t % 2, :].rearrange("p (h c) -> p h c", h=HEADS),
                                                rows[:, 0, :].rearrange("p (h c) -> p h c", h=HEADS), ALU.add).then_inc(v_ready, 1)

                    def copy_diagonal(kind, j, dst):
                        vec.wait_ge(diag_summed, i * DIAGS + (DIAG_AT[kind, j] + 1))
                        nc.vector.tensor_copy(dst[:, j % 2], m.ps[0:P, 5, 0:2 * T].rearrange("p (t h) -> p t h", h=2)).then_inc(diag_copied, 1)

                    for b in ATTENTION:
                        jk, jf = keys_of(b), features_of(b)
                        for s in range(T + 2):
                            if b >= 0 and s < T:
                                vec.wait_ge(qs_summed, i * NT + (b * T + s + 1))
                                nc.vector.tensor_reduce(q_max[:, s % 2, :], m.ps[0:P, 6 + s % 2, :].rearrange("p (h c) -> p h c", h=2), X, ALU.max)
                                vec.drain()
                                if b * T + s >= 2:
                                    vec.wait_ge(q_exp, i * NT + (b * T + s - 1))
                                nc.vector.scalar_tensor_tensor(q_shift[:, s % 2, :], q_max[:, s % 2, :], -1.0, q_diag[:, b % 2, s, :],
                                                               ALU.mult, ALU.subtract).then_inc(q_shift_ready, 1)
                            if s == 1 and jf is not None:
                                vec.wait_ge(k_all_ready, i * PAIRS + (jf + 1))
                                for h in range(2):
                                    last = nc.vector.tensor_scalar(k_shift[:, :, h], k_diag[:, jf % 2, :, h], k_all[:, h:h + 1], -1.0,
                                                                   ALU.add, ALU.mult)
                                last.then_inc(k_shift_ready, 1)
                            if jk is not None and s < T:
                                vec.wait_ge(ks_copied, i * NT + (jk * T + s + 1))
                                nc.vector.tensor_reduce(k_max[:, :, s], kp[:, jk % 2, s, :].rearrange("p (h c) -> p h c", h=2), X, ALU.max)
                            if s == K_DIAG_STEP + 1 and jk is not None:
                                copy_diagonal("k", jk, k_diag)
                            if s == Q_DIAG_STEP + 1 and jf is not None:
                                copy_diagonal("q", jf, q_diag)
                            t = s - 1
                            if b >= 0 and 0 <= t < T:
                                vec.wait_ge(qp_turned, i * NT + (b * T + t + 1))
                                if b * T + t >= 2:
                                    vec.wait_ge(o_summed, i * NT + (b * T + t - 1))
                                nc.vector.tensor_scalar(qpT[:, t % 2, :], m.ps[:, t % 2, 0:4 * P], FEATURE_EPS, None, ALU.add).then_inc(qpT_ready, 1)
                            t = s - 2
                            if b >= 0 and 0 <= t < T:
                                vec.wait_ge(o_summed, i * NT + (b * T + t + 1))
                                ov = m.ps[0:P, 4, 0:2 * VW].rearrange("p (h c) -> p h c", h=2)
                                nc.vector.reciprocal(rden[:, t % 2, :], ov[:, :, DH])
                                vec.drain()
                                for h in range(2):
                                    last = nc.vector.tensor_scalar(o[:, t, (2 * b + h) * DH:(2 * b + h + 1) * DH], ov[:, h, 0:DH],
                                                                   rden[:, t % 2, h:h + 1], None, ALU.mult)
                                last.then_inc(o_ready, 1)
                        if jk is not None:
                            vec.drain()
                            nc.vector.tensor_reduce(k_top[:], k_max[:], X, ALU.max).then_inc(k_top_ready, 1)
                            vec.drain()
                    for n, (k, (t0, t1)) in enumerate(TURNS):
                        vec.wait_ge(oT_high, i * G + (n + 1))
                        nc.vector.tensor_tensor(yT[:, 1, k, t0 * P:t1 * P], m.ps[:, n % 4, 0:(t1 - t0) * P],
                                                yT[:, 0, k, t0 * P:t1 * P].bitcast(F32), ALU.subtract).then_inc(oT_low, 1)
                    vec.wait_ge(bo_added, i * T + T)
                    vec.wait_ge(o_turned, i * G + G)
                    for g, (t0, t1) in enumerate(GROUPS3):
                        for t in range(t0, t1):
                            vec.wait_ge(wo_summed, i * T + (t + 1))
                            nc.vector.tensor_tensor(xm[:, t, :], xm[:, t, :], m.ps[0:P, 6 + t % 2, :], ALU.add).then_inc(wo_added, 1)
                        vec.drain()
                        norm_group(i, 1, g)
                    for n, (k, (t0, t1)) in enumerate(TURNS):
                        split_high(i, G + n, yT[:, 0, k, t0 * P:t1 * P], (t1 - t0) * P)
                    vec.wait_ge(b2_added, i * T + T)
                    for b in range(QUARTERS):
                        for c, (c0, cn) in enumerate(CHUNKS):
                            for f in range(K):
                                split_high(i, 2 * G + b * HQ + c * K + f, hT[:, 0, f, c0:c0 + cn], cn)
                        for t in range(T):
                            vec.wait_ge(ff_summed, i * FT_ALL + (b * T + t + 1))
                            nc.vector.tensor_tensor(xm[:, t, :], xm[:, t, :], m.ps[0:P, t % 2, :], ALU.add).then_inc(ff_added, 1)
                        vec.drain()

            @block.gpsimd
            def _(pool):
                def weight_low(i, n):
                    pool.wait_ge(w_high, i * BLOCKS + n + 1)
                    pool.tensor_tensor(slots[SLOT[n]][:, 1], landing[:], slots[SLOT[n]][:, 0].bitcast(F32), ALU.subtract).then_inc(w_split, 1)

                def split_low(i, n, dst, high, width):
                    pool.wait_ge(high_ready, i * SPLITS + n + 1)
                    pool.tensor_tensor(dst, tmp[:, n % 2, 0:width], high.bitcast(F32), ALU.subtract).then_inc(low_ready, 1)

                def square(i, kind, j):
                    d = i * DIAGS + DIAG_AT[kind, j]
                    if d:
                        pool.wait_ge(diag_summed, d)
                    srcT = kT if kind == "k" else qT
                    pool.tensor_tensor(squares[:], srcT[:, j, :], srcT[:, j, :], ALU.mult).then_inc(squares_ready, 1)

                pool.wait_ge(x_loaded, 16)
                for i in range(DEPTH):
                    weight_low(i, WQ)
                    for n, (k, (t0, t1)) in enumerate(TURNS):
                        split_low(i, n, yT[:, 1, k, t0 * P:t1 * P], yT[:, 0, k, t0 * P:t1 * P], (t1 - t0) * P)
                    weight_low(i, WK)
                    pool.wait_ge(rows_loaded, i * 48 + 48)
                    for t in range(T):
                        pool.tensor_tensor(xm[:, t, :], xm[:, t, :], rows[:, 1, :], ALU.add).then_inc(bo_added, 1)
                        if t == 4:
                            weight_low(i, WV)
                    pool.wait_ge(qk_copied, i * 2 * NQ + 2 * NQ)
                    for b in ATTENTION:
                        jk, jf = keys_of(b), features_of(b)
                        if jk is not None:
                            square(i, "k", jk)
                        if jf is not None:
                            for t in range(T):
                                pool.wait_ge(k_exp, i * NT + jf * T + t + 1)
                                pool.tensor_scalar(kp[:, jf % 2, t, :], kp[:, jf % 2, t, :], FEATURE_EPS, 1.0, ALU.add, ALU.mult).then_inc(kp_ready, 1)
                                if t == 3:
                                    square(i, "q", jf)
                        if jk is not None:
                            pool.wait_ge(k_top_ready, i * PAIRS + jk + 1)
                            pool.partition_all_reduce(k_all[:], k_top[:], P, MAX_REDUCE).then_inc(k_all_ready, 1)
                    weight_low(i, WO)
                    weight_low(i, W1[0])
                    for n, (k, (t0, t1)) in enumerate(TURNS):
                        split_low(i, G + n, yT[:, 1, k, t0 * P:t1 * P], yT[:, 0, k, t0 * P:t1 * P], (t1 - t0) * P)
                    for t in range(T):
                        pool.tensor_tensor(xm[:, t, :], xm[:, t, :], rows[:, 2, :], ALU.add).then_inc(b2_added, 1)
                    for b in range(QUARTERS):
                        for c, (c0, cn) in enumerate(CHUNKS):
                            for f in range(K):
                                split_low(i, 2 * G + b * HQ + c * K + f, hT[:, 1, f, c0:c0 + cn], hT[:, 0, f, c0:c0 + cn], cn)
                            if c == 0:
                                weight_low(i, W2[b])
                            if c == 2 and b + 1 < QUARTERS:
                                weight_low(i, W1[b + 1])


def stage_shift_unit(nc, m, x, gnn_dram, out):
    MARK, SHL, SHR, LO, DIGITS, OUT = 0, 39, 40, 64, 16, 128
    with ExitStack() as ctx:
        def sb(name, shape, dt=F32):
            return ctx.enter_context(nc.sbuf_tensor(name, shape, dt))

        def sem(name):
            return ctx.enter_context(nc.semaphore(name))

        y = sb("y", [P, T, D])
        gnn = sb("gnn", [P, T, D])
        ln = sb("ln", [P, T, D])
        st = sb("st2", [P, T, 6])
        mv = sb("mv2", [P, T, 2])
        std = sb("std2", [P, T])
        rstd = sb("rstd2", [P, T])
        count_i = sb("count_i", [P, 2, DIGITS], I32)
        down = sb("down", [P, DIGITS])
        up = sb("up", [P, DIGITS])
        first = sb("first", [P, T, 3, DIGITS])
        best = sb("best", [P, T, 3])
        found = sb("found", [P, T, 3])
        digit = sb("digit", [P, T, 3])
        flag = sb("flag", [P, 5, T])
        value = sb("value", [P, T])
        value_i = sb("value_i", [P, 2, T], I32)
        shift_i = sb("amount_i", [P, T], I32)
        shifted_i = sb("shifted_i", [P, 2, T], I32)
        shifted = sb("shifted", [P, 2, T])
        result = sb("result", [P, T])
        result_i = sb("result_i", [P, T], I32)
        nibble_i = sb("nibble_i", [P, 2, T], I32)
        nibble = sb("nibble", [P, 2, T])
        amp = sb("amp", [P, T])
        hot = sb("hot2", [P, T, 2, DIGITS])

        x_loaded, gnn_loaded = sem("y_loaded"), sem("gnn_loaded")
        counts_made, var_ready, std_made = sem("counts_made"), sem("var_ready2"), sem("std_made2")
        out_ready, out_stored = sem("out_ready"), sem("out_stored")
        xv = x.rearrange("(t p) d -> p t d", p=P)
        ov = out.rearrange("(t p) d -> p t d", p=P)

        with nc.Block() as block:
            @block.sync
            def _(sp):
                sp.dma_start(y[:], xv).then_inc(x_loaded, 16)
                sp.dma_start(gnn[:], gnn_dram.rearrange("(t p) d -> p t d", p=P)).then_inc(gnn_loaded, 16)
                for h in range(2):
                    a, b = h * T // 2, (h + 1) * T // 2
                    sp.wait_ge(out_ready, b)
                    sp.dma_start(ov[:, a:b, :], ln[:, a:b, :]).then_inc(out_stored, 16)
                sp.wait_ge(out_stored, 32)

            @block.gpsimd
            def _(pool):
                pool.iota(count_i[:, 0], pattern=[[-1, DIGITS]], base=DIGITS, channel_multiplier=0).then_inc(counts_made, 1)
                pool.iota(count_i[:, 1], pattern=[[1, DIGITS]], base=0, channel_multiplier=0).then_inc(counts_made, 1)

            @block.scalar
            def _(act):
                act.wait_ge(var_ready, 1)
                nc.scalar.activation(std[:], mv[:, :, 1], ACT.Sqrt, bias=m.eps_col[0:P, :]).then_inc(std_made, 1)

            @block.vector
            def _(vec):
                v = nc.vector
                vec.wait_ge(counts_made, 2)
                v.tensor_copy(down[:], count_i[:, 0])
                v.tensor_copy(up[:], count_i[:, 1])
                vec.wait_ge(x_loaded, 16)
                vec.wait_ge(gnn_loaded, 16)
                for t in range(T):
                    v.tensor_tensor(y[:, t, :], y[:, t, :], gnn[:, t, :], ALU.add)
                vec.drain()
                for t in range(T):
                    v.tensor_tensor(y[:, t, :], y[:, t, :], m.xm[:, t, :], ALU.add)
                vec.drain()
                emit_norm_stats(nc, vec, std_made, var_ready, 1, y, st, mv, rstd, std)
                for t in range(T):
                    v.tensor_scalar(ln[:, t, :], y[:, t, :], mv[:, t, 0:1], rstd[:, t:t + 1], ALU.subtract, ALU.mult)
                vec.drain()
                v.scalar_tensor_tensor(first[:].rearrange("p t a d -> p t (a d)"), ln[:, :, LO:LO + 3 * DIGITS], 0.5,
                                       ln[:, :, LO:LO + 3 * DIGITS], ALU.is_gt, ALU.bypass)
                for n, c in enumerate((MARK, SHL, SHR)):
                    v.tensor_scalar(flag[:, n, :], ln[:, :, c], 0.5, None, ALU.is_gt)
                vec.drain()
                for a in range(3):
                    v.tensor_tensor(first[:, :, a, :], first[:, :, a, :], down[:].unsqueeze(1).to_broadcast([P, T, DIGITS]), ALU.mult)
                vec.drain()
                v.tensor_reduce(best[:], first[:], X, ALU.max)
                vec.drain()
                v.tensor_scalar(found[:], best[:], 0.0, None, ALU.is_gt)
                v.tensor_scalar(digit[:], best[:], -1.0, float(DIGITS), ALU.mult, ALU.add)
                vec.drain()
                v.tensor_tensor(digit[:], digit[:], found[:], ALU.mult)
                vec.drain()
                v.scalar_tensor_tensor(value[:], digit[:, :, 1], float(DIGITS), digit[:, :, 0], ALU.mult, ALU.add)
                v.tensor_copy(shift_i[:], digit[:, :, 2])
                vec.drain()
                v.tensor_copy(value_i[:, 0], value[:])
                vec.drain()
                v.tensor_tensor(shifted_i[:, 0], value_i[:, 0], shift_i[:], ALU.logical_shift_left)
                v.tensor_tensor(shifted_i[:, 1], value_i[:, 0], shift_i[:], ALU.logical_shift_right)
                v.tensor_tensor(flag[:, 3, :], flag[:, 0, :], flag[:, 1, :], ALU.mult)
                v.tensor_tensor(flag[:, 4, :], flag[:, 0, :], flag[:, 2, :], ALU.mult)
                vec.drain()
                v.tensor_scalar(shifted_i[:, 0], shifted_i[:, 0], 255, None, ALU.bitwise_and)
                v.tensor_tensor(flag[:, 4, :], flag[:, 4, :], flag[:, 3, :], ALU.is_gt)
                vec.drain()
                v.tensor_copy(shifted[:], shifted_i[:])
                v.tensor_tensor(amp[:], flag[:, 3, :], flag[:, 4, :], ALU.add)
                vec.drain()
                v.tensor_tensor(shifted[:], shifted[:], flag[:, 3:5, :], ALU.mult)
                v.tensor_scalar(amp[:], amp[:], 2.0, None, ALU.mult)
                vec.drain()
                v.tensor_tensor(result[:], shifted[:, 0], shifted[:, 1], ALU.add)
                vec.drain()
                v.tensor_copy(result_i[:], result[:])
                vec.drain()
                v.tensor_scalar(nibble_i[:, 0], result_i[:], 15, None, ALU.bitwise_and)
                v.tensor_scalar(nibble_i[:, 1], result_i[:], 4, None, ALU.logical_shift_right)
                vec.drain()
                v.tensor_copy(nibble[:], nibble_i[:])
                vec.drain()
                for a in range(2):
                    v.tensor_tensor(hot[:, :, a, :], up[:].unsqueeze(1).to_broadcast([P, T, DIGITS]),
                                    nibble[:, a, :].unsqueeze(2).to_broadcast([P, T, DIGITS]), ALU.is_equal)
                vec.drain()
                for a in range(2):
                    v.tensor_tensor(hot[:, :, a, :], hot[:, :, a, :], amp[:].unsqueeze(2).to_broadcast([P, T, DIGITS]), ALU.mult)
                vec.drain()
                v.tensor_tensor(ln[:, :, OUT:OUT + 2 * DIGITS], ln[:, :, OUT:OUT + 2 * DIGITS],
                                hot[:].rearrange("p t a d -> p t (a d)"), ALU.add)
                vec.drain()
                for t in range(T):
                    v.tensor_tensor(ln[:, t, :], ln[:, t, :], y[:, t, :], ALU.add).then_inc(out_ready, 1)


def gps_block(nc, a, out):
    xn_dram = nc.dram_tensor("xn_dram", [N, D], F32, kind="Internal").ap()
    gnn_dram = nc.dram_tensor("gnn_dram", [N, D], F32, kind="Internal").ap()
    with ExitStack() as ctx:
        ctx.enter_context(nc.allow_non_contiguous_dma(reason="bias vectors, one feature per partition"))

        def sb(name, shape, dt=F32):
            return ctx.enter_context(nc.sbuf_tensor(name, shape, dt))

        m = OnChip()
        m.ps = ctx.enter_context(nc.psum_tensor("ps", [128, 8, 512], F32))
        m.ident = sb("ident", [128, 128])
        m.ones = sb("ones", [128, 128])
        m.eps_col = sb("eps_col", [128, 1])
        with ExitStack() as graph:
            def gsb(name, shape, dt=F32):
                return graph.enter_context(nc.sbuf_tensor(name, shape, dt))

            m.adjT = gsb("adjT", [P, T, NPAD])
            m.xnT = gsb("xnT", [128, K, N])
            m.meanT = gsb("meanT", [128, K, N])
            m.inv_col = gsb("inv_col", [P, T])
            m.gate = gsb("gate", [P, EXPERTS, T])
            with ExitStack() as counting:
                def csb(name, shape, dt=F32):
                    return counting.enter_context(nc.sbuf_tensor(name, shape, dt))

                m.xn = csb("xn", [P, T, D])
                m.src_rowT = csb("src_rowT", [CE, NC])
                m.keyT = csb("keyT", [CE, NC])
                m.shift = csb("shift", [P, NG])
                m.hot = csb("hot", [P, GW], F16)
                m.ranges = csb("ranges", [1, 3, NG], I32)
                stage_normalise_and_index(nc, m, a["x"], a["src"], a["dst"], xn_dram)
                stage_count_edges(nc, m)
                stage_gates_and_first_sum(nc, m, a["L0_gnn_gate_W"], a["L0_gnn_gate_b"])
            stage_experts(nc, m, a["L0_gnn_Wl"], a["L0_gnn_bl"], a["L0_gnn_Wr"], gnn_dram)
        m.xm = sb("xm", [P, T, D])
        nc.disable_value_cache = True
        stage_mixer(nc, m, {k[len("L0_mix_"):]: v for k, v in a.items() if k.startswith("L0_mix_")}, xn_dram)
        stage_shift_unit(nc, m, a["x"], gnn_dram, out)


_INS = ["x", "src", "dst", "L0_gnn_gate_W", "L0_gnn_gate_b", "L0_gnn_Wl", "L0_gnn_bl", "L0_gnn_Wr", "L0_mix_ln1_g", "L0_mix_ln1_b",
        "L0_mix_ln2_g", "L0_mix_ln2_b", "L0_mix_Wq", "L0_mix_bq", "L0_mix_Wk", "L0_mix_bk", "L0_mix_Wv", "L0_mix_bv",
        "L0_mix_Wo", "L0_mix_bo", "L0_mix_proj", "L0_mix_W1", "L0_mix_b1", "L0_mix_W2", "L0_mix_b2"]


def kernel(**inputs):
    import concourse.bacc as bacc
    from concourse.bass_utils import run_bass_kernel_spmd

    nc = bacc.Bacc("TRN2", target_bir_lowering=False, num_devices=1)
    arrays, args = {}, {}
    for name in _INS:
        arr = np.ascontiguousarray(inputs[name])
        arrays["in_" + name] = arr
        args[name] = nc.dram_tensor("in_" + name, arr.shape, mybir.dt.from_np(arr.dtype), kind="ExternalInput").ap()
    out = nc.dram_tensor("out", (N, D), F32, kind="ExternalOutput").ap()
    gps_block(nc, args, out)
    r = run_bass_kernel_spmd(nc, [arrays], core_ids=[0])
    return r.results[0]["out"]
```

```python
from contextlib import ExitStack

import numpy as np

import concourse.bass as bass
from concourse import mybir

F32 = mybir.dt.float32
F32R = mybir.dt.float32r
F16 = mybir.dt.float16
BF16 = mybir.dt.bfloat16
I32 = mybir.dt.int32
ACT = mybir.ActivationFunctionType
ALU = mybir.AluOpType
X = mybir.AxisListType.X
MAX_REDUCE = bass.bass_isa.ReduceOp.max

N, D, E = 1250, 512, 40000
T = 10
P = N // T
K = D // 128
CHUNKS = ((0, 500), (500, 500), (1000, 250))
GROUPS3 = ((0, 4), (4, 8), (8, 10))

CE = 125
NC = E // CE
CQ, CR = 4, NC // 4
B = 5
NB = NC // B
DG = 50
NG = N // DG
GW = DG * T
SLOTS = 4
BANKS = 5
R = 2 * B
LO_BITS, STEPS_BITS = 6, 7
assert NB <= 1 << LO_BITS and NB < 1 << STEPS_BITS and NB * NG << (LO_BITS + STEPS_BITS) < 1 << 24 and NG % BANKS == 0

EXPERTS = 4
DEPTH, HEADS, DH, M = 2, 8, 64, 256
PAIRS = HEADS // 2
FF = 2048
FT = FF // 128
NORM = float(DH) ** -0.25
FEATURE_EPS = 1e-4
LN_EPS = 1e-5
XN, MEAN = 0, 1
EXACT_COUNTS = 1 << 12
FC, FCN = 5, 250
FCT = FCN // P


class OnChip:
    pass


def tile(t):
    return slice(t * P, (t + 1) * P)


def emit_norm_stats(nc, vec, act_done, std_ready, seen, src, st, mv, rstd, std):
    for t in range(T):
        last = nc.vector.bn_stats(st[:, t, :], src[:, t, :])
    vec.drain()
    for t in range(T):
        last = nc.vector.bn_aggr(mv[:, t, :], st[:, t, :])
    last.then_inc(std_ready, 1)
    vec.wait_ge(act_done, seen)
    nc.vector.reciprocal(rstd[:], std[:])
    vec.drain()


def stage_normalise_and_index(nc, m, x, src, dst, xn_dram):
    with ExitStack() as ctx:
        def sb(name, shape, dt=F32):
            return ctx.enter_context(nc.sbuf_tensor(name, shape, dt))

        def sem(name):
            return ctx.enter_context(nc.semaphore(name))

        x_in = nc.alloc_sbuf_tensor_at("x_in", [P, T, D], F32, offset=m.at_parts)
        st = sb("st0", [P, T, 6])
        mv = sb("mv0", [P, T, 2])
        std = sb("std0", [P, T])
        rstd = sb("rstd0", [P, T])
        edge_i = sb("edge_i", [CR, 2, CQ, CE], I32)
        edge_f = sb("edge_f", [CR, 2, CQ, CE])
        src_tile = sb("src_tile", [CR, CQ, CE])
        src_row = sb("src_row", [CR, CQ, CE])
        key = sb("key", [CR, CQ, CE])
        chunk_min = sb("chunk_min", [CR, CQ])
        chunk_max = sb("chunk_max", [CR, CQ])
        step_i = sb("step_i", [CR, CQ, CR // B], I32)
        step_f = sb("step_f", [CR, CQ, CR // B])
        step_of = sb("step_of", [CR, CQ])
        step_up = sb("step_up", [CR, CQ])
        step_down = sb("step_down", [CR, CQ])
        group_i = sb("group_i", [CR, NG], I32)
        group_lo = sb("group_lo", [CR, NG])
        group_hi = sb("group_hi", [CR, NG])
        cand = sb("cand", [CR, 2, CQ, NG])
        ends = sb("ends", [CR, 2, NG])
        ends_all = sb("ends_all", [CR, 2, NG])
        rng = sb("rng", [1, 6, NG])
        shift_i = sb("shift_i", [P, NG], I32)
        hot_i = sb("hot_i", [P, GW], I32)

        x_loaded = [sem("x_loaded0"), sem("x_loaded1")]
        edges_loaded = sem("edges_loaded")
        consts_made = sem("consts_made")
        ident_cleared = sem("ident_cleared")
        var_ready = sem("var_ready")
        std_made = sem("std_made")
        xn_ready = sem("xn_ready")
        xn_turned = sem("xn_turned")
        xnT_copied = sem("xnT_copied")
        keys_ready = sem("keys_ready")
        keys_turned = sem("keys_turned")
        ends_local = sem("ends_local")
        ends_global = sem("ends_global")
        xn_stored = sem("xn_stored")

        xv = x.rearrange("(t p) d -> p t d", p=P)
        H = T // 2
        with nc.Block() as block:
            @block.sync
            def _(sp):
                for h in range(2):
                    sp.dma_start(x_in[:, h * H:(h + 1) * H, :], xv[:, h * H:(h + 1) * H, :]).then_inc(x_loaded[h], 16)
                for n, a in enumerate((src, dst)):
                    sp.dma_start(edge_i[:, n], a.rearrange("(q r e) -> r q e", q=CQ, e=CE)).then_inc(edges_loaded, 16)
                sp.wait_ge(xn_ready, T)
                sp.dma_start(xn_dram.rearrange("(t p) d -> p t d", p=P), m.xn[:]).then_inc(xn_stored, 16)
                sp.wait_ge(xn_stored, 16)

            @block.gpsimd
            def _(pool):
                pool.memset(m.ident[:], 0.0).then_inc(ident_cleared, 1)
                pool.wait_ge(ident_cleared, 1)
                pool.affine_select(out=m.ident[:], in_=m.ident[:], compare_op=ALU.not_equal, fill=1.0,
                                   base=0, pattern=[[-1, 128]], channel_multiplier=1).then_inc(consts_made, 1)
                pool.memset(m.ones[:], 1.0).then_inc(consts_made, 1)
                pool.memset(m.eps_col[:], LN_EPS).then_inc(consts_made, 1)
                pool.iota(step_i[:], pattern=[[0, CQ], [-B, CR // B]], base=-B, channel_multiplier=1).then_inc(consts_made, 1)
                pool.iota(group_i[:], pattern=[[DG, NG]], base=0, channel_multiplier=0).then_inc(consts_made, 1)
                pool.iota(shift_i[:], pattern=[[-GW, NG]], base=0, channel_multiplier=0).then_inc(consts_made, 1)
                pool.iota(hot_i[:], pattern=[[1, GW]], base=0, channel_multiplier=0).then_inc(consts_made, 1)
                pool.wait_ge(ends_local, 1)
                pool.partition_all_reduce(ends_all[:], ends[:], CR, MAX_REDUCE).then_inc(ends_global, 1)

            @block.scalar
            def _(act):
                act.wait_ge(consts_made, 7)
                act.wait_ge(var_ready, 1)
                nc.scalar.activation(std[:], mv[:, :, 1], ACT.Sqrt, bias=m.eps_col[0:P, :]).then_inc(std_made, 1)
                for t in range(T):
                    act.wait_ge(xn_turned, t + 1)
                    nc.scalar.activation(m.xnT[:, :, tile(t)],
                                         m.ps[:, t % 4, 0:D // 128 * P].rearrange("p (k n) -> p k n", k=K),
                                         ACT.Copy).then_inc(xnT_copied, 1)

            @block.vector
            def _(vec):
                vec.wait_ge(consts_made, 7)
                for h in range(2):
                    vec.wait_ge(x_loaded[h], 16)
                emit_norm_stats(nc, vec, std_made, var_ready, 1, x_in, st, mv, rstd, std)
                for t in range(T):
                    nc.vector.tensor_scalar(m.xn[:, t, :], x_in[:, t, :], mv[:, t, 0:1], rstd[:, t:t + 1],
                                            ALU.subtract, ALU.mult).then_inc(xn_ready, 1)

                vec.wait_ge(edges_loaded, 32)
                nc.vector.tensor_copy(edge_f[:], edge_i[:])
                vec.drain()
                nc.vector.tensor_scalar(src_tile[:], edge_f[:, 0], float(P), None, ALU.is_ge)
                for k in range(2, T):
                    vec.drain()
                    nc.vector.scalar_tensor_tensor(src_tile[:], edge_f[:, 0], float(k * P), src_tile[:], ALU.is_ge, ALU.add)
                vec.drain()
                nc.vector.scalar_tensor_tensor(src_row[:], src_tile[:], -float(P), edge_f[:, 0], ALU.mult, ALU.add)
                nc.vector.scalar_tensor_tensor(key[:], edge_f[:, 1], float(T), src_tile[:], ALU.mult, ALU.add)\
                    .then_inc(keys_ready, 1)

                nc.vector.tensor_reduce(chunk_min[:], edge_f[:, 1], X, ALU.min)
                nc.vector.tensor_reduce(chunk_max[:], edge_f[:, 1], X, ALU.max)
                nc.vector.tensor_copy(step_f[:], step_i[:])
                nc.vector.tensor_copy(group_lo[:], group_i[:])
                vec.drain()
                nc.vector.tensor_scalar(step_f[:], step_f[:], 0.0, None, ALU.is_ge)
                nc.vector.tensor_scalar(group_hi[:], group_lo[:], float(DG), None, ALU.add)
                vec.drain()
                nc.vector.tensor_reduce(step_of[:], step_f[:], X, ALU.add)
                vec.drain()
                for q in range(CQ):
                    nc.vector.tensor_scalar(step_up[:, q:q + 1], step_of[:, q:q + 1], float(q * CR // B + 1), None, ALU.add)
                vec.drain()
                nc.vector.tensor_scalar(step_down[:], step_up[:], -1.0, float(NB + 1), ALU.mult, ALU.add)
                vec.drain()
                for q in range(CQ):
                    nc.vector.tensor_scalar(cand[:, 0, q, :], group_lo[:], chunk_max[:, q:q + 1], step_down[:, q:q + 1],
                                            ALU.is_le, ALU.mult)
                    nc.vector.tensor_scalar(cand[:, 1, q, :], group_hi[:], chunk_min[:, q:q + 1], step_up[:, q:q + 1],
                                            ALU.is_gt, ALU.mult)
                vec.drain()
                for n in range(2):
                    nc.vector.tensor_reduce(ends[:, n, :], cand[:, n].rearrange("p q g -> p g q"), X, ALU.max)\
                        .then_inc(ends_local, 1) if n else \
                        nc.vector.tensor_reduce(ends[:, n, :], cand[:, n].rearrange("p q g -> p g q"), X, ALU.max)
                nc.vector.tensor_copy(m.shift[:], shift_i[:])
                nc.vector.tensor_copy(m.hot[:], hot_i[:])
                vec.wait_ge(ends_global, 1)
                nc.vector.tensor_scalar(rng[:, 0], ends_all[0:1, 0], -1.0, float(NB), ALU.mult, ALU.add)
                vec.drain()
                nc.vector.tensor_scalar(rng[:, 0], rng[:, 0], float(NB - 1), None, ALU.min)
                vec.drain()
                nc.vector.tensor_tensor(rng[:, 1], ends_all[0:1, 1], rng[:, 0], ALU.subtract)
                vec.drain()
                nc.vector.tensor_scalar(rng[:, 1], rng[:, 1], 1.0, None, ALU.max)
                vec.drain()
                at, width = 1, 1
                while width < NG:
                    to = 2 if at != 2 else 3
                    nc.vector.tensor_copy(rng[:, to, 0:width], rng[:, at, 0:width])
                    nc.vector.tensor_tensor(rng[:, to, width:NG], rng[:, at, width:NG], rng[:, at, 0:NG - width], ALU.add)
                    vec.drain()
                    at, width = to, 2 * width
                nc.vector.tensor_tensor(rng[:, 4], rng[:, at], rng[:, 1], ALU.subtract)
                vec.drain()
                nc.vector.scalar_tensor_tensor(rng[:, 5], rng[:, 4], float(1 << STEPS_BITS), rng[:, 1], ALU.mult, ALU.add)
                vec.drain()
                nc.vector.scalar_tensor_tensor(rng[:, 4], rng[:, 5], float(1 << LO_BITS), rng[:, 0], ALU.mult, ALU.add)
                vec.drain()
                nc.vector.tensor_copy(m.ranges[:], rng[:, 4])
                vec.wait_ge(keys_turned, 1)
                nc.vector.tensor_copy(m.src_rowT[:], m.ps[0:CE, 4, 0:NC])
                nc.vector.tensor_copy(m.keyT[:], m.ps[0:CE, 5, 0:NC])

            @block.tensor
            def _(pe):
                pe.wait_ge(consts_made, 7)
                for t in range(T):
                    pe.wait_ge(xn_ready, t + 1)
                    if t >= 4:
                        pe.wait_ge(xnT_copied, t - 3)
                    for k in range(K):
                        last = nc.tensor.transpose(m.ps[:, t % 4, k * P:(k + 1) * P], m.xn[:, t, k * 128:(k + 1) * 128],
                                                   m.ident[0:P, 0:P])
                    last.then_inc(xn_turned, 1)
                pe.wait_ge(keys_ready, 1)
                for n, a in enumerate((src_row, key)):
                    for q in range(CQ):
                        last = nc.tensor.transpose(m.ps[0:CE, 4 + n, q * CR:(q + 1) * CR], a[:, q, :], m.ident[0:CR, 0:CR])
                last.then_inc(keys_turned, 1)


def stage_count_edges(nc, m):
    LO, STEPS = (1 << LO_BITS) - 1, (1 << STEPS_BITS) - 1
    with ExitStack() as ctx:
        def sb(name, shape, dt):
            return ctx.enter_context(nc.sbuf_tensor(name, shape, dt))

        def sem(name):
            return ctx.enter_context(nc.semaphore(name))

        row_hot = nc.alloc_sbuf_tensor_at("row_hot", [CE, NC, P], BF16, offset=m.at_parts)
        off = sb("off", [CE, 2, R, P], BF16)
        off_squared = sb("off_squared", [CE, 2, R, P], BF16)
        key_hot = sb("key_hot", [CE, SLOTS, B, GW], BF16)
        group_key = sb("group_key", [CE, 2 * NC], F32)
        zeros = sb("zeros", [CE, GW], BF16)
        off_ready = sem("off_ready")
        off_free = sem("off_free")
        rows_ready = sem("rows_ready")
        hots_ready = sem("hots_ready")
        slots_free = sem("slots_free")
        group_counted = sem("group_counted")
        banks_free = sem("banks_free")
        zeroed = sem("zeroed")

        def decode(eng, g):
            entry = eng.value_load(m.ranges[0:1, bass.ds(g, 1)], min_val=0, max_val=(1 << 24) - 1)
            return entry & LO, (entry >> LO_BITS) & STEPS, entry >> (LO_BITS + STEPS_BITS)

        with nc.Block() as block:
            @block.gpsimd
            def _(pool):
                pool.sem_inc(off_free, 2)
                with pool.Fori(0, NC // R // 2) as pair:
                    for half in range(2):
                        r = pair * 2 + half
                        pool.wait_ge(off_free, r + 1)
                        pool.tensor_tensor(off[:, half], m.hot[0:CE, 0:P].unsqueeze(1).to_broadcast([CE, R, P]),
                                           m.src_rowT[:, bass.ds(r * R, R)].unsqueeze(2).to_broadcast([CE, R, P]),
                                           ALU.subtract).then_inc(off_ready, 1)

            @block.vector
            def _(vec):
                nc.vector.memset(zeros[:], 0.0).then_inc(zeroed, 1)
                with vec.Fori(0, NG) as g:
                    lo, steps, before = decode(vec, g)
                    keys_at = (g & 1) * NC
                    nc.vector.tensor_scalar(group_key[:, bass.ds(keys_at, NC)], m.keyT[:],
                                            m.shift[0:CE, bass.ds(g, 1)], None, ALU.add)
                    vec.drain()
                    with vec.Fori(0, steps) as j:
                        vec.wait_ge(slots_free, before + j + 1)
                        slot = (before + j) & (SLOTS - 1)
                        step = nc.s_assert_within(lo + j, 0, NB - 1, skip_runtime_bounds_check_because="lo + steps <= NB")
                        first = keys_at + step * B
                        for b in range(B):
                            last = nc.vector.tensor_scalar(key_hot[:, bass.ds(slot, 1), b, :], m.hot[0:CE, :],
                                                           group_key[:, bass.ds(first + b, 1)], None, ALU.is_equal)
                        last.then_inc(hots_ready, 1)

            @block.tensor
            def _(pe):
                pe.sem_inc(slots_free, SLOTS)
                pe.wait_ge(zeroed, 1)
                with pe.Fori(0, NG // BANKS) as turn:
                    for bank in range(BANKS):
                        g = turn * BANKS + bank
                        acc = m.ps[0:P, bank, 0:GW]
                        lo, steps, before = decode(pe, g)
                        pe.wait_ge(banks_free, g + 1)
                        nc.tensor.matmul(acc, zeros[:, 0:P], zeros[:], start=True, stop=False)
                        with pe.Fori(0, steps) as j:
                            step = nc.s_assert_within(lo + j, 0, NB - 1, skip_runtime_bounds_check_because="lo + steps <= NB")
                            pe.wait_ge(rows_ready, (step >> 1) + 1)
                            pe.wait_ge(hots_ready, before + j + 1)
                            slot = (before + j) & (SLOTS - 1)
                            for b in range(B):
                                last = nc.tensor.matmul(acc, row_hot[:, bass.ds(step * B + b, 1), :].rearrange("p o n -> p (o n)"),
                                                        key_hot[:, bass.ds(slot, 1), b, :].rearrange("p o n -> p (o n)"),
                                                        start=False, stop=False)
                            last.then_inc(slots_free, 1)
                        nc.tensor.matmul(acc, zeros[:, 0:P], zeros[:], start=False, stop=True).then_inc(group_counted, 1)

            @block.scalar
            def _(act):
                act.sem_inc(banks_free, BANKS)
                with act.Fori(0, NC // R // 2) as pair:
                    for half in range(2):
                        r = pair * 2 + half
                        act.wait_ge(off_ready, r + 1)
                        nc.scalar.activation(off_squared[:, half], off[:, half], ACT.Square).then_inc(off_free, 1)
                        act.drain()
                        nc.scalar.activation(row_hot[:, bass.ds(r * R, R), :], off_squared[:, half], ACT.Relu,
                                             bias=m.ones[0:CE, 0:1], scale=-1.0).then_inc(rows_ready, 1)
                with act.Fori(0, NG // BANKS) as turn:
                    for bank in range(BANKS):
                        g = turn * BANKS + bank
                        act.wait_ge(group_counted, g + 1)
                        act.wait_ge(group_counted, 1)
                        nc.scalar.activation(m.adjT[:, :, bass.ds(g * DG, DG)],
                                             m.ps[0:P, bank, 0:GW].rearrange("p (d s) -> p s d", s=T),
                                             ACT.Copy).then_inc(banks_free, 1)


def stage_gates_and_first_sum(nc, m, gate_W, gate_b, adj_dram):
    with ExitStack() as ctx:
        def sb(name, shape, dt=F32):
            return ctx.enter_context(nc.sbuf_tensor(name, shape, dt))

        def sem(name):
            return ctx.enter_context(nc.semaphore(name))

        gw = sb("gw", [128, K, EXPERTS])
        gb = sb("gb", [P, EXPERTS])
        lg = sb("lg", [P, T, EXPERTS])
        top = sb("top", [P, T])
        total = sb("total", [P, T])
        gates = sb("gates", [P, EXPERTS, T])
        rank = sb("rank", [P, EXPERTS, T])
        beats = sb("beats", [P, EXPERTS, T])
        deg_part = sb("deg_part", [P, N])
        inv_row = sb("inv_row", [128, N])
        inv_tmp = sb("inv_tmp", [128, N])
        inv_ctmp = sb("inv_ctmp", [P, T])
        mean = sb("mean", [128, 2, CHUNKS[0][1]])
        top_chunk = sb("top_chunk", [1, len(CHUNKS)])
        top_all = sb("top_all", [1, 1])

        gate_loaded = sem("gate_loaded")
        gate_summed = sem("gate_summed")
        gate_shifted = sem("gate_shifted")
        gate_exp = sem("gate_exp")
        deg_part_ready = sem("deg_part_ready")
        deg_summed = sem("deg_summed")
        sums_ready = sem("sums_ready")
        mean_ready = sem("mean_ready")
        mean_high = sem("mean_high")
        mean_low = sem("mean_low")
        xn_high = sem("xn_high")
        adj_stored = sem("adj_stored")

        SUMS = [(f, chunk) for f in range(K) for chunk in CHUNKS]
        RING = 3
        with nc.Block() as block:
            @block.sync
            def _(sp):
                sp.dma_start(gw[:], gate_W.rearrange("(k p) e -> p k e", p=128)).then_inc(gate_loaded, 16)
                sp.dma_start(gb[:], gate_b.partition_broadcast(P)).then_inc(gate_loaded, 16)
                sp.dma_start(adj_dram, m.adjT[:]).then_inc(adj_stored, 16)
                sp.wait_ge(adj_stored, 16)

            @block.tensor
            def _(pe):
                pe.wait_ge(gate_loaded, 32)
                for t in range(T):
                    for k in range(K):
                        last = nc.tensor.matmul(m.ps[0:P, 7, t * EXPERTS:(t + 1) * EXPERTS], m.xnT[:, k, tile(t)], gw[:, k, :],
                                                start=(k == 0), stop=(k == K - 1))
                last.then_inc(gate_summed, 1)
                n = 0
                for f in range(K):
                    for c0, cn in CHUNKS:
                        if n == 3:
                            pe.wait_ge(deg_part_ready, 1)
                            for i, (d0, dn) in enumerate(CHUNKS):
                                nc.tensor.matmul(m.ps[:, i, 0:dn], m.ones[0:P, :], deg_part[:, d0:d0 + dn], start=True, stop=True)
                            for t in range(T):
                                last = nc.tensor.matmul(m.ps[0:P, 3, t:t + 1], deg_part[:, tile(t)], m.ones[0:P, 0:1],
                                                        start=True, stop=True)
                            last.then_inc(deg_summed, 1)
                        if n >= RING:
                            pe.wait_ge(mean_ready, n - RING + 1)
                        for s in range(T):
                            last = nc.tensor.matmul(m.ps[:, 4 + n % RING, 0:cn], m.xn[:, s, f * 128:(f + 1) * 128],
                                                    m.adjT[:, s, c0:c0 + cn], start=(s == 0), stop=(s == T - 1))
                        last.then_inc(sums_ready, 1)
                        n += 1

            @block.scalar
            def _(act):
                for k in range(K):
                    nc.scalar.activation(m.parts[:, XN, 0, k, :], m.xnT[:, k, :], ACT.Copy).then_inc(xn_high, 1)
                act.wait_ge(gate_shifted, 1)
                nc.scalar.activation(lg[:], lg[:], ACT.Exp).then_inc(gate_exp, 1)
                for n, (f, (c0, cn)) in enumerate(SUMS):
                    act.wait_ge(mean_ready, n + 1)
                    nc.scalar.activation(m.parts[:, MEAN, 0, f, c0:c0 + cn], mean[:, n % 2, 0:cn], ACT.Copy).then_inc(mean_high, 1)

            @block.gpsimd
            def _(pool):
                for k in range(K):
                    pool.wait_ge(xn_high, k + 1)
                    pool.tensor_tensor(m.parts[:, XN, 1, k, :], m.xnT[:, k, :], m.parts[:, XN, 0, k, :].bitcast(F32), ALU.subtract)
                for n, (f, (c0, cn)) in enumerate(SUMS):
                    pool.wait_ge(mean_high, n + 1)
                    pool.tensor_tensor(m.parts[:, MEAN, 1, f, c0:c0 + cn], mean[:, n % 2, 0:cn],
                                       m.parts[:, MEAN, 0, f, c0:c0 + cn].bitcast(F32), ALU.subtract).then_inc(mean_low, 1)

            @block.vector
            def _(vec):
                nc.vector.tensor_reduce(deg_part[:], m.adjT[:, :, 0:N].rearrange("p s d -> p d s"), X, ALU.add)\
                    .then_inc(deg_part_ready, 1)
                vec.wait_ge(gate_loaded, 32)
                vec.wait_ge(gate_summed, 1)
                nc.vector.tensor_tensor(lg[:], m.ps[0:P, 7, 0:T * EXPERTS].rearrange("p (t e) -> p t e", e=EXPERTS),
                                        gb[:].unsqueeze(1).to_broadcast([P, T, EXPERTS]), ALU.add)
                vec.drain()
                nc.vector.tensor_reduce(top[:], lg[:], X, ALU.max)
                vec.drain()
                nc.vector.tensor_tensor(lg[:], lg[:], top[:].unsqueeze(2).to_broadcast([P, T, EXPERTS]), ALU.subtract)\
                    .then_inc(gate_shifted, 1)
                vec.wait_ge(deg_summed, 1)
                for i, (d0, dn) in enumerate(CHUNKS):
                    nc.vector.tensor_scalar(inv_tmp[:, d0:d0 + dn], m.ps[:, i, 0:dn], 1.0, None, ALU.max)
                nc.vector.tensor_scalar(inv_ctmp[:], m.ps[0:P, 3, 0:T], 1.0, None, ALU.max)
                vec.drain()
                nc.vector.reciprocal(inv_tmp[:], inv_tmp[:])
                nc.vector.reciprocal(inv_ctmp[:], inv_ctmp[:])
                vec.drain()
                for i, (d0, dn) in enumerate(CHUNKS):
                    nc.vector.scalar_tensor_tensor(inv_row[:, d0:d0 + dn], m.ps[:, i, 0:dn], 0.0, inv_tmp[:, d0:d0 + dn],
                                                   ALU.is_gt, ALU.mult)
                nc.vector.scalar_tensor_tensor(m.inv_col[:], m.ps[0:P, 3, 0:T], 0.0, inv_ctmp[:], ALU.is_gt, ALU.mult)
                vec.drain()
                for i, (d0, dn) in enumerate(CHUNKS):
                    nc.vector.tensor_reduce(top_chunk[:, i:i + 1], m.ps[0:1, i, 0:dn], X, ALU.max)
                vec.drain()
                nc.vector.tensor_reduce(top_all[:], top_chunk[:], X, ALU.max)
                vec.drain()
                nc.vector.tensor_copy(m.top_degree[:], top_all[:])
                for n, (f, (c0, cn)) in enumerate(SUMS):
                    vec.wait_ge(sums_ready, n + 1)
                    if n >= 2:
                        vec.wait_ge(mean_low, n - 1)
                    nc.vector.tensor_tensor(mean[:, n % 2, 0:cn], m.ps[:, 4 + n % RING, 0:cn], inv_row[:, c0:c0 + cn],
                                            ALU.mult).then_inc(mean_ready, 1)
                vec.wait_ge(gate_exp, 1)
                nc.vector.tensor_reduce(total[:], lg[:], X, ALU.add)
                vec.drain()
                nc.vector.reciprocal(total[:], total[:])
                vec.drain()
                for e in range(EXPERTS):
                    nc.vector.tensor_tensor(gates[:, e, :], lg[:, :, e], total[:], ALU.mult)
                vec.drain()
                for e in range(EXPERTS):
                    rest = [f for f in range(EXPERTS) if f != e]
                    for f in rest:
                        nc.vector.tensor_tensor(beats[:, f, :], gates[:, f, :], gates[:, e, :], ALU.is_ge if f < e else ALU.is_gt)
                    vec.drain()
                    nc.vector.tensor_tensor(rank[:, e, :], beats[:, rest[0], :], beats[:, rest[1], :], ALU.add)
                    vec.drain()
                    nc.vector.tensor_tensor(rank[:, e, :], rank[:, e, :], beats[:, rest[2], :], ALU.add)
                    vec.drain()
                    nc.vector.scalar_tensor_tensor(m.gate[:, e, :], rank[:, e, :], 1.5, gates[:, e, :], ALU.is_lt, ALU.mult)


def emit_split_product(nc, out, lhs, rhs, first, last):
    lhs_high, lhs_low = lhs
    rhs_high, rhs_low = rhs
    nc.tensor.matmul(out, lhs_high, rhs_high, start=first, stop=False)
    nc.tensor.matmul(out, lhs_high, rhs_low, start=False, stop=False)
    return nc.tensor.matmul(out, lhs_low, rhs_high, start=False, stop=last)


def stage_experts(nc, m, Wl, bl, Wr, adj_dram, g_dram, u_dram, gnn_dram):
    LAND = 2
    G_RING = U_RING = 4
    NC3 = len(CHUNKS)
    HN = K * NC3
    LAST = EXPERTS - 1
    ORDER = (("first", 0), ("first", 1), ("second", 0), ("first", 2), ("second", 1), ("second", 2))
    with ExitStack() as ctx:
        def sb(name, shape, dt=F32):
            return ctx.enter_context(nc.sbuf_tensor(name, shape, dt))

        def sem(name):
            return ctx.enter_context(nc.semaphore(name))

        tmp = sb("h_exact", [128, 2, CHUNKS[0][1]])
        staged = sb("staged", [P, 2, 2, D])
        bl1_rows = sb("bl1_rows", [EXPERTS * K, 128])
        bl1 = sb("bl1", [128, EXPERTS * K])
        bl2 = sb("bl2", [P, D])
        BLOCK_BYTES, G_BYTES = K * D * 4, T * D * 4
        at_h = -(-nc.sbuf_base // 64) * 64
        at_g = at_h + 2 * 2 * K * CHUNKS[0][1] * 4
        at_w1 = at_g + 4 * BLOCK_BYTES
        at_land = at_w1 + 4 * BLOCK_BYTES
        assert at_g + 4 * G_BYTES <= at_land + LAND * BLOCK_BYTES and 2 * G_BYTES >= 4 * BLOCK_BYTES

        def place(name, shape, dt, offset):
            return nc.alloc_sbuf_tensor_at(name, shape, dt, offset=offset)

        hT = place("hT", [128, 2, 2, K, CHUNKS[0][1]], F32R, at_h)
        w2 = place("w2", [128, 2, 2, K, D], F32R, at_g)
        w1 = place("w1", [128, 2, 2, K, D], F32R, at_w1)
        landing = place("w_landing", [128, LAND, K, D], F32, at_land)
        adj = place("adj", [P, T, N], F32R, m.at_parts)
        at_acc = m.at_parts + -(-T * N * 4 // 64) * 64
        acc = place("acc", [P, T, D], F32, at_acc)
        g_in = place("g_in", [P, G_RING, D], F32, at_acc + G_BYTES)
        assert at_acc + G_BYTES + G_RING * D * 4 <= m.at_parts + 4 * K * N * 4
        g = [place(f"g{n}", [P, 2, T, D], F32R, at_g + (1 - n) * 2 * G_BYTES) for n in range(2)]
        u_in = place("u_in", [P, U_RING, D], F32, at_h)
        o = place("o_gnn", [P, 2, D], F32, at_h + U_RING * D * 4)

        bl1_loaded, bl1_turned, bl1_ready, bl2_loaded, bl2_used = (
            sem("bl1_loaded"), sem("bl1_turned"), sem("bl1_ready"), sem("bl2_loaded"), sem("bl2_used"))
        landed = [sem("landed0"), sem("landed1")]
        w_high, w_split = sem("e_high"), sem("e_split")
        h_summed, h_exact, h_high, h_low = sem("h_summed"), sem("h_exact_ready"), sem("h_high"), sem("h_low")
        g_summed, g_staged, u_summed, u_staged = sem("g_summed"), sem("g_staged"), sem("u_summed"), sem("u_staged")
        g_stored = [sem("g_stored0"), sem("g_stored1")]
        u_stored = [sem("u_stored0"), sem("u_stored1")]
        adj_loaded = sem("adj_loaded")
        g_loaded = [sem(f"g_loaded{n}") for n in range(G_RING)]
        u_loaded = [sem(f"u_loaded{n}") for n in range(U_RING)]
        g_high, g_low, out_summed, out_read, out_added, gnn_stored = (
            sem("g_high"), sem("g_low"), sem("out_summed"), sem("out_read"), sem("out_added"), sem("gnn_stored"))
        TILES = [range(*c) for c in GROUPS3]

        with nc.Block() as block:
            @block.sync
            def _(sp):
                def load_block(n):
                    W, layer = (Wl, Wr)[n % 2], n // 2 % 2
                    if n >= LAND:
                        sp.wait_ge(w_split, n - LAND + 1)
                    sp.dma_start(landing[:, n % LAND], W[n // 4, layer].rearrange("(k p) n -> p k n", p=128)).then_inc(landed[n % LAND], 16)

                def store(e, c):
                    for t in TILES[c]:
                        sp.wait_ge(g_staged, e * T + t + 1 + 2)
                        sp.dma_start(g_dram[e, t], staged[:, t % 2, 0]).then_inc(g_stored[t % 2], 16)
                        sp.wait_ge(u_staged, e * T + t + 1 + 2)
                        sp.dma_start(u_dram[e, t], staged[:, t % 2, 1]).then_inc(u_stored[t % 2], 16)

                def load_g(e, t):
                    n = e * T + t
                    if n >= G_RING:
                        sp.wait_ge(g_low, n - G_RING + 1)
                    sp.dma_start(g_in[:, n % G_RING], g_dram[e, t]).then_inc(g_loaded[n % G_RING], 16)

                def load_u(e, t):
                    n = e * T + t
                    if n >= U_RING:
                        sp.wait_ge(out_added, n - U_RING + 1)
                    sp.dma_start(u_in[:, n % U_RING], u_dram[e, t]).then_inc(u_loaded[n % U_RING], 16)

                load_block(0)
                load_block(1)
                for e in range(EXPERTS):
                    sp.dma_start(bl1_rows[e * K:(e + 1) * K, :], bl[e, 0].rearrange("(k p) -> k p", p=128)).then_inc(bl1_loaded, 16)
                load_block(2)
                load_block(3)
                for e in range(EXPERTS):
                    if e:
                        sp.wait_ge(bl2_used, e)
                    sp.dma_start(bl2[:], bl[e, 1].partition_broadcast(P)).then_inc(bl2_loaded, 16)
                    if e < LAST:
                        load_block(4 * e + 4)
                        load_block(4 * e + 5)
                    store(e, 0)
                    if e == LAST:
                        sp.wait_ge(h_summed, EXPERTS * HN)
                        sp.dma_start(adj[:].bitcast(F32), adj_dram).then_inc(adj_loaded, 16)
                        for n in range(2):
                            sp.wait_ge(g_stored[n], 16 * (T // 2) + 16)
                        for t in range(G_RING):
                            load_g(0, t)
                    store(e, 1)
                    if e < LAST:
                        load_block(4 * e + 6)
                        load_block(4 * e + 7)
                    store(e, 2)
                for n in range(2):
                    sp.wait_ge(g_stored[n], 16 * (EXPERTS * T // 2) + 16)
                    sp.wait_ge(u_stored[n], 16 * (EXPERTS * T // 2) + 16)
                for t in range(G_RING, T):
                    load_g(0, t)
                for e in range(EXPERTS):
                    for t in range(T):
                        load_u(e, t)
                        if e < LAST:
                            load_g(e + 1, t)
                sp.wait_ge(out_added, EXPERTS * T)
                sp.dma_start(gnn_dram.rearrange("(t p) d -> p t d", p=P), acc[:]).then_inc(gnn_stored, 16)
                sp.wait_ge(gnn_stored, 16)

            @block.tensor
            def _(pe):
                def first_layer(e, c):
                    c0, cn = CHUNKS[c]
                    for f in range(K):
                        n = c * K + f
                        if n >= 4:
                            pe.wait_ge(h_exact, e * HN + (n - 3))
                        for source, wt in ((MEAN, 0), (XN, 1)):
                            for k in range(K):
                                last = emit_split_product(nc, m.ps[:, n % 4, 0:cn],
                                                          [w1[:, wt, h, k, f * 128:(f + 1) * 128] for h in range(2)],
                                                          [m.parts[:, source, h, k, c0:c0 + cn] for h in range(2)],
                                                          wt == 0 and k == 0, wt == 1 and k == K - 1)
                        last.then_inc(h_summed, 1)

                def second_layer(e, c):
                    pe.wait_ge(h_low, e * HN + ((c + 1) * K + 2))
                    for t in TILES[c]:
                        at = (t - TILES[c][0]) * P
                        for wt, free, summed in ((0, g_staged, g_summed), (1, u_staged, u_summed)):
                            pe.wait_ge(free, e * T + (t + 1))
                            for k in range(K):
                                last = emit_split_product(nc, m.ps[0:P, 4 + t % 2 * 2 + wt, :],
                                                          [hT[:, c % 2, h, k, at:at + P] for h in range(2)],
                                                          [w2[:, wt, h, k, :] for h in range(2)], k == 0, k == K - 1)
                            last.then_inc(summed, 1)

                pe.wait_ge(bl1_loaded, EXPERTS * 16)
                nc.tensor.transpose(m.ps[:, 0, 0:EXPERTS * K], bl1_rows[:], m.ident[0:EXPERTS * K, 0:EXPERTS * K]).then_inc(bl1_turned, 1)
                pe.wait_ge(bl1_ready, 1)
                with pe.Fori(0, EXPERTS) as e:
                    for layer, c in ORDER:
                        if layer == "first":
                            if c == 0:
                                pe.wait_ge(w_split, e * 4 + 2)
                            first_layer(e, c)
                        else:
                            if c == 0:
                                pe.wait_ge(w_split, e * 4 + 4)
                            second_layer(e, c)

                def counts_times_g(e, half, exact):
                    for t in range(T):
                        pe.wait_ge(out_read, e * T + (t + 1))
                        for s in range(T):
                            counts = adj[:, s, tile(t)]
                            for h in range(2):
                                part = g[half][:, h, s, :]
                                last = nc.tensor.matmul(m.ps[0:P, t % 2, :], counts if exact else counts.bitcast(F32),
                                                        part if exact else part.bitcast(F32),
                                                        start=(s == 0 and h == 0), stop=(s == T - 1 and h == 1))
                        last.then_inc(out_summed, 1)

                pe.wait_ge(adj_loaded, 16)
                top_degree = pe.value_load(m.top_degree[0:1, 0:1], min_val=0, max_val=E)
                with pe.Fori(0, EXPERTS // 2) as pair:
                    for half in range(2):
                        e = pair * 2 + half
                        pe.wait_ge(g_low, e * T + T)
                        with pe.If(top_degree > EXACT_COUNTS):
                            counts_times_g(e, half, False)
                        with pe.Else():
                            counts_times_g(e, half, True)

            @block.scalar
            def _(act):
                def weight_high(block_n, e):
                    n = block_n % 2
                    act.wait_ge(landed[n], e * 32 + 16 * (block_n // 2 + 1))
                    dst = (w1, w2)[block_n // 2 % 2]
                    nc.scalar.activation(dst[:, n, 0], landing[:, n], ACT.Copy).then_inc(w_high, 1)

                def hidden(e, c):
                    c0, cn = CHUNKS[c]
                    for f in range(K):
                        n = c * K + f
                        act.wait_ge(h_summed, e * HN + (n + 1))
                        act.wait_ge(h_low, e * HN + (n + 1))
                        act.wait_ge(bl1_ready, 1)
                        nc.scalar.activation(tmp[:, n % 2, 0:cn], m.ps[:, n % 4, 0:cn], ACT.Relu, bias=bl1[:, bass.ds(e * K + f, 1)])\
                            .then_inc(h_exact, 1)

                def stage_g(e, c):
                    for t in TILES[c]:
                        act.wait_ge(g_summed, e * T + (t + 1))
                        act.wait_ge(g_stored[t % 2], e * (16 * T // 2) + 16 * (t // 2 + 1))
                        nc.scalar.activation(staged[:, t % 2, 0], m.ps[0:P, 4 + t % 2 * 2, :], ACT.Copy).then_inc(g_staged, 1)

                def expert(e, last):
                    weight_high(2, e)
                    weight_high(3, e)
                    for layer, c in ORDER:
                        if layer == "first":
                            hidden(e, c)
                        else:
                            stage_g(e, c)
                        if (layer, c) == ("first", 2) and not last:
                            weight_high(4, e)
                            weight_high(5, e)
                    act.wait_ge(u_summed, e * T + T)

                act.sem_inc(g_staged, 2)
                act.sem_inc(g_stored[0], 16)
                act.sem_inc(g_stored[1], 16)
                weight_high(0, 0)
                weight_high(1, 0)
                with act.Fori(0, LAST) as e:
                    expert(e, False)
                expert(LAST, True)
                for e in range(EXPERTS):
                    if e >= 2:
                        act.wait_ge(out_summed, (e - 1) * T)
                    for t in range(T):
                        n = e * T + t
                        act.wait_ge(g_loaded[n % G_RING], 16 * (n // G_RING + 1))
                        nc.scalar.activation(g[e % 2][:, 0, t, :], g_in[:, n % G_RING], ACT.Copy).then_inc(g_high, 1)

            @block.gpsimd
            def _(pool):
                def weight_low(block_n, e):
                    n = block_n % 2
                    pool.wait_ge(w_high, e * 4 + (block_n + 1))
                    dst = (w1, w2)[block_n // 2 % 2]
                    pool.tensor_tensor(dst[:, n, 1], landing[:, n], dst[:, n, 0].bitcast(F32), ALU.subtract).then_inc(w_split, 1)

                def expert(e, last):
                    weight_low(2, e)
                    weight_low(3, e)
                    for c, (c0, cn) in enumerate(CHUNKS):
                        for f in range(K):
                            n = c * K + f
                            pool.wait_ge(h_high, e * HN + (n + 1))
                            pool.tensor_tensor(hT[:, c % 2, 1, f, 0:cn], tmp[:, n % 2, 0:cn], hT[:, c % 2, 0, f, 0:cn].bitcast(F32),
                                               ALU.subtract).then_inc(h_low, 1)
                    if not last:
                        weight_low(4, e)
                        weight_low(5, e)

                pool.sem_inc(h_low, 2)
                weight_low(0, 0)
                weight_low(1, 0)
                with pool.Fori(0, LAST) as e:
                    expert(e, False)
                expert(LAST, True)
                for e in range(EXPERTS):
                    for t in range(T):
                        n = e * T + t
                        pool.wait_ge(g_high, n + 1)
                        pool.tensor_tensor(g[e % 2][:, 1, t, :], g_in[:, n % G_RING], g[e % 2][:, 0, t, :].bitcast(F32),
                                           ALU.subtract).then_inc(g_low, 1)

            @block.vector
            def _(vec):
                vec.wait_ge(bl1_turned, 1)
                nc.vector.tensor_copy(bl1[:], m.ps[:, 0, 0:EXPERTS * K]).then_inc(bl1_ready, 1)
                vec.sem_inc(u_staged, 2)
                vec.sem_inc(u_stored[0], 16)
                vec.sem_inc(u_stored[1], 16)
                with vec.Fori(0, EXPERTS) as e:
                    for layer, c in ORDER:
                        c0, cn = CHUNKS[c]
                        if layer == "first":
                            for f in range(K):
                                n = c * K + f
                                vec.wait_ge(h_exact, e * HN + (n + 1))
                                nc.vector.tensor_copy(hT[:, c % 2, 0, f, 0:cn], tmp[:, n % 2, 0:cn]).then_inc(h_high, 1)
                        else:
                            if c == 0:
                                vec.wait_ge(bl2_loaded, e * 16 + 16)
                            for t in TILES[c]:
                                vec.wait_ge(u_summed, e * T + (t + 1))
                                vec.wait_ge(u_stored[t % 2], e * (16 * T // 2) + 16 * (t // 2 + 1))
                                nc.vector.tensor_tensor(staged[:, t % 2, 1], m.ps[0:P, 4 + t % 2 * 2 + 1, :], bl2[:], ALU.add)\
                                    .then_inc(u_staged, 1)
                    vec.drain().then_inc(bl2_used, 1)
                vec.sem_inc(out_read, 2)
                nc.vector.memset(acc[:], 0.0)
                vec.drain()
                for e in range(EXPERTS):
                    for t in range(T):
                        n = e * T + t
                        vec.wait_ge(out_summed, n + 1)
                        vec.wait_ge(u_loaded[n % U_RING], 16 * (n // U_RING + 1))
                        nc.vector.scalar_tensor_tensor(o[:, t % 2, :], m.ps[0:P, t % 2, :], m.inv_col[:, t:t + 1], u_in[:, n % U_RING],
                                                       ALU.mult, ALU.add).then_inc(out_read, 1)
                        vec.drain()
                        nc.vector.tensor_scalar(o[:, t % 2, :], o[:, t % 2, :], 0.0, m.gate[:, e, t:t + 1], ALU.max, ALU.mult)
                        vec.drain()
                        nc.vector.tensor_tensor(acc[:, t, :], acc[:, t, :], o[:, t % 2, :], ALU.add).then_inc(out_added, 1)


def stage_mixer(nc, m, w, xn_dram):
    WQ, WK, WV, WO = range(4)
    QUARTERS = FF // D
    BLOCKS = 4 + 2 * QUARTERS
    W1 = [4 + 2 * b for b in range(QUARTERS)]
    W2 = [5 + 2 * b for b in range(QUARTERS)]
    SLOT = [0, 1, 0, 1] + [0, 1, 2, 3] * (QUARTERS // 2)
    VW = DH + 1
    CW = 6 * K + FT
    xm = m.xm
    with ExitStack() as ctx:
        def sb(name, shape, dt=F32):
            return ctx.enter_context(nc.sbuf_tensor(name, shape, dt))

        def sem(name):
            return ctx.enter_context(nc.semaphore(name))

        qp = sb("qp", [P, 2, 2 * M])
        qpT = sb("qpT", [128, 2, 4 * P])
        tmp = qpT
        context = sb("context", [128, 2, 4, VW])
        squares = sb("squares", [128, N])
        proj = sb("proj", [128, 2, 2, DH])
        projT = sb("projT", [128, 2 * M])
        halves = sb("halves", [128, 2])
        col_rows = sb("col_rows", [DEPTH * CW, 128])
        all_cols = sb("all_cols", [128, DEPTH * CW])
        layer_cols = sb("layer_cols", [128, CW])
        cols = layer_cols[:, 0:4 * K].rearrange("p (a k) -> p a k", a=4)
        qk_bias = layer_cols[:, 4 * K:6 * K].rearrange("p (a k) -> p a k", a=2)
        b1 = layer_cols[:, 6 * K:CW]
        rows = sb("rows", [P, 3, D])
        st = sb("st1", [P, T, 6])
        mv = sb("mv1", [P, T, 2])
        std = sb("std1", [P, T])
        rstd = sb("rstd1", [P, T])
        k_max = sb("k_max", [P, 2, T])
        k_top = sb("k_top", [P, 2])
        k_all = sb("k_all", [P, 2])
        k_diag = sb("k_diag", [P, 2, T, 2])
        q_diag = sb("q_diag", [P, 2, T, 2])
        k_shift = sb("k_shift", [P, T, 2])
        q_max = sb("q_max", [P, 2, 2])
        q_shift = sb("q_shift", [P, 2, 2])
        rden = sb("rden", [P, 2, 2])

        SLOT_BYTES, KP_BYTES, V_BYTES = 2 * K * D * 4, T * D * 4, T * HEADS * VW * 4
        at_y = -(-nc.sbuf_base // 64) * 64
        at_qk = at_y + 2 * K * N * 4
        at_kp = at_qk + 2 * K * N * 4
        at_v = at_kp + 2 * KP_BYTES
        at_o = at_v + V_BYTES
        assert 2 * SLOT_BYTES + K * D * 4 <= 2 * KP_BYTES and 2 * SLOT_BYTES <= V_BYTES + KP_BYTES and SLOT_BYTES <= V_BYTES

        def place(name, shape, dt, offset):
            return nc.alloc_sbuf_tensor_at(name, shape, dt, offset=offset)

        yT = place("yT", [128, 2, K, N], F32R, at_y)
        qT = place("qT", [128, K, N], F32, at_qk)
        kT = place("kT", [128, K, N], F32, at_qk + K * N * 4)
        hT = place("hidT", [128, 2, K, N], F32R, at_qk)
        kp = place("kp", [P, 2, T, D], F32, at_kp)
        landing = place("landing", [128, K, D], F32, at_kp + 2 * SLOT_BYTES)
        v = place("v", [P, T, HEADS, VW], F32, at_v)
        o = place("o", [P, T, D], F32, at_o)
        z = o
        slots = [place(f"wslot{n}", [128, 2, K, D], F32R, (at_kp if n < 2 else at_v) + n % 2 * SLOT_BYTES) for n in range(4)]

        x_loaded, cols_loaded, rows_loaded, proj_loaded = sem("xm_loaded"), sem("cols_loaded"), sem("rows_loaded"), sem("proj_loaded")
        w_landed, w_high, w_split = sem("w_landed"), sem("w_high"), sem("w_split")
        cols_turned, layer_cols_ready = sem("cols_turned"), sem("layer_cols_ready")
        proj_turned, projT_ready, halves_ready = sem("proj_turned"), sem("projT_ready"), sem("halves_ready")
        var_ready, std_made, z_ready, y_turned = sem("var_ready1"), sem("std_made1"), sem("z_ready"), sem("y_turned")
        exact_ready, high_ready, low_ready = sem("exact_ready"), sem("high_ready"), sem("low_ready")
        qk_summed, qk_copied, v_summed, v_ready = sem("qk_summed"), sem("qk_copied"), sem("v_summed"), sem("v_ready")
        squares_ready, diag_summed, diag_copied = sem("squares_ready"), sem("diag_summed"), sem("diag_copied")
        ks_summed, ks_copied, k_top_ready, k_all_ready = sem("ks_summed"), sem("ks_copied"), sem("k_top_ready"), sem("k_all_ready")
        k_shift_ready, k_exp, kp_ready = sem("k_shift_ready"), sem("k_exp"), sem("kp_ready")
        context_summed, context_ready = sem("context_summed"), sem("context_ready")
        qs_summed, q_shift_ready, q_exp = sem("qs_summed"), sem("q_shift_ready"), sem("q_exp")
        qp_turned, qpT_ready, o_summed, o_ready = sem("qp_turned"), sem("qpT_ready"), sem("o_summed"), sem("o_ready")
        bo_added, b2_added, o_turned, oT_high, oT_low = sem("bo_added"), sem("b2_added"), sem("o_turned"), sem("oT_high"), sem("oT_low")
        wo_summed, wo_added, h_summed, ff_summed, ff_added = (
            sem("wo_summed"), sem("wo_added"), sem("ffh_summed"), sem("ff_summed"), sem("ff_added"))

        TURNS = [(k, g) for k in range(K) for g in GROUPS3]
        G = len(TURNS)
        NQ = K * len(CHUNKS)
        NT = PAIRS * T
        HQ = K * len(CHUNKS)
        SPLITS = 2 * G + QUARTERS * HQ
        FT_ALL = QUARTERS * T
        DIAGS = 2 * PAIRS
        ATTENTION = range(-2, PAIRS)

        def keys_of(b):
            return b + 2 if b + 2 < PAIRS else None

        def features_of(b):
            return b + 1 if 0 <= b + 1 < PAIRS else None

        def diag_order():
            order = []
            for b in ATTENTION:
                order += [("k", keys_of(b))] * (keys_of(b) is not None) + [("q", features_of(b))] * (features_of(b) is not None)
            return order

        DIAG_AT = {key: n for n, key in enumerate(diag_order())}
        K_DIAG_STEP, Q_DIAG_STEP = 3, 8

        with nc.Block() as block:
            @block.sync
            def _(sp):
                sp.dma_start(xm[:], xn_dram.rearrange("(t p) d -> p t d", p=P)).then_inc(x_loaded, 16)
                for n, a in enumerate(("ln1_g", "ln1_b", "ln2_g", "ln2_b", "bq", "bk")):
                    sp.dma_start(col_rows[n * DEPTH * K:(n + 1) * DEPTH * K, :], w[a].rearrange("l (k p) -> (l k) p", p=128)).then_inc(cols_loaded, 16)
                sp.dma_start(col_rows[6 * DEPTH * K:, :], w["b1"].rearrange("l (f p) -> (l f) p", p=128)).then_inc(cols_loaded, 16)
                for i in range(DEPTH):
                    blocks = [w[a][i] for a in ("Wq", "Wk", "Wv", "Wo")]
                    for b in range(QUARTERS):
                        blocks += [w["W1"][i, :, b * D:(b + 1) * D], w["W2"][i, b * D:(b + 1) * D, :]]
                    for n, a in enumerate(blocks):
                        if i * BLOCKS + n:
                            sp.wait_ge(w_split, i * BLOCKS + n)
                        if n == WO:
                            sp.wait_ge(context_summed, i * PAIRS + PAIRS)
                        sp.dma_start(landing[:], a.rearrange("(k p) n -> p k n", p=128)).then_inc(w_landed, 16)
                        if n == WQ:
                            pv = w["proj"][i].rearrange("(a p) d -> p a d", p=128)
                            if i:
                                sp.wait_ge(proj_turned, i)
                            for c in range(2):
                                sp.dma_start(proj[:, :, c, :], pv).then_inc(proj_loaded, 16)
                            if i:
                                sp.wait_ge(b2_added, i * T)
                            for j, r in enumerate(("bv", "bo", "b2")):
                                sp.dma_start(rows[:, j], w[r][i].partition_broadcast(P)).then_inc(rows_loaded, 16)

            @block.tensor
            def _(pe):
                def parts(n):
                    return slots[SLOT[n]]

                def turn_rows(i, half):
                    for n, (k, (t0, t1)) in enumerate(TURNS):
                        pe.wait_ge(z_ready, i * 2 * T + (half * T + t1))
                        if n >= 4:
                            pe.wait_ge(exact_ready, i * SPLITS + (half * G + n - 3))
                        for t in range(t0, t1):
                            last = nc.tensor.transpose(m.ps[:, n % 4, (t - t0) * P:(t - t0 + 1) * P], z[:, t, k * 128:(k + 1) * 128],
                                                       m.ident[0:P, 0:P])
                        last.then_inc(y_turned, 1)
                    pe.wait_ge(low_ready, i * SPLITS + (half * G + G))

                def diagonal(i, kind, j):
                    d = DIAG_AT[kind, j]
                    pe.wait_ge(squares_ready, i * DIAGS + (d + 1))
                    if d:
                        pe.wait_ge(diag_copied, i * DIAGS + d)
                    for t in range(T):
                        last = nc.tensor.matmul(m.ps[0:P, 5, 2 * t:2 * t + 2], squares[:, tile(t)], halves[:], start=True, stop=True)
                    last.then_inc(diag_summed, 1)

                def attention_block(i, b):
                    jk, jf = keys_of(b), features_of(b)
                    for s in range(T + 2):
                        if b >= 0 and s < T:
                            if b * T + s >= 2:
                                pe.wait_ge(q_exp, i * NT + (b * T + s - 1))
                            nc.tensor.matmul(m.ps[0:P, 6 + s % 2, :], qT[:, b, tile(s)], projT[:], start=True, stop=True).then_inc(qs_summed, 1)
                        if jk is not None and s < T:
                            if jk * T + s >= 2:
                                pe.wait_ge(ks_copied, i * NT + (jk * T + s - 1))
                            nc.tensor.matmul(m.ps[0:P, 2 + s % 2, :], kT[:, jk, tile(s)], projT[:], start=True, stop=True).then_inc(ks_summed, 1)
                        if s == K_DIAG_STEP and jk is not None:
                            if jf:
                                pe.wait_ge(context_ready, i * PAIRS + jf)
                            diagonal(i, "k", jk)
                        if s == Q_DIAG_STEP and jf is not None:
                            if jf:
                                pe.wait_ge(context_ready, i * PAIRS + jf)
                            diagonal(i, "q", jf)
                        t = s - 1
                        if b >= 0 and 0 <= t < T:
                            pe.wait_ge(q_exp, i * NT + (b * T + t + 1))
                            if b * T + t >= 2:
                                pe.wait_ge(qpT_ready, i * NT + (b * T + t - 1))
                            for c in range(4):
                                last = nc.tensor.transpose(m.ps[:, t % 2, c * P:(c + 1) * P], qp[:, t % 2, c * 128:(c + 1) * 128],
                                                           m.ident[0:P, 0:P])
                            last.then_inc(qp_turned, 1)
                        t = s - 2
                        if b >= 0 and 0 <= t < T:
                            if t == 0:
                                pe.wait_ge(context_ready, i * PAIRS + (b + 1))
                            pe.wait_ge(qpT_ready, i * NT + (b * T + t + 1))
                            if b * T + t:
                                pe.wait_ge(o_ready, i * NT + (b * T + t))
                            for h in range(2):
                                for a in range(2):
                                    last = nc.tensor.matmul(m.ps[0:P, 4, h * VW:(h + 1) * VW],
                                                            qpT[:, t % 2, (2 * h + a) * P:(2 * h + a + 1) * P], context[:, b % 2, 2 * h + a, :],
                                                            start=(a == 0), stop=(a == 1))
                            last.then_inc(o_summed, 1)
                    if jf is not None:
                        pe.wait_ge(kp_ready, i * NT + (jf * T + T))
                        pe.wait_ge(diag_copied, i * DIAGS + (DIAG_AT["q", jf] + 1))
                        for c in range(4):
                            for t in range(T):
                                last = nc.tensor.matmul(m.ps[:, 5, c * VW:(c + 1) * VW], kp[:, jf % 2, t, c * 128:(c + 1) * 128],
                                                        v[:, t, 2 * jf + c // 2, :], start=(t == 0), stop=(t == T - 1))
                        last.then_inc(context_summed, 1)

                pe.wait_ge(cols_loaded, 112)
                nc.tensor.transpose(m.ps[:, 6, 0:DEPTH * CW], col_rows[:], m.ident[0:DEPTH * CW, 0:DEPTH * CW]).then_inc(cols_turned, 1)
                with pe.Fori(0, DEPTH) as i:
                    pe.wait_ge(proj_loaded, i * 32 + 32)
                    for a in range(2):
                        last = nc.tensor.transpose(m.ps[:, 4, a * 128:(a + 1) * 128], proj[:, a].rearrange("p c d -> p (c d)"), m.ident[:])
                    last.then_inc(proj_turned, 1)
                    turn_rows(i, 0)
                    pe.wait_ge(projT_ready, i + 1)
                    pe.wait_ge(layer_cols_ready, i + 1)
                    n = 0
                    for block_n in (WQ, WK):
                        pe.wait_ge(w_split, i * BLOCKS + (block_n + 1))
                        wt = parts(block_n)
                        for f in range(K):
                            for c0, cn in CHUNKS:
                                if n >= 4:
                                    pe.wait_ge(qk_copied, i * 2 * NQ + (n - 3))
                                for k in range(K):
                                    last = emit_split_product(nc, m.ps[:, 4 + n % 4, 0:cn],
                                                              [wt[:, h, k, f * 128:(f + 1) * 128] for h in range(2)],
                                                              [yT[:, h, k, c0:c0 + cn] for h in range(2)], k == 0, k == K - 1)
                                last.then_inc(qk_summed, 1)
                                n += 1
                    pe.wait_ge(w_split, i * BLOCKS + (WV + 1))
                    wt = parts(WV)
                    for t in range(T):
                        if t >= 2:
                            pe.wait_ge(v_ready, i * T + (t - 1))
                        for k in range(K):
                            last = emit_split_product(nc, m.ps[0:P, t % 2, :], [yT[:, h, k, tile(t)] for h in range(2)],
                                                      [wt[:, h, k, :] for h in range(2)], k == 0, k == K - 1)
                        last.then_inc(v_summed, 1)
                    pe.wait_ge(qk_copied, i * 2 * NQ + 2 * NQ)
                    pe.wait_ge(v_ready, i * T + T)
                    pe.wait_ge(halves_ready, 1)
                    for b in ATTENTION:
                        attention_block(i, b)
                    pe.wait_ge(o_ready, i * NT + NT)
                    for n, (k, (t0, t1)) in enumerate(TURNS):
                        if n >= 4:
                            pe.wait_ge(oT_low, i * G + (n - 3))
                        for t in range(t0, t1):
                            last = nc.tensor.transpose(m.ps[:, n % 4, (t - t0) * P:(t - t0 + 1) * P], o[:, t, k * 128:(k + 1) * 128],
                                                       m.ident[0:P, 0:P])
                        last.then_inc(o_turned, 1)
                    pe.wait_ge(w_split, i * BLOCKS + (WO + 1))
                    pe.wait_ge(oT_low, i * G + G)
                    wt = parts(WO)
                    for t in range(T):
                        if t >= 2:
                            pe.wait_ge(wo_added, i * T + (t - 1))
                        for k in range(K):
                            last = emit_split_product(nc, m.ps[0:P, 6 + t % 2, :], [yT[:, h, k, tile(t)] for h in range(2)],
                                                      [wt[:, h, k, :] for h in range(2)], k == 0, k == K - 1)
                        last.then_inc(wo_summed, 1)
                    turn_rows(i, 1)
                    for b in range(QUARTERS):
                        pe.wait_ge(w_split, i * BLOCKS + (W1[b] + 1))
                        wt = parts(W1[b])
                        for c, (c0, cn) in enumerate(CHUNKS):
                            for f in range(K):
                                n = b * HQ + c * K + f
                                if n >= 4:
                                    pe.wait_ge(exact_ready, i * SPLITS + (2 * G + n - 3))
                                for k in range(K):
                                    last = emit_split_product(nc, m.ps[:, 4 + n % 4, 0:cn],
                                                              [wt[:, h, k, f * 128:(f + 1) * 128] for h in range(2)],
                                                              [yT[:, h, k, c0:c0 + cn] for h in range(2)], k == 0, k == K - 1)
                                last.then_inc(h_summed, 1)
                        pe.wait_ge(w_split, i * BLOCKS + (W2[b] + 1))
                        wt = parts(W2[b])
                        for c, (t0, t1) in enumerate(GROUPS3):
                            pe.wait_ge(low_ready, i * SPLITS + (2 * G + b * HQ + (c + 1) * K))
                            for t in range(t0, t1):
                                if b * T + t >= 2:
                                    pe.wait_ge(ff_added, i * FT_ALL + (b * T + t - 1))
                                for k in range(K):
                                    last = emit_split_product(nc, m.ps[0:P, t % 2, :], [hT[:, h, k, tile(t)] for h in range(2)],
                                                              [wt[:, h, k, :] for h in range(2)], k == 0, k == K - 1)
                                last.then_inc(ff_summed, 1)

            @block.scalar
            def _(act):
                def weight_high(i, n):
                    act.wait_ge(w_landed, i * 16 * BLOCKS + 16 * (n + 1))
                    nc.scalar.activation(slots[SLOT[n]][:, 0], landing[:], ACT.Copy).then_inc(w_high, 1)

                def norm_rows(i, half):
                    for g, (t0, t1) in enumerate(GROUPS3):
                        act.wait_ge(var_ready, i * 6 + (half * 3 + g + 1))
                        nc.scalar.activation(std[:, t0:t1], mv[:, t0:t1, 1], ACT.Sqrt, bias=m.eps_col[0:P, :]).then_inc(std_made, 1)
                    for n, (k, (t0, t1)) in enumerate(TURNS):
                        act.wait_ge(y_turned, i * 2 * G + (half * G + n + 1))
                        if n >= 2:
                            act.wait_ge(low_ready, i * SPLITS + (half * G + n - 1))
                        nc.scalar.activation(tmp[:, n % 2, 0:(t1 - t0) * P], m.ps[:, n % 4, 0:(t1 - t0) * P], ACT.Identity,
                                             bias=cols[:, 2 * half + 1, k:k + 1], scale=cols[:, 2 * half, k:k + 1])\
                            .then_inc(exact_ready, 1)

                with act.Fori(0, DEPTH) as i:
                    weight_high(i, WQ)
                    act.wait_ge(layer_cols_ready, i + 1)
                    norm_rows(i, 0)
                    weight_high(i, WK)
                    n = 0
                    for a, dstT in enumerate((qT, kT)):
                        for f in range(K):
                            for c0, cn in CHUNKS:
                                act.wait_ge(qk_summed, i * 2 * NQ + (n + 1))
                                nc.scalar.activation(dstT[:, f, c0:c0 + cn], m.ps[:, 4 + n % 4, 0:cn], ACT.Identity,
                                                     bias=qk_bias[:, a, f:f + 1], scale=NORM).then_inc(qk_copied, 1)
                                n += 1
                        if a == 0:
                            weight_high(i, WV)
                    for b in ATTENTION:
                        jk, jf = keys_of(b), features_of(b)
                        for s in range(T + 2):
                            if b >= 0 and s < T:
                                act.wait_ge(q_shift_ready, i * NT + (b * T + s + 1))
                                if b * T + s >= 2:
                                    act.wait_ge(qp_turned, i * NT + (b * T + s - 1))
                                for h in range(2):
                                    last = nc.scalar.activation(qp[:, s % 2, h * M:(h + 1) * M], m.ps[0:P, 6 + s % 2, h * M:(h + 1) * M], ACT.Exp,
                                                                bias=q_shift[:, s % 2, h:h + 1])
                                last.then_inc(q_exp, 1)
                            if jk is not None and s < T:
                                act.wait_ge(ks_summed, i * NT + (jk * T + s + 1))
                                nc.scalar.activation(kp[:, jk % 2, s, :], m.ps[0:P, 2 + s % 2, :], ACT.Copy).then_inc(ks_copied, 1)
                            t = s - 2
                            if jf is not None and 0 <= t < T:
                                if t == 0:
                                    act.wait_ge(k_shift_ready, i * PAIRS + (jf + 1))
                                for h in range(2):
                                    scores = kp[:, jf % 2, t, h * M:(h + 1) * M]
                                    last = nc.scalar.activation(scores, scores, ACT.Exp, bias=k_shift[:, t, h:h + 1])
                                last.then_inc(k_exp, 1)
                            if b == PAIRS - 1 and s == 4:
                                weight_high(i, WO)
                            if b == PAIRS - 1 and s == 9:
                                weight_high(i, W1[0])
                        if jf is not None:
                            act.wait_ge(context_summed, i * PAIRS + (jf + 1))
                            nc.scalar.activation(context[:, jf % 2], m.ps[:, 5, 0:4 * VW].rearrange("p (c n) -> p c n", c=4), ACT.Copy)\
                                .then_inc(context_ready, 1)
                    for n, (k, (t0, t1)) in enumerate(TURNS):
                        act.wait_ge(o_turned, i * G + (n + 1))
                        nc.scalar.activation(yT[:, 0, k, t0 * P:t1 * P], m.ps[:, n % 4, 0:(t1 - t0) * P], ACT.Copy).then_inc(oT_high, 1)
                    norm_rows(i, 1)
                    for b in range(QUARTERS):
                        for c, (c0, cn) in enumerate(CHUNKS):
                            for f in range(K):
                                n = b * HQ + c * K + f
                                act.wait_ge(h_summed, i * QUARTERS * HQ + (n + 1))
                                if n >= 2:
                                    act.wait_ge(low_ready, i * SPLITS + (2 * G + n - 1))
                                nc.scalar.activation(tmp[:, n % 2, 0:cn], m.ps[:, 4 + n % 4, 0:cn], ACT.Gelu, bias=b1[:, b * K + f:b * K + f + 1])\
                                    .then_inc(exact_ready, 1)
                            if c == 0:
                                if b >= 2:
                                    act.wait_ge(ff_summed, i * FT_ALL + (b - 1) * T)
                                weight_high(i, W2[b])
                            if c == 2 and b + 1 < QUARTERS:
                                weight_high(i, W1[b + 1])
                    act.wait_ge(ff_summed, i * FT_ALL + FT_ALL)

            @block.vector
            def _(vec):
                nc.vector.memset(projT[:], 0.0)
                nc.vector.memset(halves[:], 0.0)
                vec.drain()
                for h in range(2):
                    last = nc.vector.memset(halves[h * DH:(h + 1) * DH, h:h + 1], 0.5)
                last.then_inc(halves_ready, 1)
                vec.wait_ge(cols_turned, 1)
                nc.vector.tensor_copy(all_cols[:], m.ps[:, 6, 0:DEPTH * CW])
                vec.drain()
                vec.wait_ge(x_loaded, 16)

                def norm_group(i, half, g):
                    t0, t1 = GROUPS3[g]
                    for t in range(t0, t1):
                        nc.vector.bn_stats(st[:, t, :], xm[:, t, :])
                    vec.drain()
                    for t in range(t0, t1):
                        last = nc.vector.bn_aggr(mv[:, t, :], st[:, t, :])
                    last.then_inc(var_ready, 1)
                    vec.wait_ge(std_made, i * 6 + (half * 3 + g + 1))
                    nc.vector.reciprocal(rstd[:, t0:t1], std[:, t0:t1])
                    vec.drain()
                    for t in range(t0, t1):
                        nc.vector.tensor_scalar(z[:, t, :], xm[:, t, :], mv[:, t, 0:1], rstd[:, t:t + 1],
                                                ALU.subtract, ALU.mult).then_inc(z_ready, 1)

                def split_high(i, n, dst, width):
                    vec.wait_ge(exact_ready, i * SPLITS + (n + 1))
                    nc.vector.tensor_copy(dst, tmp[:, n % 2, 0:width]).then_inc(high_ready, 1)

                with vec.Fori(0, DEPTH) as i:
                    nc.vector.tensor_copy(layer_cols[:, 0:6 * K].rearrange("p (a k) -> p a k", a=6),
                                          all_cols[:, 0:6 * DEPTH * K].rearrange("p (a l k) -> p l a k", a=6, l=DEPTH)[:, bass.ds(i, 1)]
                                          .rearrange("p o a k -> p (o a) k"))
                    nc.vector.tensor_copy(b1, all_cols[:, 6 * DEPTH * K:].rearrange("p (l f) -> p l f", l=DEPTH)[:, bass.ds(i, 1)]
                                          .rearrange("p o f -> p (o f)"))
                    vec.drain()
                    nc.vector.tensor_scalar(qk_bias, qk_bias, NORM, None, ALU.mult).then_inc(layer_cols_ready, 1)
                    for g in range(len(GROUPS3)):
                        norm_group(i, 0, g)
                    for n, (k, (t0, t1)) in enumerate(TURNS):
                        split_high(i, n, yT[:, 0, k, t0 * P:t1 * P], (t1 - t0) * P)
                    vec.wait_ge(proj_turned, i + 1)
                    for h in range(2):
                        last = nc.vector.tensor_copy(projT[h * DH:(h + 1) * DH, h * M:(h + 1) * M], m.ps[h * DH:(h + 1) * DH, 4, 0:M])
                    last.then_inc(projT_ready, 1)
                    vec.wait_ge(rows_loaded, i * 48 + 48)
                    for t in range(T):
                        vec.wait_ge(v_summed, i * T + (t + 1))
                        if t == 0:
                            nc.vector.memset(v[:, :, :, DH:VW], 1.0)
                        nc.vector.tensor_tensor(v[:, t, :, 0:DH], m.ps[0:P, t % 2, :].rearrange("p (h c) -> p h c", h=HEADS),
                                                rows[:, 0, :].rearrange("p (h c) -> p h c", h=HEADS), ALU.add).then_inc(v_ready, 1)

                    def copy_diagonal(kind, j, dst):
                        vec.wait_ge(diag_summed, i * DIAGS + (DIAG_AT[kind, j] + 1))
                        nc.vector.tensor_copy(dst[:, j % 2], m.ps[0:P, 5, 0:2 * T].rearrange("p (t h) -> p t h", h=2)).then_inc(diag_copied, 1)

                    for b in ATTENTION:
                        jk, jf = keys_of(b), features_of(b)
                        for s in range(T + 2):
                            if b >= 0 and s < T:
                                vec.wait_ge(qs_summed, i * NT + (b * T + s + 1))
                                nc.vector.tensor_reduce(q_max[:, s % 2, :], m.ps[0:P, 6 + s % 2, :].rearrange("p (h c) -> p h c", h=2), X, ALU.max)
                                vec.drain()
                                if b * T + s >= 2:
                                    vec.wait_ge(q_exp, i * NT + (b * T + s - 1))
                                nc.vector.scalar_tensor_tensor(q_shift[:, s % 2, :], q_max[:, s % 2, :], -1.0, q_diag[:, b % 2, s, :],
                                                               ALU.mult, ALU.subtract).then_inc(q_shift_ready, 1)
                            if s == 1 and jf is not None:
                                vec.wait_ge(k_all_ready, i * PAIRS + (jf + 1))
                                for h in range(2):
                                    last = nc.vector.tensor_scalar(k_shift[:, :, h], k_diag[:, jf % 2, :, h], k_all[:, h:h + 1], -1.0,
                                                                   ALU.add, ALU.mult)
                                last.then_inc(k_shift_ready, 1)
                            if jk is not None and s < T:
                                vec.wait_ge(ks_copied, i * NT + (jk * T + s + 1))
                                nc.vector.tensor_reduce(k_max[:, :, s], kp[:, jk % 2, s, :].rearrange("p (h c) -> p h c", h=2), X, ALU.max)
                            if s == K_DIAG_STEP + 1 and jk is not None:
                                copy_diagonal("k", jk, k_diag)
                            if s == Q_DIAG_STEP + 1 and jf is not None:
                                copy_diagonal("q", jf, q_diag)
                            t = s - 1
                            if b >= 0 and 0 <= t < T:
                                vec.wait_ge(qp_turned, i * NT + (b * T + t + 1))
                                if b * T + t >= 2:
                                    vec.wait_ge(o_summed, i * NT + (b * T + t - 1))
                                nc.vector.tensor_scalar(qpT[:, t % 2, :], m.ps[:, t % 2, 0:4 * P], FEATURE_EPS, None, ALU.add).then_inc(qpT_ready, 1)
                            t = s - 2
                            if b >= 0 and 0 <= t < T:
                                vec.wait_ge(o_summed, i * NT + (b * T + t + 1))
                                ov = m.ps[0:P, 4, 0:2 * VW].rearrange("p (h c) -> p h c", h=2)
                                nc.vector.reciprocal(rden[:, t % 2, :], ov[:, :, DH])
                                vec.drain()
                                for h in range(2):
                                    last = nc.vector.tensor_scalar(o[:, t, (2 * b + h) * DH:(2 * b + h + 1) * DH], ov[:, h, 0:DH],
                                                                   rden[:, t % 2, h:h + 1], None, ALU.mult)
                                last.then_inc(o_ready, 1)
                        if jk is not None:
                            vec.drain()
                            nc.vector.tensor_reduce(k_top[:], k_max[:], X, ALU.max).then_inc(k_top_ready, 1)
                            vec.drain()
                    for n, (k, (t0, t1)) in enumerate(TURNS):
                        vec.wait_ge(oT_high, i * G + (n + 1))
                        nc.vector.tensor_tensor(yT[:, 1, k, t0 * P:t1 * P], m.ps[:, n % 4, 0:(t1 - t0) * P],
                                                yT[:, 0, k, t0 * P:t1 * P].bitcast(F32), ALU.subtract).then_inc(oT_low, 1)
                    vec.wait_ge(bo_added, i * T + T)
                    vec.wait_ge(o_turned, i * G + G)
                    for g, (t0, t1) in enumerate(GROUPS3):
                        for t in range(t0, t1):
                            vec.wait_ge(wo_summed, i * T + (t + 1))
                            nc.vector.tensor_tensor(xm[:, t, :], xm[:, t, :], m.ps[0:P, 6 + t % 2, :], ALU.add).then_inc(wo_added, 1)
                        vec.drain()
                        norm_group(i, 1, g)
                    for n, (k, (t0, t1)) in enumerate(TURNS):
                        split_high(i, G + n, yT[:, 0, k, t0 * P:t1 * P], (t1 - t0) * P)
                    vec.wait_ge(b2_added, i * T + T)
                    for b in range(QUARTERS):
                        for c, (c0, cn) in enumerate(CHUNKS):
                            for f in range(K):
                                split_high(i, 2 * G + b * HQ + c * K + f, hT[:, 0, f, c0:c0 + cn], cn)
                        for t in range(T):
                            vec.wait_ge(ff_summed, i * FT_ALL + (b * T + t + 1))
                            nc.vector.tensor_tensor(xm[:, t, :], xm[:, t, :], m.ps[0:P, t % 2, :], ALU.add).then_inc(ff_added, 1)
                        vec.drain()

            @block.gpsimd
            def _(pool):
                def weight_low(i, n):
                    pool.wait_ge(w_high, i * BLOCKS + n + 1)
                    pool.tensor_tensor(slots[SLOT[n]][:, 1], landing[:], slots[SLOT[n]][:, 0].bitcast(F32), ALU.subtract).then_inc(w_split, 1)

                def split_low(i, n, dst, high, width):
                    pool.wait_ge(high_ready, i * SPLITS + n + 1)
                    pool.tensor_tensor(dst, tmp[:, n % 2, 0:width], high.bitcast(F32), ALU.subtract).then_inc(low_ready, 1)

                def square(i, kind, j):
                    d = i * DIAGS + DIAG_AT[kind, j]
                    if d:
                        pool.wait_ge(diag_summed, d)
                    srcT = kT if kind == "k" else qT
                    pool.tensor_tensor(squares[:], srcT[:, j, :], srcT[:, j, :], ALU.mult).then_inc(squares_ready, 1)

                pool.wait_ge(x_loaded, 16)
                for i in range(DEPTH):
                    weight_low(i, WQ)
                    for n, (k, (t0, t1)) in enumerate(TURNS):
                        split_low(i, n, yT[:, 1, k, t0 * P:t1 * P], yT[:, 0, k, t0 * P:t1 * P], (t1 - t0) * P)
                    weight_low(i, WK)
                    pool.wait_ge(rows_loaded, i * 48 + 48)
                    for t in range(T):
                        pool.tensor_tensor(xm[:, t, :], xm[:, t, :], rows[:, 1, :], ALU.add).then_inc(bo_added, 1)
                        if t == 4:
                            weight_low(i, WV)
                    pool.wait_ge(qk_copied, i * 2 * NQ + 2 * NQ)
                    for b in ATTENTION:
                        jk, jf = keys_of(b), features_of(b)
                        if jk is not None:
                            square(i, "k", jk)
                        if jf is not None:
                            for t in range(T):
                                pool.wait_ge(k_exp, i * NT + jf * T + t + 1)
                                pool.tensor_scalar(kp[:, jf % 2, t, :], kp[:, jf % 2, t, :], FEATURE_EPS, 1.0, ALU.add, ALU.mult).then_inc(kp_ready, 1)
                                if t == 3:
                                    square(i, "q", jf)
                        if jk is not None:
                            pool.wait_ge(k_top_ready, i * PAIRS + jk + 1)
                            pool.partition_all_reduce(k_all[:], k_top[:], P, MAX_REDUCE).then_inc(k_all_ready, 1)
                    weight_low(i, WO)
                    weight_low(i, W1[0])
                    for n, (k, (t0, t1)) in enumerate(TURNS):
                        split_low(i, G + n, yT[:, 1, k, t0 * P:t1 * P], yT[:, 0, k, t0 * P:t1 * P], (t1 - t0) * P)
                    for t in range(T):
                        pool.tensor_tensor(xm[:, t, :], xm[:, t, :], rows[:, 2, :], ALU.add).then_inc(b2_added, 1)
                    for b in range(QUARTERS):
                        for c, (c0, cn) in enumerate(CHUNKS):
                            for f in range(K):
                                split_low(i, 2 * G + b * HQ + c * K + f, hT[:, 1, f, c0:c0 + cn], hT[:, 0, f, c0:c0 + cn], cn)
                            if c == 0:
                                weight_low(i, W2[b])
                            if c == 2 and b + 1 < QUARTERS:
                                weight_low(i, W1[b + 1])


def stage_shift_unit(nc, m, x, gnn_dram, out):
    MARK, SHL, SHR, LO, DIGITS, OUT = 0, 39, 40, 64, 16, 128
    with ExitStack() as ctx:
        def sb(name, shape, dt=F32):
            return ctx.enter_context(nc.sbuf_tensor(name, shape, dt))

        def sem(name):
            return ctx.enter_context(nc.semaphore(name))

        y = sb("y", [P, T, D])
        gnn = sb("gnn", [P, T, D])
        ln = sb("ln", [P, T, D])
        st = sb("st2", [P, T, 6])
        mv = sb("mv2", [P, T, 2])
        std = sb("std2", [P, T])
        rstd = sb("rstd2", [P, T])
        count_i = sb("count_i", [P, 2, DIGITS], I32)
        down = sb("down", [P, DIGITS])
        up = sb("up", [P, DIGITS])
        first = sb("first", [P, T, 3, DIGITS])
        best = sb("best", [P, T, 3])
        found = sb("found", [P, T, 3])
        digit = sb("digit", [P, T, 3])
        flag = sb("flag", [P, 5, T])
        value = sb("value", [P, T])
        value_i = sb("value_i", [P, 2, T], I32)
        shift_i = sb("amount_i", [P, T], I32)
        shifted_i = sb("shifted_i", [P, 2, T], I32)
        shifted = sb("shifted", [P, 2, T])
        result = sb("result", [P, T])
        result_i = sb("result_i", [P, T], I32)
        nibble_i = sb("nibble_i", [P, 2, T], I32)
        nibble = sb("nibble", [P, 2, T])
        amp = sb("amp", [P, T])
        hot = sb("hot2", [P, T, 2, DIGITS])

        x_loaded, gnn_loaded = sem("y_loaded"), sem("gnn_loaded")
        counts_made, var_ready, std_made = sem("counts_made"), sem("var_ready2"), sem("std_made2")
        out_ready, out_stored = sem("out_ready"), sem("out_stored")
        xv = x.rearrange("(t p) d -> p t d", p=P)
        ov = out.rearrange("(t p) d -> p t d", p=P)

        with nc.Block() as block:
            @block.sync
            def _(sp):
                sp.dma_start(y[:], xv).then_inc(x_loaded, 16)
                sp.dma_start(gnn[:], gnn_dram.rearrange("(t p) d -> p t d", p=P)).then_inc(gnn_loaded, 16)
                for h in range(2):
                    a, b = h * T // 2, (h + 1) * T // 2
                    sp.wait_ge(out_ready, b)
                    sp.dma_start(ov[:, a:b, :], ln[:, a:b, :]).then_inc(out_stored, 16)
                sp.wait_ge(out_stored, 32)

            @block.gpsimd
            def _(pool):
                pool.iota(count_i[:, 0], pattern=[[-1, DIGITS]], base=DIGITS, channel_multiplier=0).then_inc(counts_made, 1)
                pool.iota(count_i[:, 1], pattern=[[1, DIGITS]], base=0, channel_multiplier=0).then_inc(counts_made, 1)

            @block.scalar
            def _(act):
                act.wait_ge(var_ready, 1)
                nc.scalar.activation(std[:], mv[:, :, 1], ACT.Sqrt, bias=m.eps_col[0:P, :]).then_inc(std_made, 1)

            @block.vector
            def _(vec):
                v = nc.vector
                vec.wait_ge(counts_made, 2)
                v.tensor_copy(down[:], count_i[:, 0])
                v.tensor_copy(up[:], count_i[:, 1])
                vec.wait_ge(x_loaded, 16)
                vec.wait_ge(gnn_loaded, 16)
                for t in range(T):
                    v.tensor_tensor(y[:, t, :], y[:, t, :], gnn[:, t, :], ALU.add)
                vec.drain()
                for t in range(T):
                    v.tensor_tensor(y[:, t, :], y[:, t, :], m.xm[:, t, :], ALU.add)
                vec.drain()
                emit_norm_stats(nc, vec, std_made, var_ready, 1, y, st, mv, rstd, std)
                for t in range(T):
                    v.tensor_scalar(ln[:, t, :], y[:, t, :], mv[:, t, 0:1], rstd[:, t:t + 1], ALU.subtract, ALU.mult)
                vec.drain()
                v.scalar_tensor_tensor(first[:].rearrange("p t a d -> p t (a d)"), ln[:, :, LO:LO + 3 * DIGITS], 0.5,
                                       ln[:, :, LO:LO + 3 * DIGITS], ALU.is_gt, ALU.bypass)
                for n, c in enumerate((MARK, SHL, SHR)):
                    v.tensor_scalar(flag[:, n, :], ln[:, :, c], 0.5, None, ALU.is_gt)
                vec.drain()
                for a in range(3):
                    v.tensor_tensor(first[:, :, a, :], first[:, :, a, :], down[:].unsqueeze(1).to_broadcast([P, T, DIGITS]), ALU.mult)
                vec.drain()
                v.tensor_reduce(best[:], first[:], X, ALU.max)
                vec.drain()
                v.tensor_scalar(found[:], best[:], 0.0, None, ALU.is_gt)
                v.tensor_scalar(digit[:], best[:], -1.0, float(DIGITS), ALU.mult, ALU.add)
                vec.drain()
                v.tensor_tensor(digit[:], digit[:], found[:], ALU.mult)
                vec.drain()
                v.scalar_tensor_tensor(value[:], digit[:, :, 1], float(DIGITS), digit[:, :, 0], ALU.mult, ALU.add)
                v.tensor_copy(shift_i[:], digit[:, :, 2])
                vec.drain()
                v.tensor_copy(value_i[:, 0], value[:])
                vec.drain()
                v.tensor_tensor(shifted_i[:, 0], value_i[:, 0], shift_i[:], ALU.logical_shift_left)
                v.tensor_tensor(shifted_i[:, 1], value_i[:, 0], shift_i[:], ALU.logical_shift_right)
                v.tensor_tensor(flag[:, 3, :], flag[:, 0, :], flag[:, 1, :], ALU.mult)
                v.tensor_tensor(flag[:, 4, :], flag[:, 0, :], flag[:, 2, :], ALU.mult)
                vec.drain()
                v.tensor_scalar(shifted_i[:, 0], shifted_i[:, 0], 255, None, ALU.bitwise_and)
                v.tensor_tensor(flag[:, 4, :], flag[:, 4, :], flag[:, 3, :], ALU.is_gt)
                vec.drain()
                v.tensor_copy(shifted[:], shifted_i[:])
                v.tensor_tensor(amp[:], flag[:, 3, :], flag[:, 4, :], ALU.add)
                vec.drain()
                v.tensor_tensor(shifted[:], shifted[:], flag[:, 3:5, :], ALU.mult)
                v.tensor_scalar(amp[:], amp[:], 2.0, None, ALU.mult)
                vec.drain()
                v.tensor_tensor(result[:], shifted[:, 0], shifted[:, 1], ALU.add)
                vec.drain()
                v.tensor_copy(result_i[:], result[:])
                vec.drain()
                v.tensor_scalar(nibble_i[:, 0], result_i[:], 15, None, ALU.bitwise_and)
                v.tensor_scalar(nibble_i[:, 1], result_i[:], 4, None, ALU.logical_shift_right)
                vec.drain()
                v.tensor_copy(nibble[:], nibble_i[:])
                vec.drain()
                for a in range(2):
                    v.tensor_tensor(hot[:, :, a, :], up[:].unsqueeze(1).to_broadcast([P, T, DIGITS]),
                                    nibble[:, a, :].unsqueeze(2).to_broadcast([P, T, DIGITS]), ALU.is_equal)
                vec.drain()
                for a in range(2):
                    v.tensor_tensor(hot[:, :, a, :], hot[:, :, a, :], amp[:].unsqueeze(2).to_broadcast([P, T, DIGITS]), ALU.mult)
                vec.drain()
                v.tensor_tensor(ln[:, :, OUT:OUT + 2 * DIGITS], ln[:, :, OUT:OUT + 2 * DIGITS],
                                hot[:].rearrange("p t a d -> p t (a d)"), ALU.add)
                vec.drain()
                for t in range(T):
                    v.tensor_tensor(ln[:, t, :], ln[:, t, :], y[:, t, :], ALU.add).then_inc(out_ready, 1)


def gps_block(nc, a, out):
    xn_dram = nc.dram_tensor("xn_dram", [N, D], F32, kind="Internal").ap()
    adj_dram = nc.dram_tensor("adj_dram", [P, T, N], F32, kind="Internal").ap()
    g_dram = nc.dram_tensor("g_dram", [EXPERTS, T, P, D], F32, kind="Internal").ap()
    u_dram = nc.dram_tensor("u_dram", [EXPERTS, T, P, D], F32, kind="Internal").ap()
    gnn_dram = nc.dram_tensor("gnn_dram", [N, D], F32, kind="Internal").ap()
    with ExitStack() as ctx:
        ctx.enter_context(nc.allow_non_contiguous_dma(reason="bias vectors, one feature per partition"))

        def sb(name, shape, dt=F32):
            return ctx.enter_context(nc.sbuf_tensor(name, shape, dt))

        m = OnChip()
        m.ps = ctx.enter_context(nc.psum_tensor("ps", [128, 8, 512], F32))
        m.ident = sb("ident", [128, 128])
        m.ones = sb("ones", [128, 128])
        m.eps_col = sb("eps_col", [128, 1])
        m.inv_col = sb("inv_col", [P, T])
        m.gate = sb("gate", [P, EXPERTS, T])
        m.top_degree = sb("top_degree", [1, 1], I32)
        with ExitStack() as graph:
            def gsb(name, shape, dt=F32):
                return graph.enter_context(nc.sbuf_tensor(name, shape, dt))

            m.at_parts = -(-nc.sbuf_base // 32) * 32
            m.parts = gsb("parts", [128, 2, 2, K, N], F32R)
            with ExitStack() as counting:
                def csb(name, shape, dt=F32):
                    return counting.enter_context(nc.sbuf_tensor(name, shape, dt))

                m.adjT = csb("adjT", [P, T, N])
                m.xnT = csb("xnT", [128, K, N])
                m.xn = csb("xn", [P, T, D])
                m.src_rowT = csb("src_rowT", [CE, NC])
                m.keyT = csb("keyT", [CE, NC])
                m.shift = csb("shift", [P, NG])
                m.hot = csb("hot", [P, GW], F16)
                m.ranges = csb("ranges", [1, NG], I32)
                stage_normalise_and_index(nc, m, a["x"], a["src"], a["dst"], xn_dram)
                stage_count_edges(nc, m)
                stage_gates_and_first_sum(nc, m, a["L0_gnn_gate_W"], a["L0_gnn_gate_b"], adj_dram)
            nc.disable_value_cache = True
            stage_experts(nc, m, a["L0_gnn_Wl"], a["L0_gnn_bl"], a["L0_gnn_Wr"], adj_dram, g_dram, u_dram, gnn_dram)
        m.xm = sb("xm", [P, T, D])
        stage_mixer(nc, m, {k[len("L0_mix_"):]: v for k, v in a.items() if k.startswith("L0_mix_")}, xn_dram)
        stage_shift_unit(nc, m, a["x"], gnn_dram, out)


_INS = ["x", "src", "dst", "L0_gnn_gate_W", "L0_gnn_gate_b", "L0_gnn_Wl", "L0_gnn_bl", "L0_gnn_Wr", "L0_mix_ln1_g", "L0_mix_ln1_b",
        "L0_mix_ln2_g", "L0_mix_ln2_b", "L0_mix_Wq", "L0_mix_bq", "L0_mix_Wk", "L0_mix_bk", "L0_mix_Wv", "L0_mix_bv",
        "L0_mix_Wo", "L0_mix_bo", "L0_mix_proj", "L0_mix_W1", "L0_mix_b1", "L0_mix_W2", "L0_mix_b2"]


def kernel(**inputs):
    import concourse.bacc as bacc
    from concourse.bass_utils import run_bass_kernel_spmd

    nc = bacc.Bacc("TRN2", target_bir_lowering=False, num_devices=1)
    arrays, args = {}, {}
    for name in _INS:
        arr = np.ascontiguousarray(inputs[name])
        arrays["in_" + name] = arr
        args[name] = nc.dram_tensor("in_" + name, arr.shape, mybir.dt.from_np(arr.dtype), kind="ExternalInput").ap()
    out = nc.dram_tensor("out", (N, D), F32, kind="ExternalOutput").ap()
    gps_block(nc, args, out)
    r = run_bass_kernel_spmd(nc, [arrays], core_ids=[0])
    return r.results[0]["out"]
```
